# Optimizing a Trainium2 kernel written in Bass

```python
import numpy as np
import jax
import jax.numpy as jnp

def _softmax(x, axis=-1):
    return jax.nn.softmax(x, axis=axis)

def _gelu(x):
    return jax.nn.gelu(x, approximate=True)

def _silu(x):
    return jax.nn.silu(x)

def _sigmoid(x):
    return jax.nn.sigmoid(x)

def _layernorm(x, axis=-1, eps=1e-05):
    m = jnp.mean(x, axis=axis, keepdims=True)
    v = jnp.var(x, axis=axis, keepdims=True)
    return (x - m) / jnp.sqrt(v + eps)

def _scatter_add(tgt, idx, src, axis=0):
    return tgt.at[idx].add(src)

def _segment_sum(src, seg, n):
    return jax.ops.segment_sum(src, seg, n)
kernel_name = 'mk_seq_postln_d2_jaxref_r8_a7a0d8'

def setup_inputs(seed: int=0):
    np.random.seed(seed)
    _w = jnp.asarray

    def _L0_attn_setup():
        import jax, jax.numpy as jnp
        import numpy as np
        NUM_HEADS = 16
        HEAD_DIM = 64
        D_MODEL = 128
        B, L = (8, 512)

        def _relative_position_encoding(seq_len, dim):
            positions = jnp.arange(seq_len, dtype=jnp.float32)[:, None]
            div_term = jnp.exp(jnp.arange(0, dim, 2, dtype=jnp.float32) * -(np.log(10000.0) / dim))
            ang = positions * div_term
            pe = jnp.zeros((seq_len, dim), dtype=jnp.float32)
            pe = pe.at[:, 0::2].set(jnp.sin(ang))
            pe = pe.at[:, 1::2].set(jnp.cos(ang))
            return pe
        key = jax.random.key(seed)
        k1, k2, k3 = jax.random.split(key, 3)
        x = jax.random.normal(k1, (B, L, D_MODEL), dtype=jnp.float32)
        w_qkv = jax.random.normal(k2, (D_MODEL, 3 * NUM_HEADS * HEAD_DIM), dtype=jnp.float32) * (1.0 / np.sqrt(D_MODEL))
        b_qkv = jnp.zeros((3 * NUM_HEADS * HEAD_DIM,), dtype=jnp.float32)
        w_out = jax.random.normal(k3, (NUM_HEADS * HEAD_DIM, D_MODEL), dtype=jnp.float32) * (1.0 / np.sqrt(NUM_HEADS * HEAD_DIM))
        b_out = jnp.zeros((D_MODEL,), dtype=jnp.float32)
        return {'x': x, 'w_qkv': w_qkv, 'b_qkv': b_qkv, 'w_out': w_out, 'b_out': b_out}
    _L0_attn_in = _L0_attn_setup()

    def _L0_ffn_setup():
        import jax, jax.numpy as jnp
        import numpy as np
        B, N, D = (4, 512, 128)
        E, S, F = (16, 64, 256)
        DO = 128
        EPS = 1e-05

        def _layernorm(x, g, b):
            mu = jnp.mean(x, axis=-1, keepdims=True)
            var = jnp.mean(jnp.square(x - mu), axis=-1, keepdims=True)
            return (x - mu) * jax.lax.rsqrt(var + EPS) * g + b
        key = jax.random.key(seed)
        ks = jax.random.split(key, 8)
        d = {'x': jax.random.normal(ks[0], (B, N, D), dtype=jnp.float32), 'norm_g': jnp.ones((D,), jnp.float32), 'norm_b': jnp.zeros((D,), jnp.float32), 'slot_g': jnp.ones((D,), jnp.float32), 'slot_b': jnp.zeros((D,), jnp.float32), 'scale': jnp.ones((1,), jnp.float32), 'slot_embeds': jax.random.normal(ks[1], (E, S, D), jnp.float32) / np.sqrt(D), 'Wg': jax.random.normal(ks[2], (E, D, F), jnp.float32) * np.sqrt(2.0 / (D + F)), 'bg': jnp.zeros((E, F), jnp.float32), 'Wu': jax.random.normal(ks[3], (E, D, F), jnp.float32) * np.sqrt(2.0 / (D + F)), 'bu': jnp.zeros((E, F), jnp.float32), 'Wd': jax.random.normal(ks[4], (E, F, DO), jnp.float32) * np.sqrt(2.0 / (F + DO)), 'bd': jnp.zeros((E, DO), jnp.float32)}
        return d
    _L0_ffn_in = _L0_ffn_setup()

    def _L1_attn_setup():
        import jax, jax.numpy as jnp
        import numpy as np
        D_MODEL, N_HEADS, D_LATENT = (128, 16, 32)
        HEAD_DIM = D_MODEL // N_HEADS
        B, T = (2, 256)

        def apply_rope(x):
            Tn, D = (x.shape[1], x.shape[3])
            inv_freq = 1.0 / 10000.0 ** (jnp.arange(0, D, 2, dtype=jnp.float32) / D)
            t = jnp.arange(Tn, dtype=jnp.float32)
            freqs = jnp.outer(t, inv_freq)
            sin_f = jnp.sin(freqs)[None, :, None, :]
            cos_f = jnp.cos(freqs)[None, :, None, :]
            x1, x2 = jnp.split(x, 2, axis=-1)
            return jnp.concatenate([x1 * cos_f - x2 * sin_f, x1 * sin_f + x2 * cos_f], axis=-1)
        key = jax.random.key(seed)
        ks = jax.random.split(key, 5)
        s = lambda fan_in: 1.0 / np.sqrt(fan_in)
        return {'x': jax.random.normal(ks[0], (B, T, D_MODEL), jnp.float32), 'Wq': jax.random.normal(ks[1], (D_MODEL, D_MODEL), jnp.float32) * s(D_MODEL), 'bq': jnp.zeros((D_MODEL,), jnp.float32), 'Wkv_down': jax.random.normal(ks[2], (D_MODEL, D_LATENT), jnp.float32) * s(D_MODEL), 'bkv_down': jnp.zeros((D_LATENT,), jnp.float32), 'Wkv_up': jax.random.normal(ks[3], (D_LATENT, 2 * D_MODEL), jnp.float32) * s(D_LATENT), 'bkv_up': jnp.zeros((2 * D_MODEL,), jnp.float32), 'Wo': jax.random.normal(ks[4], (D_MODEL, D_MODEL), jnp.float32) * s(D_MODEL), 'bo': jnp.zeros((D_MODEL,), jnp.float32)}
    _L1_attn_in = _L1_attn_setup()

    def _L1_ffn_setup():
        import jax, jax.numpy as jnp
        import numpy as np
        B, S, H = (2, 128, 128)
        E, F, K = (8, 352, 2)
        NORM_TOPK = True
        key = jax.random.key(seed)
        k0, k1, k2, k3, k4 = jax.random.split(key, 5)
        hidden_states = jax.random.normal(k0, (B, S, H), jnp.float32)
        gate_w = jax.random.normal(k1, (H, E), jnp.float32) * 0.02
        w_gate = jax.random.normal(k2, (E, H, F), jnp.float32) * 0.02
        w_up = jax.random.normal(k3, (E, H, F), jnp.float32) * 0.02
        w_down = jax.random.normal(k4, (E, F, H), jnp.float32) * 0.02
        return {'hidden_states': hidden_states, 'gate_w': gate_w, 'w_gate': w_gate, 'w_up': w_up, 'w_down': w_down}
    _L1_ffn_in = _L1_ffn_setup()
    _d = {'L0_attn_x': _L0_attn_in['x'], 'L0_attn_w_qkv': _L0_attn_in['w_qkv'], 'L0_attn_b_qkv': _L0_attn_in['b_qkv'], 'L0_attn_w_out': _L0_attn_in['w_out'], 'L0_attn_b_out': _L0_attn_in['b_out'], 'L0_ffn_norm_g': _L0_ffn_in['norm_g'], 'L0_ffn_norm_b': _L0_ffn_in['norm_b'], 'L0_ffn_slot_g': _L0_ffn_in['slot_g'], 'L0_ffn_slot_b': _L0_ffn_in['slot_b'], 'L0_ffn_scale': _L0_ffn_in['scale'], 'L0_ffn_slot_embeds': _L0_ffn_in['slot_embeds'], 'L0_ffn_Wg': _L0_ffn_in['Wg'], 'L0_ffn_bg': _L0_ffn_in['bg'], 'L0_ffn_Wu': _L0_ffn_in['Wu'], 'L0_ffn_bu': _L0_ffn_in['bu'], 'L0_ffn_Wd': _L0_ffn_in['Wd'], 'L0_ffn_bd': _L0_ffn_in['bd'], 'L1_attn_Wq': _L1_attn_in['Wq'], 'L1_attn_bq': _L1_attn_in['bq'], 'L1_attn_Wkv_down': _L1_attn_in['Wkv_down'], 'L1_attn_bkv_down': _L1_attn_in['bkv_down'], 'L1_attn_Wkv_up': _L1_attn_in['Wkv_up'], 'L1_attn_bkv_up': _L1_attn_in['bkv_up'], 'L1_attn_Wo': _L1_attn_in['Wo'], 'L1_attn_bo': _L1_attn_in['bo'], 'L1_ffn_gate_w': _L1_ffn_in['gate_w'], 'L1_ffn_w_gate': _L1_ffn_in['w_gate'], 'L1_ffn_w_up': _L1_ffn_in['w_up'], 'L1_ffn_w_down': _L1_ffn_in['w_down']}
    _x0 = _d['L0_attn_x']
    _d['L0_attn_x'] = jax.random.normal(jax.random.fold_in(jax.random.key(seed), 1), (4, 512, 128), dtype=_x0.dtype)
    del _x0
    return _d

def reference(L0_attn_x, L0_attn_w_qkv, L0_attn_b_qkv, L0_attn_w_out, L0_attn_b_out, L0_ffn_norm_g, L0_ffn_norm_b, L0_ffn_slot_g, L0_ffn_slot_b, L0_ffn_scale, L0_ffn_slot_embeds, L0_ffn_Wg, L0_ffn_bg, L0_ffn_Wu, L0_ffn_bu, L0_ffn_Wd, L0_ffn_bd, L1_attn_Wq, L1_attn_bq, L1_attn_Wkv_down, L1_attn_bkv_down, L1_attn_Wkv_up, L1_attn_bkv_up, L1_attn_Wo, L1_attn_bo, L1_ffn_gate_w, L1_ffn_w_gate, L1_ffn_w_up, L1_ffn_w_down):

    def _L0_attn_ref(x, w_qkv, b_qkv, w_out, b_out):
        import jax, jax.numpy as jnp
        import numpy as np
        NUM_HEADS = 16
        HEAD_DIM = 64
        D_MODEL = 128
        B, L = (8, 512)

        def _relative_position_encoding(seq_len, dim):
            positions = jnp.arange(seq_len, dtype=jnp.float32)[:, None]
            div_term = jnp.exp(jnp.arange(0, dim, 2, dtype=jnp.float32) * -(np.log(10000.0) / dim))
            ang = positions * div_term
            pe = jnp.zeros((seq_len, dim), dtype=jnp.float32)
            pe = pe.at[:, 0::2].set(jnp.sin(ang))
            pe = pe.at[:, 1::2].set(jnp.cos(ang))
            return pe
        Bq, Lq, _ = x.shape
        qkv = x @ w_qkv + b_qkv
        qkv = qkv.reshape(Bq, Lq, NUM_HEADS, 3 * HEAD_DIM)
        q, k, v = jnp.split(qkv, 3, axis=-1)
        pos_enc = _relative_position_encoding(Lq, HEAD_DIM)
        k = k + pos_enc[None, :, None, :]
        scale = jnp.sqrt(jnp.float32(HEAD_DIM))
        attn = jnp.einsum('blhd,bl gd->blhg'.replace(' ', ''), q, k) / scale
        attn = jax.nn.softmax(attn, axis=-1)
        out = jnp.einsum('blhg,blgd->blhd', attn, v)
        out = out.reshape(Bq, Lq, NUM_HEADS * HEAD_DIM)
        return out @ w_out + b_out

    def _L0_ffn_ref(x, norm_g, norm_b, slot_g, slot_b, scale, slot_embeds, Wg, bg, Wu, bu, Wd, bd):
        import jax, jax.numpy as jnp
        import numpy as np
        B, N, D = (4, 512, 128)
        E, S, F = (16, 64, 256)
        DO = 128
        EPS = 1e-05

        def _layernorm(x, g, b):
            mu = jnp.mean(x, axis=-1, keepdims=True)
            var = jnp.mean(jnp.square(x - mu), axis=-1, keepdims=True)
            return (x - mu) * jax.lax.rsqrt(var + EPS) * g + b
        x = _layernorm(x, norm_g, norm_b)
        se = _layernorm(slot_embeds, slot_g, slot_b) * scale
        logits = jnp.einsum('bnd,esd->bnes', x, se)
        dispatch = jax.nn.softmax(logits, axis=1)
        combine = jax.nn.softmax(logits.reshape(x.shape[0], x.shape[1], -1), axis=-1)
        slots = jnp.einsum('bnd,bnes->besd', x, dispatch)
        gate = jax.nn.gelu(jnp.einsum('besd,edf->besf', slots, Wg) + bg[None, :, None, :], approximate=False)
        up = jnp.einsum('besd,edf->besf', slots, Wu) + bu[None, :, None, :]
        eout = jnp.einsum('besf,efo->beso', gate * up, Wd) + bd[None, :, None, :]
        eout = eout.reshape(eout.shape[0], -1, eout.shape[-1])
        return jnp.einsum('bns,bso->bno', combine, eout)

    def _L1_attn_ref(x, Wq, bq, Wkv_down, bkv_down, Wkv_up, bkv_up, Wo, bo):
        import jax, jax.numpy as jnp
        import numpy as np
        D_MODEL, N_HEADS, D_LATENT = (128, 16, 32)
        HEAD_DIM = D_MODEL // N_HEADS
        B, T = (2, 256)

        def apply_rope(x):
            Tn, D = (x.shape[1], x.shape[3])
            inv_freq = 1.0 / 10000.0 ** (jnp.arange(0, D, 2, dtype=jnp.float32) / D)
            t = jnp.arange(Tn, dtype=jnp.float32)
            freqs = jnp.outer(t, inv_freq)
            sin_f = jnp.sin(freqs)[None, :, None, :]
            cos_f = jnp.cos(freqs)[None, :, None, :]
            x1, x2 = jnp.split(x, 2, axis=-1)
            return jnp.concatenate([x1 * cos_f - x2 * sin_f, x1 * sin_f + x2 * cos_f], axis=-1)
        Bn, Tn = (x.shape[0], x.shape[1])
        q = x @ Wq + bq
        kv = (x @ Wkv_down + bkv_down) @ Wkv_up + bkv_up
        q = q.reshape(Bn, Tn, N_HEADS, HEAD_DIM)
        kv = kv.reshape(Bn, Tn, N_HEADS, 2 * HEAD_DIM)
        k, v = jnp.split(kv, 2, axis=-1)
        q = apply_rope(q)
        k = apply_rope(k)
        q = q.transpose(0, 2, 1, 3)
        k = k.transpose(0, 2, 1, 3)
        v = v.transpose(0, 2, 1, 3)
        att = jnp.einsum('bhqd,bhkd->bhqk', q, k) / jnp.sqrt(jnp.float32(HEAD_DIM))
        idx = jnp.arange(Tn, dtype=jnp.float32)
        dist_signed = idx[:, None] - idx[None, :]
        log_sparse = -0.1 * jnp.log(jnp.abs(dist_signed) + 1.0)
        decay = jnp.exp(-jnp.maximum(dist_signed, 0.0) * 0.01)
        att = att + (log_sparse + jnp.log(decay + 1e-09))[None, None]
        att = jax.nn.softmax(att, axis=-1)
        out = jnp.einsum('bhqk,bhkd->bhqd', att, v)
        memory_k = jnp.mean(k, axis=2, keepdims=True)
        memory_v = jnp.mean(v, axis=2, keepdims=True)
        memory_scores = jnp.einsum('bhqd,bhkd->bhqk', q, memory_k)
        infini_out = jax.nn.sigmoid(memory_scores) * memory_v
        out = out + 0.2 * infini_out
        out = out.transpose(0, 2, 1, 3).reshape(Bn, Tn, D_MODEL)
        return out @ Wo + bo

    def _L1_ffn_ref(hidden_states, gate_w, w_gate, w_up, w_down):
        import jax, jax.numpy as jnp
        import numpy as np
        B, S, H = (2, 128, 128)
        E, F, K = (8, 352, 2)
        NORM_TOPK = True
        b, s, h = hidden_states.shape
        x = hidden_states.reshape(-1, h)
        T = x.shape[0]
        n_experts = w_gate.shape[0]
        logits = x @ gate_w
        probs = jax.nn.softmax(logits.astype(jnp.float32), axis=-1)
        top_w, sel = jax.lax.top_k(probs, K)
        if NORM_TOPK:
            top_w = top_w / top_w.sum(axis=-1, keepdims=True)
        top_w = top_w.astype(x.dtype)
        combine = jnp.zeros((T, n_experts), x.dtype)
        combine = combine.at[jnp.arange(T)[:, None], sel].add(top_w)
        g = jnp.einsum('td,edf->tef', x, w_gate)
        u = jnp.einsum('td,edf->tef', x, w_up)
        hcur = jax.nn.silu(g) * u
        y = jnp.einsum('tef,efd->ted', hcur, w_down)
        out = jnp.einsum('ted,te->td', y, combine)
        return out.reshape(b, s, h)
    x = L0_attn_x
    x = _layernorm(x + _L0_attn_ref(x, L0_attn_w_qkv, L0_attn_b_qkv, L0_attn_w_out, L0_attn_b_out), axis=-1)
    x = _layernorm(x + _L0_ffn_ref(x, L0_ffn_norm_g, L0_ffn_norm_b, L0_ffn_slot_g, L0_ffn_slot_b, L0_ffn_scale, L0_ffn_slot_embeds, L0_ffn_Wg, L0_ffn_bg, L0_ffn_Wu, L0_ffn_bu, L0_ffn_Wd, L0_ffn_bd), axis=-1)
    x = _layernorm(x + _L1_attn_ref(x, L1_attn_Wq, L1_attn_bq, L1_attn_Wkv_down, L1_attn_bkv_down, L1_attn_Wkv_up, L1_attn_bkv_up, L1_attn_Wo, L1_attn_bo), axis=-1)
    x = _layernorm(x + _L1_ffn_ref(x, L1_ffn_gate_w, L1_ffn_w_gate, L1_ffn_w_up, L1_ffn_w_down), axis=-1)
    return x

_drawn_inputs = setup_inputs


def setup_inputs(seed=0):
    import zlib

    import numpy as np

    out = dict(_drawn_inputs(seed))
    spreads = {'L0_attn_b_qkv': (0.0, 0.1),
     'L0_attn_b_out': (0.0, 0.1),
     'L0_ffn_norm_g': (1.0, 0.2),
     'L0_ffn_norm_b': (0.0, 0.1),
     'L0_ffn_slot_g': (1.0, 0.2),
     'L0_ffn_slot_b': (0.0, 0.1),
     'L0_ffn_bg': (0.0, 0.1),
     'L0_ffn_bu': (0.0, 0.1),
     'L0_ffn_bd': (0.0, 0.1),
     'L1_attn_bq': (0.0, 0.509),
     'L1_attn_bkv_down': (0.0, 0.1),
     'L1_attn_bkv_up': (0.0, 0.1),
     'L1_attn_bo': (0.0, 0.1)}
    factors = {'L1_ffn_gate_w': 8.0, 'L1_ffn_w_gate': 8.0, 'L1_ffn_w_up': 8.0, 'L1_ffn_w_down': 8.0}
    for name, (base, spread) in spreads.items():
        noise = np.random.default_rng([zlib.crc32(name.encode()), seed]).standard_normal(out[name].shape)
        drawn = base * np.exp(spread * noise) if base else spread * noise
        out[name] = jnp.asarray(drawn.astype(out[name].dtype))
    for name, factor in factors.items():
        out[name] = (out[name] * factor).astype(out[name].dtype)
    return out
```

```python
import numpy as np
from contextlib import ExitStack

import concourse.bass as bass
from concourse import mybir

F32 = mybir.dt.float32
F32R = mybir.dt.float32r
I32 = mybir.dt.int32
U32 = mybir.dt.uint32
ALU = mybir.AluOpType
ACT = mybir.ActivationFunctionType
AX = mybir.AxisListType

P = 128
B, T, D = 4, 512, 128
NB = T // P
NT = B * NB
H0, HD0 = 16, 64
E0, S0, F0 = 16, 64, 256
ST = E0 * S0 // P
H1, HD1, LAT = 16, 8, 32
G1 = 4
HG = H1 // G1
E1, F1 = 8, 352
FT = (F1 + P - 1) // P
EPS = 1e-5


def wait(eng, sem, value):
    if not isinstance(value, int) or value > 0:
        eng.wait_ge(sem, value)


class Counted:

    def __init__(self, sem):
        self.sem, self.base = sem, 0

    def wait(self, eng, n):
        if n > 0:
            eng.wait_ge(self.sem, self.base + n)

    def done(self, n):
        self.base += n


class Phase:

    def __init__(self, nc, tag):
        self.nc, self.tag, self.stack = nc, tag, ExitStack()

    def sb(self, name, shape, dt=F32):
        return self.stack.enter_context(self.nc.sbuf_tensor(f"{self.tag}_{name}", shape, dt))

    def ps(self, name, shape, dt=F32):
        return self.stack.enter_context(self.nc.psum_tensor(f"{self.tag}_{name}", shape, dt))

    def sem(self, name):
        return self.stack.enter_context(self.nc.semaphore(f"{self.tag}_{name}"))

    def __enter__(self):
        return self

    def __exit__(self, *a):
        return self.stack.__exit__(*a)


def pipeline(eng, stages, per, iters):
    for u in range(per):
        for stage, lag in stages:
            if u >= lag:
                stage(0, u - lag)
    with eng.Fori(1, iters) as i:
        for u in range(per):
            for stage, lag in stages:
                stage(i if u >= lag else i - 1, (u - lag) % per)
    for u in range(max(lag for _, lag in stages)):
        for stage, lag in stages:
            if u < lag:
                stage(iters - 1, per + u - lag)


def transpose_tokens(nc, tag, sems, src, dst, ident, tiles=NT):
    s_t, s_c = sems["turned"], sems["turn_copied"]
    with Phase(nc, tag) as ph:
        pt = [ph.ps(f"pt{k}", [P, T]) for k in range(2)]
        with nc.Block() as block:
            @block.tensor
            def _(pe):
                for b in range(tiles // NB):
                    s_c.wait(pe, b - 1)
                    for n in range(NB):
                        last = nc.tensor.transpose(pt[b % 2][:, n * P:(n + 1) * P], src[:, b * NB + n, :], ident[:, :])
                    last.then_inc(s_t.sem, 1)

            @block.vector
            def _(v):
                for b in range(tiles // NB):
                    s_t.wait(v, b + 1)
                    nc.vector.tensor_copy(dst[:, b * T:(b + 1) * T], pt[b % 2][:, :]).then_inc(s_c.sem, 1)
    s_t.done(tiles // NB)
    s_c.done(tiles // NB)


def norm_rows(nc, tag, sems, src, dst, tiles, epsc, gain=None, shift=None, scale=None, out=None):
    s_st, s_mv, s_sd, s_r, s_x = (sems[n] for n in ("stats", "mean_var", "std", "rstd", "normed"))
    s_g, s_y, s_out = (sems[n] for n in ("gained", "shifted", "out"))
    with Phase(nc, tag) as ph:
        stats, mv = ph.sb("stats", [P, tiles, 6]), ph.sb("mv", [P, tiles, 2])
        std, rstd = ph.sb("std", [P, tiles]), ph.sb("rstd", [P, tiles])
        with nc.Block() as block:
            @block.vector
            def _(v):
                for t in range(tiles):
                    nc.vector.bn_stats(stats[:, t, :], src[:, t, :]).then_inc(s_st.sem, 1)
                for t in range(tiles):
                    s_st.wait(v, t + 1)
                    nc.vector.bn_aggr(mv[:, t, :], stats[:, t, :]).then_inc(s_mv.sem, 1)
                s_sd.wait(v, 1)
                nc.vector.reciprocal(rstd[:, :], std[:, :]).then_inc(s_r.sem, 1)
                s_r.wait(v, 1)
                for t in range(tiles):
                    nc.vector.tensor_scalar(dst[:, t, :], src[:, t, :], mv[:, t, 0:1], rstd[:, t:t + 1],
                                            ALU.subtract, ALU.mult).then_inc(s_x.sem, 1)
                if gain is not None:
                    s_x.wait(v, tiles)
                    wide = [P, tiles, D]
                    nc.vector.tensor_tensor(dst[:, :, :], dst[:, :, :], gain.unsqueeze(1).broadcast_to(wide),
                                            ALU.mult).then_inc(s_g.sem, 1)
                    s_g.wait(v, 1)
                    nc.vector.tensor_tensor(dst[:, :, :], dst[:, :, :], shift.unsqueeze(1).broadcast_to(wide),
                                            ALU.add).then_inc(s_y.sem, 1)
                    if scale is not None:
                        s_y.wait(v, 1)
                        nc.vector.tensor_scalar(dst[:, :, :], dst[:, :, :], scale[:, 0:1], None, ALU.mult)

            @block.scalar
            def _(a):
                s_mv.wait(a, tiles)
                nc.scalar.activation(std[:, :], mv[:, :, 1], ACT.Sqrt, bias=epsc[:, 0:1]).then_inc(s_sd.sem, 1)

            if out is not None:
                @block.sync
                def _(sp):
                    for b in range(B):
                        s_x.wait(sp, NB * (b + 1))
                        sp.dma_start(out[b].rearrange("(n p) d -> p n d", p=P),
                                     dst[:, b * NB:(b + 1) * NB, :]).then_inc(s_out.sem, 16)
                    s_out.wait(sp, 16 * B)
    for s, n in ((s_st, tiles), (s_mv, tiles), (s_sd, 1), (s_r, 1), (s_x, tiles)):
        s.done(n)
    if gain is not None:
        s_g.done(1)
        s_y.done(1)


def load_columns(nc, tag, ident, jobs):
    with Phase(nc, tag) as ph:
        rows = [ph.sb(f"rows{k}", [P, P]) for k in range(len(jobs))]
        pt = [ph.ps(f"pt{k}", [P, P]) for k in range(len(jobs))]
        s_l, s_t, s_c = ph.sem("loaded"), ph.sem("transposed"), ph.sem("copied")
        total = 16 * sum(len(j[0]) for j in jobs)
        with nc.Block() as block:
            @block.sync
            def _(sp):
                for k, (parts, r, n, dst) in enumerate(jobs):
                    for r0, c0, src in parts:
                        sp.dma_start(rows[k][r0:r0 + src.shape[0], c0:c0 + src.shape[1]], src).then_inc(s_l, 16)

            @block.tensor
            def _(pe):
                pe.wait_ge(s_l, total)
                for k, (parts, r, n, dst) in enumerate(jobs):
                    nc.tensor.transpose(pt[k][0:n, 0:r], rows[k][0:r, 0:n], ident[0:r, 0:r]).then_inc(s_t, 1)

            @block.vector
            def _(v):
                for k, (parts, r, n, dst) in enumerate(jobs):
                    v.wait_ge(s_t, k + 1)
                    nc.vector.tensor_copy(dst[0:n, 0:r], pt[k][0:n, 0:r]).then_inc(s_c, 1)


GT = P // H0
GC = P // GT
NOT_OWN = -2.0 ** 100


def attention0(nc, x_nat, xT, ident, w_qkv, bias, w_out, b_out, posT_in, own_in):
    SL = 4 * NB
    L_S, L_R, L_T, L_PV, L_Y = 4, 5, 7, 8, 9
    with Phase(nc, "a0") as ph:
        w = ph.sb("w", [P, 3, H0 // 2, 2, HD0])
        posb = ph.sb("posb", [P, 2, 4, T])
        posT = ph.sb("posT", [P, T])
        QKV = [ph.sb(n, [P, 2, P, H0]) for n in ("q", "k", "v")]
        V = ph.sb("vrows", [P, 8, 4, HD0])
        PR = ph.sb("probs", [P, 4, 4, P])
        PT = ph.sb("probsT", [P, 2, 4, P])
        OT = ph.sb("oT", [P, 2, P, H0 // 2])
        nmax, sums, rsum = (ph.sb(n, [P, 4, 4]) for n in ("nmax", "sums", "rsum"))
        wo, bo = ph.sb("wo", [P, H0 // 2, D]), ph.sb("bo", [P, D])
        PJ = [ph.ps(f"proj{k}", [P, 4, P]) for k in range(2)]
        SC = [ph.ps(f"scores{k}", [P, 4, P]) for k in range(2)]
        TB, VB, OB, Y = (ph.ps(n, [P, 4, P]) for n in ("turned", "vturned", "outT", "y"))
        s_w, s_c, s_wo, s_z, s_pb = (ph.sem(n) for n in ("weights", "constants", "wout", "zeros", "posb_"))
        s_pj, s_pe, s_S, s_mx, s_e, s_r, s_n = (ph.sem(n) for n in ("projected", "proj_in", "scored", "maxed", "exped", "recip", "normed"))
        s_vt, s_vc, s_T, s_tc, s_pv, s_oa, s_od, s_y, s_x, s_xb = (
            ph.sem(n) for n in ("vturned_", "v_in", "turned_", "copied", "pv", "o_a", "o_d", "y_", "x", "xb"))

        def project(i, u):
            q, s = u // 4, u % 4
            if s == 3:
                return
            for k in range(2):
                m = 6 * q + 2 * s + k
                wait(nc.tensor, s_pe, 2 * (i * 24 + m - 1))
                for j in range(4):
                    last = nc.tensor.matmul(PJ[k][:, j, :], w[:, s, 4 * k + j, :, :].rearrange("p h d -> p (h d)"),
                                            xT[:, bass.ds(i * T + q * P, P)], start=True, stop=True)
                last.then_inc(s_pj, 1)

        def group(t, u, n):
            q, s = u // 4, u % 4
            at = (4 * s + n) * GT
            return t[:, q % 2, at:at + GT, :].rearrange("p t h -> p (t h)")

        def turn_v(i, u):
            q, s = u // 4, u % 4
            if s == 0:
                wait(nc.tensor, s_pe, 2 * (i * 24 + 6 * q + 6))
            wait(nc.tensor, s_vc, i * SL + u)
            for n in range(4):
                last = nc.tensor.transpose(VB[:, n, :], group(QKV[2], u, n), ident[:, :])
            last.then_inc(s_vt, 1)

        def scores(i, u):
            wait(nc.tensor, s_e, i * SL + u - 1)
            for n in range(4):
                last = nc.tensor.matmul(SC[u % 2][:, n, :], group(QKV[0], u, n), group(QKV[1], u, n), start=True, stop=True)
            last.then_inc(s_S, 1)

        def turn(i, u):
            wait(nc.tensor, s_n, i * SL + u + 1)
            wait(nc.tensor, s_tc, i * SL + u)
            for n in range(4):
                last = nc.tensor.transpose(TB[:, n, :], PR[:, u % 4, n, :], ident[:, :])
            last.then_inc(s_T, 1)

        def pv(i, u):
            wait(nc.tensor, s_tc, i * SL + u + 1)
            wait(nc.tensor, s_vc, i * SL + u + 1)
            wait(nc.tensor, s_oa, i * SL + u)
            wait(nc.tensor, s_od, i * SL + u)
            for n in range(4):
                last = nc.tensor.matmul(OB[0:HD0, n, :], V[:, u % 8, n, :], PT[:, u % 2, n, :], start=True, stop=True)
            last.then_inc(s_pv, 1)

        def out_proj(i, u):
            q, s = u // 4, u % 4
            if s < 3:
                return
            wait(nc.tensor, s_oa, i * SL + u + 1)
            wait(nc.tensor, s_od, i * SL + u + 1)
            wait(nc.tensor, s_x, i * NB + q)
            for m in range(H0 // 2):
                last = nc.tensor.matmul(Y[:, 0, :], OT[:, q % 2, :, m], wo[:, m, :], start=(m == 0), stop=(m == H0 // 2 - 1))
            last.then_inc(s_y, 1)

        def proj_in(i, u):
            q, s = u // 4, u % 4
            if s == 3:
                return
            n = i * SL + 4 * q - 4
            wait(nc.vector, s_vt if s == 2 else s_S, n)
            for k in range(2):
                wait(nc.vector, s_pj, i * 24 + 6 * q + 2 * s + k + 1)
                for half in range(2):
                    rows = slice(half * HD0, (half + 1) * HD0)
                    h = 8 * k + 4 * half
                    out = QKV[s][0:HD0, q % 2, :, h:h + 4].rearrange("p t h -> p h t")
                    if s == 1:
                        last = nc.vector.tensor_tensor(out, PJ[k][rows, :, :], posb[rows, k, :, q * P:(q + 1) * P], ALU.add)
                    else:
                        last = nc.vector.scalar_tensor_tensor(
                            out=out, in0=PJ[k][rows, :, :], scalar=HD0 ** -0.5 if s == 0 else 1.0,
                            in1=bias[rows, s * H0 + h:s * H0 + h + 4].unsqueeze(2).broadcast_to([HD0, 4, P]),
                            op0=ALU.mult, op1=ALU.add)
                    last.then_inc(s_pe, 1)

        def neg_max(i, u):
            wait(nc.vector, s_S, i * SL + u + 1)
            wait(nc.vector, s_e, i * SL + u - 3)
            nc.vector.tensor_reduce(nmax[:, u % 4, :], SC[u % 2][:, :, :], AX.X, ALU.max, negate=True).then_inc(s_mx, 1)

        def recip(i, u):
            wait(nc.vector, s_e, i * SL + u + 1)
            wait(nc.vector, s_n, i * SL + u - 3)
            nc.vector.reciprocal(rsum[:, u % 4, :], sums[:, u % 4, :]).then_inc(s_r, 1)

        def o_rows(u, par):
            q, s = u // 4, u % 4
            dst = OT[par * HD0:(par + 1) * HD0, q % 2, 4 * s * GT:(4 * s + 4) * GT, :]
            src = OB[0:HD0, :, :].rearrange("p n (t m r) -> p (n t) m r", t=GT, r=2)[:, :, :, par]
            return dst, src

        def o_free(eng, i, u):
            q, s = u // 4, u % 4
            if s == 0:
                wait(eng, s_y, i * NB + q - 1)

        def o_out_v(i, u):
            wait(nc.vector, s_pv, i * SL + u + 1)
            wait(nc.vector, s_oa, i * SL + u + 1)
            dst, src = o_rows(u, 1)
            o_free(nc.vector, i, u)
            nc.vector.tensor_copy(dst, src).then_inc(s_od, 1)

        def add(i, u):
            q, s = u // 4, u % 4
            if s < 3:
                return
            wait(nc.vector, s_y, i * NB + q + 1)
            x = x_nat[:, bass.ds(i * NB + q, 1), :].rearrange("p o d -> p (o d)")
            nc.vector.tensor_tensor(x, Y[:, 0, :], x, ALU.add).then_inc(s_x, 1)

        def exps(i, u):
            wait(nc.scalar, s_mx, i * SL + u + 1)
            wait(nc.scalar, s_r, i * SL + u - 3)
            wait(nc.scalar, s_T, i * SL + u - 3)
            for n in range(4):
                last = nc.scalar.activation(PR[:, u % 4, n, :], SC[u % 2][:, n, :], ACT.Exp,
                                            bias=nmax[:, u % 4, n:n + 1], accum_out=sums[:, u % 4, n:n + 1])
            last.then_inc(s_e, 1)

        def v_in(i, u):
            wait(nc.scalar, s_vt, i * SL + u + 1)
            wait(nc.scalar, s_pv, i * SL + u - 7)
            nc.scalar.activation(V[:, u % 8, :, :], VB[:, :, 0:HD0], ACT.Copy).then_inc(s_vc, 1)

        def copy_turned(i, u):
            wait(nc.scalar, s_T, i * SL + u + 1)
            wait(nc.scalar, s_pv, i * SL + u - 1)
            nc.scalar.activation(PT[:, u % 2, :, :], TB[:, :, :], ACT.Copy).then_inc(s_tc, 1)

        def o_out_a(i, u):
            wait(nc.scalar, s_pv, i * SL + u + 1)
            dst, src = o_rows(u, 0)
            o_free(nc.scalar, i, u)
            nc.scalar.activation(dst, src, ACT.Copy).then_inc(s_oa, 1)

        def normalise(i, u):
            wait(nc.gpsimd, s_r, i * SL + u + 1)
            pr = PR[:, u % 4, :, :]
            nc.gpsimd.tensor_tensor(pr, pr, rsum[:, u % 4, :].unsqueeze(2).broadcast_to([P, 4, P]), ALU.mult).then_inc(s_n, 1)

        with nc.Block() as block:
            @block.sync
            def _(sp):
                for c in range(3):
                    for k in range(2):
                        for half in range(2):
                            h = 8 * k + 4 * half
                            sp.dma_start(w[:, c, 4 * k:4 * k + 4, half, :],
                                         w_qkv.rearrange("p (h c d) -> p c h d", h=H0, c=3)[:, c, h:h + 4, :]).then_inc(s_w, 16)
                sp.dma_start(posT[:, :], posT_in).then_inc(s_c, 16)
                sp.wait_ge(s_z, 3)
                for t in range(2):
                    for par in range(2):
                        sp.dma_start(QKV[t][HD0:HD0 + GT, par, :, :].rearrange("p t h -> p (t h)"), own_in[t]).then_inc(s_c, 16)
                sp.dma_start(wo[:, :, :], w_out.rearrange("(k p) n -> p k n", p=P)).then_inc(s_wo, 16)
                sp.dma_start(bo[:, :], b_out[None, :].broadcast_to([P, D])).then_inc(s_wo, 16)

            @block.tensor
            def _(pe):
                pe.wait_ge(s_w, 16 * 12)
                pe.wait_ge(s_c, 16 * 5)
                pe.wait_ge(s_wo, 32)
                pipeline(pe, [(turn, L_T), (project, 0), (turn_v, L_S), (scores, L_S), (pv, L_PV), (out_proj, L_Y)], SL, B)

            @block.vector
            def _(v):
                for t in QKV:
                    nc.vector.memset(t[HD0:P, :, :, :], 0.0).then_inc(s_z, 1)
                v.wait_ge(s_wo, 32)
                nc.vector.tensor_tensor(x_nat[:, :, :], x_nat[:, :, :], bo[:, None, :].broadcast_to([P, NT, D]), ALU.add).then_inc(s_xb, 1)
                v.wait_ge(s_c, 16 * 5)
                for half in range(2):
                    rows = slice(half * HD0, (half + 1) * HD0)
                    for k in range(2):
                        h = H0 + 8 * k + 4 * half
                        nc.vector.tensor_tensor(posb[rows, k, :, :], posT[rows, None, :].broadcast_to([HD0, 4, T]),
                                                bias[rows, h:h + 4].unsqueeze(2).broadcast_to([HD0, 4, T]), ALU.add).then_inc(s_pb, 1)
                v.wait_ge(s_xb, 1)
                v.wait_ge(s_pb, 4)
                pipeline(v, [(proj_in, 0), (neg_max, L_S), (recip, L_R), (o_out_v, L_PV), (add, L_Y)], SL, B)

            @block.scalar
            def _(a):
                pipeline(a, [(copy_turned, L_T), (v_in, L_S), (exps, L_S), (o_out_a, L_PV)], SL, B)

            @block.gpsimd
            def _(g):
                pipeline(g, [(normalise, L_R)], SL, B)


def dispatch0(nc, xn, xnT, seT, slotsT, ident):
    L_T, L_M = 2, 3
    with Phase(nc, "d0") as ph:
        xs = ph.sb("xs", [P, 2, NB, D])
        DI = ph.sb("dispatch", [P, 2, T])
        DT = ph.sb("dispatchT", [P, 2, NB, P])
        nmax, sums, rsum = (ph.sb(n, [P, 2, 1]) for n in ("nmax", "sums", "rsum"))
        LG = [ph.ps(f"logits{k}", [P, T]) for k in range(2)]
        TB = [ph.ps(f"turned{k}", [P, NB, P]) for k in range(2)]
        SB_ = [ph.ps(f"slots{k}", [P, T]) for k in range(2)]
        s_xs, s_l, s_mx, s_e, s_r, s_n, s_T, s_t, s_m, s_o = (
            ph.sem(n) for n in ("xs_in", "logits_", "maxed", "exped", "recip", "normed", "turned_", "copied", "mixed", "out"))

        def logits(b, u):
            wait(nc.tensor, s_e, b * ST + u - 1)
            nc.tensor.matmul(LG[u % 2][:, :], seT[:, u * P:(u + 1) * P], xnT[:, bass.ds(b * T, T)],
                             start=True, stop=True).then_inc(s_l, 1)

        def turn(b, u):
            wait(nc.tensor, s_n, b * ST + u + 1)
            wait(nc.tensor, s_t, b * ST + u - 1)
            for n in range(NB):
                last = nc.tensor.transpose(TB[u % 2][:, n, :], DI[:, u % 2, n * P:(n + 1) * P], ident[:, :])
            last.then_inc(s_T, 1)

        def mix(b, u):
            wait(nc.tensor, s_t, b * ST + u + 1)
            if u == 0:
                wait(nc.tensor, s_xs, b + 1)
            wait(nc.tensor, s_o, b * ST + u - 1)
            for n in range(NB):
                last = nc.tensor.matmul(SB_[u % 2][:, 0:P], xs[:, 0, n, :], DT[:, u % 2, n, :],
                                        start=(n == 0), stop=(n == NB - 1))
            last.then_inc(s_m, 1)

        def neg_max(b, u):
            wait(nc.vector, s_l, b * ST + u + 1)
            wait(nc.vector, s_e, b * ST + u - 1)
            nc.vector.tensor_reduce(nmax[:, u % 2, :], LG[u % 2][:, :], AX.X, ALU.max, negate=True).then_inc(s_mx, 1)

        def recip(b, u):
            wait(nc.vector, s_e, b * ST + u + 1)
            wait(nc.vector, s_n, b * ST + u - 1)
            nc.vector.reciprocal(rsum[:, u % 2, :], sums[:, u % 2, :]).then_inc(s_r, 1)

        def copy_turned(b, u):
            wait(nc.vector, s_T, b * ST + u + 1)
            wait(nc.vector, s_m, b * ST + u - 1)
            nc.vector.tensor_copy(DT[:, u % 2, :, :], TB[u % 2][:, :, :]).then_inc(s_t, 1)

        def exps(b, u):
            wait(nc.scalar, s_mx, b * ST + u + 1)
            wait(nc.scalar, s_r, b * ST + u - 1)
            wait(nc.scalar, s_T, b * ST + u - 1)
            nc.scalar.activation(DI[:, u % 2, :], LG[u % 2][:, :], ACT.Exp, bias=nmax[:, u % 2, :],
                                 accum_out=sums[:, u % 2, :]).then_inc(s_e, 1)

        def slots_out(b, u):
            wait(nc.scalar, s_m, b * ST + u + 1)
            nc.scalar.activation(slotsT[:, bass.ds(b, 1), u * P:(u + 1) * P].rearrange("p o s -> p (o s)"),
                                 SB_[u % 2][:, 0:P], ACT.Copy).then_inc(s_o, 1)

        def stage_x(b, u):
            if u == 0:
                wait(nc.gpsimd, s_m, b * ST)
                nc.gpsimd.tensor_copy(xs[:, 0, :, :], xn[:, bass.ds(b * NB, NB), :]).then_inc(s_xs, 1)

        def normalise(b, u):
            wait(nc.gpsimd, s_r, b * ST + u + 1)
            nc.gpsimd.tensor_tensor(DI[:, u % 2, :], DI[:, u % 2, :], rsum[:, u % 2, :].broadcast_to([P, T]),
                                    ALU.mult).then_inc(s_n, 1)

        with nc.Block() as block:
            @block.tensor
            def _(pe):
                pipeline(pe, [(logits, 0), (turn, L_T), (mix, L_M)], ST, B)

            @block.vector
            def _(v):
                pipeline(v, [(neg_max, 0), (recip, 1), (copy_turned, L_T)], ST, B)

            @block.scalar
            def _(a):
                pipeline(a, [(exps, 0), (slots_out, L_M)], ST, B)

            @block.gpsimd
            def _(g):
                pipeline(g, [(normalise, 1), (stage_x, L_M)], ST, B)


def experts0(nc, ident, slotsT, eout, bgT, buT, Wg, Wu, Wd, bd):
    R, C = 4, B * S0
    KF = F0 // P
    with Phase(nc, "e0") as ph:
        wg, wu = ph.sb("wg", [P, R, F0]), ph.sb("wu", [P, R, F0])
        wd = ph.sb("wd", [P, R, KF, D])
        bdb = ph.sb("bd", [P, ST, D])
        h, hu = ph.sb("h", [P, 2, KF, C]), ph.sb("hu", [P, 2, KF, C])
        G = [ph.ps(f"gate{k}", [P, KF, C]) for k in range(2)]
        U = [ph.ps(f"up{k}", [P, KF, C]) for k in range(2)]
        EO = [ph.ps(f"out{k}", [P, B, D]) for k in range(2)]
        s_w = [ph.sem(f"weights{q}") for q in range(R)]
        s_bd, s_g, s_h, s_m, s_d, s_o = (ph.sem(n) for n in ("bd_in", "gated", "gelu", "times", "down", "out_"))

        def load(sp, i, q):
            e = i * R + q
            sp.dma_start(wg[:, q, :], Wg[bass.ds(e, 1)].rearrange("o d f -> d (o f)")).then_inc(s_w[q], 16)
            sp.dma_start(wu[:, q, :], Wu[bass.ds(e, 1)].rearrange("o d f -> d (o f)")).then_inc(s_w[q], 16)
            sp.dma_start(wd[:, q, :, :], Wd[bass.ds(e, 1)].rearrange("o (k p) n -> p (o k) n", p=P)).then_inc(s_w[q], 16)

        def gate_up(i, u):
            n = i * R + u
            wait(nc.tensor, s_w[u], (i + 1) * 48)
            wait(nc.tensor, s_m, n - 1)
            for bank, ww in ((G, wg), (U, wu)):
                for k in range(KF):
                    last = nc.tensor.matmul(bank[u % 2][:, k, :].rearrange("p (b s) -> p b s", b=B),
                                            ww[:, u, k * P:(k + 1) * P],
                                            slotsT[:, :, bass.ds(n * S0, S0)], start=True, stop=True)
            last.then_inc(s_g, 1)

        def down(i, u):
            n = i * R + u
            wait(nc.tensor, s_m, n + 1)
            wait(nc.tensor, s_o, i * (R // 2) + u // 2 - 1)
            for b in range(B):
                for k in range(KF):
                    last = nc.tensor.matmul(EO[u // 2][(u % 2) * S0:(u % 2 + 1) * S0, b, :],
                                            hu[:, u % 2, k, b * S0:(b + 1) * S0], wd[:, u, k, :],
                                            start=(k == 0), stop=(k == KF - 1))
            last.then_inc(s_d, 1)

        def gelu(i, u):
            n = i * R + u
            wait(nc.scalar, s_g, n + 1)
            wait(nc.scalar, s_m, n - 1)
            for k in range(KF):
                last = nc.scalar.activation(h[:, u % 2, k, :], G[u % 2][:, k, :], ACT.Gelu,
                                            bias=bgT[:, bass.ds(n * KF + k, 1)])
            last.then_inc(s_h, 1)

        def times(i, u):
            n = i * R + u
            wait(nc.vector, s_h, n + 1)
            wait(nc.vector, s_d, n - 1)
            for k in range(KF):
                last = nc.vector.scalar_tensor_tensor(out=hu[:, u % 2, k, :], in0=U[u % 2][:, k, :],
                                                      scalar=buT[:, bass.ds(n * KF + k, 1)], in1=h[:, u % 2, k, :],
                                                      op0=ALU.add, op1=ALU.mult)
            last.then_inc(s_m, 1)

        def out(i, u):
            if u % 2 == 1:
                n = i * R + u
                wait(nc.vector, s_d, n + 1)
                st = i * (R // 2) + u // 2
                nc.vector.tensor_tensor(eout[:, bass.ds(st, 1), :, :].rearrange("p o b d -> p (o b) d"), EO[u // 2][:, :, :],
                                        bdb[:, bass.ds(st, 1), :].broadcast_to([P, B, D]),
                                        ALU.add).then_inc(s_o, 1)

        with nc.Block() as block:
            @block.sync
            def _(sp):
                for q in range(2):
                    src = bd.rearrange("(t q) d -> q t d", q=2)[q:q + 1]
                    sp.dma_start(bdb[q * S0:(q + 1) * S0, :, :], src.broadcast_to([S0, ST, D])).then_inc(s_bd, 16)
                for q in range(R):
                    load(sp, 0, q)
                with sp.Fori(1, E0 // R) as i:
                    for q in range(R):
                        sp.wait_ge(s_d, i * R + q - R + 1)
                        load(sp, i, q)

            @block.tensor
            def _(pe):
                pipeline(pe, [(gate_up, 0), (down, 1)], R, E0 // R)

            @block.scalar
            def _(a):
                pipeline(a, [(gelu, 0)], R, E0 // R)

            @block.vector
            def _(v):
                v.wait_ge(s_bd, 32)
                pipeline(v, [(times, 0), (out, 1)], R, E0 // R)


def combine0(nc, x_nat, xnT, seT, eout, ident):
    L_T, L_Y = 1, 2
    with Phase(nc, "c0") as ph:
        xs = ph.sb("xs", [P, T])
        CO = ph.sb("combine", [P, 2, ST * P])
        CT = ph.sb("combineT", [P, 2, ST, P])
        nmax = ph.sb("nmax", [P, 2, 1])
        sums, rsum = ph.sb("sums", [P, 4, 1]), ph.sb("rsum", [P, 4, 1])
        LG = [ph.ps(f"logits{k}", [P, ST * P]) for k in range(2)]
        TB = ph.ps("turned", [P, ST, P])
        Y = [ph.ps(f"y{k}", [P, T]) for k in range(2)]
        s_xs, s_l, s_mx, s_e, s_r, s_T, s_ta, s_td, s_y, s_o = (
            ph.sem(n) for n in ("xs_in", "logits_", "maxed", "exped", "recip", "turned_", "copied_a", "copied_d", "mixed", "out"))
        HS = ST // 2

        def logits(b, u):
            if u == 0:
                wait(nc.tensor, s_xs, b + 1)
            wait(nc.tensor, s_e, b * NB + u - 1)
            for k in range(2):
                last = nc.tensor.matmul(LG[u % 2][:, k * T:(k + 1) * T], xs[:, u * P:(u + 1) * P],
                                        seT[:, k * T:(k + 1) * T], start=True, stop=True)
            last.then_inc(s_l, 1)

        def turn(b, u):
            wait(nc.tensor, s_e, b * NB + u + 1)
            wait(nc.tensor, s_ta, b * NB + u)
            wait(nc.tensor, s_td, b * NB + u)
            for k in range(ST):
                last = nc.tensor.transpose(TB[:, k, :], CO[:, u % 2, k * P:(k + 1) * P], ident[:, :])
            last.then_inc(s_T, 1)

        def mix(b, u):
            wait(nc.tensor, s_ta, b * NB + u + 1)
            wait(nc.tensor, s_td, b * NB + u + 1)
            wait(nc.tensor, s_o, b * NB + u - 1)
            for k in range(ST):
                last = nc.tensor.matmul(Y[u % 2][:, 0:D], CT[:, u % 2, k, :],
                                        eout[:, k, bass.ds(b, 1), :].rearrange("p o d -> p (o d)"),
                                        start=(k == 0), stop=(k == ST - 1))
            last.then_inc(s_y, 1)

        def neg_max(b, u):
            wait(nc.vector, s_l, b * NB + u + 1)
            wait(nc.vector, s_e, b * NB + u - 1)
            nc.vector.tensor_reduce(nmax[:, u % 2, :], LG[u % 2][:, :], AX.X, ALU.max, negate=True).then_inc(s_mx, 1)

        def recip(b, u):
            wait(nc.vector, s_e, b * NB + u + 1)
            wait(nc.vector, s_o, b * NB + u - 3)
            nc.vector.reciprocal(rsum[:, u % 4, :], sums[:, u % 4, :]).then_inc(s_r, 1)

        def copy_turned_v(b, u):
            wait(nc.vector, s_T, b * NB + u + 1)
            wait(nc.vector, s_y, b * NB + u - 1)
            nc.vector.tensor_copy(CT[:, u % 2, 0:HS, :], TB[:, 0:HS, :]).then_inc(s_td, 1)

        def add(b, u):
            wait(nc.vector, s_y, b * NB + u + 1)
            wait(nc.vector, s_r, b * NB + u + 1)
            x = x_nat[:, bass.ds(b * NB + u, 1), :].rearrange("p o d -> p (o d)")
            nc.vector.scalar_tensor_tensor(out=x, in0=Y[u % 2][:, 0:D], scalar=rsum[:, u % 4, :], in1=x,
                                           op0=ALU.mult, op1=ALU.add).then_inc(s_o, 1)

        def exps(b, u):
            wait(nc.scalar, s_mx, b * NB + u + 1)
            wait(nc.scalar, s_r, b * NB + u - 3)
            wait(nc.scalar, s_T, b * NB + u - 1)
            nc.scalar.activation(CO[:, u % 2, :], LG[u % 2][:, :], ACT.Exp, bias=nmax[:, u % 2, :],
                                 accum_out=sums[:, u % 4, :]).then_inc(s_e, 1)

        def copy_turned_a(b, u):
            wait(nc.scalar, s_T, b * NB + u + 1)
            wait(nc.scalar, s_y, b * NB + u - 1)
            nc.scalar.activation(CT[:, u % 2, HS:ST, :], TB[:, HS:ST, :], ACT.Copy).then_inc(s_ta, 1)

        with nc.Block() as block:
            @block.gpsimd
            def _(g):
                nc.gpsimd.tensor_copy(xs[:, :], xnT[:, 0:T]).then_inc(s_xs, 1)
                with g.Fori(1, B) as b:
                    g.wait_ge(s_l, b * NB)
                    nc.gpsimd.tensor_copy(xs[:, :], xnT[:, bass.ds(b * T, T)]).then_inc(s_xs, 1)

            @block.tensor
            def _(pe):
                pipeline(pe, [(logits, 0), (turn, L_T), (mix, L_Y)], NB, B)

            @block.vector
            def _(v):
                pipeline(v, [(neg_max, 0), (recip, 1), (copy_turned_v, L_T), (add, L_Y)], NB, B)

            @block.scalar
            def _(a):
                pipeline(a, [(exps, 0), (copy_turned_a, L_T)], NB, B)


RS = 4 * HD1


def prepare1(nc, xT, ident, qsT, ksT, vN, infT, bias, ones, Wq, Wkvd, Wkvu, bkvu, cos_in, sin_in):
    W4, HALF = [P, NB, H1, HD1], HD1 // 2
    TURNS = 2 * G1 + 1
    with Phase(nc, "p1") as ph:
        wq, wd, wu = ph.sb("wq", [P, D]), ph.sb("wd", [P, LAT]), ph.sb("wu", [LAT, 2 * D])
        bu = ph.sb("bu", [P, 2 * D])
        cos, sin = ph.sb("cos", [P, NB, HALF]), ph.sb("sin", [P, NB, HALF])
        qT, cT = ph.sb("qT", [P, T]), ph.sb("cT", [LAT, T])
        kv = ph.sb("kv", [P, NB, H1, 2 * HD1])
        x, rot, hi, st = ({s: ph.sb(n + s, sh) for s in "qk"} for n, sh in
                          (("x", W4), ("rot", W4), ("hi", W4), ("st", [P, NB * H1, 4, HD1])))
        tt = {s: [ph.sb(f"t{k}{s}", [P, NB, H1, HALF]) for k in range(4)] for s in "qk"}
        rs = ph.sb("rs", W4)
        prod, inf = ph.sb("prod", W4), ph.sb("inf", W4)
        score, gate, gate2 = (ph.sb(n, [P, NB, H1]) for n in ("score", "gate", "gate2"))
        PQ, PN, PC = ph.ps("pq", [P, T]), ph.ps("pn", [P, T]), ph.ps("pc", [P, T])
        KV = ph.ps("pkv", [P, NB, 2 * D])
        PM = ph.ps("pmean", [P, T])
        PT = [ph.ps(f"turned{k}", [P, T]) for k in range(2)]
        s_w, s_pq, s_qT, s_pc, s_cT, s_pn, s_kv = (ph.sem(n) for n in ("weights", "pq_", "qT_", "pc_", "cT_", "pn_", "pkv_"))
        s_x = {s: ph.sem("x_" + s) for s in "qk"}
        s_t = {s: ph.sem("products_" + s) for s in "qk"}
        s_rot = {s: ph.sem("rotated_" + s) for s in "qk"}
        s_hi = {s: ph.sem("high_" + s) for s in "qk"}
        s_st = {s: ph.sem("stacked_" + s) for s in "qk"}
        s_sc, s_rs, s_v, s_mn, s_pr, s_g, s_g2, s_inf, s_tt, s_to = (
            ph.sem(n) for n in ("score_", "scaled", "v_", "mean", "prod_", "gate_", "gate2_", "inf_", "tt", "to"))

        def sequences(eng, fn):
            fn(0)
            with eng.Fori(1, B) as b:
                fn(b)

        def flat(t):
            return t[:, :, :, :].rearrange("p n h d -> p (n h d)")

        def rotate(eng, e, s, b):
            c4, s4 = (t[:, :, None, :].broadcast_to([P, NB, H1, HALF]) for t in (cos, sin))
            x1, x2 = x[s][:, :, :, 0:HALF], x[s][:, :, :, HALF:HD1]
            t = tt[s]
            eng.wait_ge(s_x[s], b + 1)
            for k, (i0, i1) in enumerate(((x1, c4), (x2, s4), (x1, s4), (x2, c4))):
                e.tensor_tensor(t[k][:, :, :, :], i0, i1, ALU.mult).then_inc(s_t[s], 1)
            eng.wait_ge(s_t[s], (b + 1) * 4)
            e.tensor_tensor(rot[s][:, :, :, 0:HALF], t[0][:, :, :, :], t[1][:, :, :, :], ALU.subtract).then_inc(s_rot[s], 1)
            e.tensor_tensor(rot[s][:, :, :, HALF:HD1], t[2][:, :, :, :], t[3][:, :, :, :], ALU.add).then_inc(s_rot[s], 1)

        def high(src, s, b):
            nc.vector.tensor_scalar(flat(hi[s]).bitcast(I32), flat(src).bitcast(I32), -4096, None,
                                    ALU.bitwise_and).then_inc(s_hi[s], 1)

        def stack(eng, e, src, s, b):
            eng.wait_ge(s_hi[s], b + 1)
            wide = [P, NB * H1, 2, HD1]
            w = lambda t: t[:, :, :, :].rearrange("p n h d -> p (n h) d")[:, :, None, :].broadcast_to(wide)
            out = (st[s][:, :, 0:2, :], st[s][:, :, 2:4, :]) if s == "q" else (st[s][:, :, 0:4:2, :], st[s][:, :, 1:4:2, :])
            e.tensor_tensor(out[1], w(src), w(hi[s]), ALU.subtract).then_inc(s_st[s], 1)
            e.tensor_copy(out[0], w(hi[s])).then_inc(s_st[s], 1)

        with nc.Block() as block:
            @block.sync
            def _(sp):
                for dst, src in ((wq[:, :], Wq), (wd[:, :], Wkvd), (wu[:, :], Wkvu),
                                 (bu[:, :], bkvu[None, :].broadcast_to([P, 2 * D])),
                                 (cos[:, :, :], cos_in), (sin[:, :, :], sin_in)):
                    sp.dma_start(dst, src).then_inc(s_w, 16)

            @block.tensor
            def _(pe):
                pe.wait_ge(s_w, 96)

                def seq(b):
                    wait(pe, s_qT, b)
                    wait(pe, s_cT, b)
                    nc.tensor.matmul(PQ[:, :], wq[:, :], xT[:, bass.ds(b * T, T)], start=True, stop=True).then_inc(s_pq, 1)
                    nc.tensor.matmul(PC[0:LAT, :], wd[:, :], xT[:, bass.ds(b * T, T)], start=True, stop=True).then_inc(s_pc, 1)
                    pe.wait_ge(s_qT, b + 1)
                    wait(pe, s_x["q"], b)
                    for n in range(NB):
                        last = nc.tensor.transpose(PN[:, n * P:(n + 1) * P], qT[:, n * P:(n + 1) * P], ident[:, :])
                    last.then_inc(s_pn, 1)
                    pe.wait_ge(s_cT, b + 1)
                    wait(pe, s_x["k"], b)
                    for n in range(NB):
                        last = nc.tensor.matmul(KV[:, n, :], cT[:, n * P:(n + 1) * P], wu[:, :], start=True, stop=True)
                    last.then_inc(s_kv, 1)
                    pe.wait_ge(s_rot["k"], (b + 1) * 2)
                    wait(pe, s_inf, b)
                    for n in range(NB):
                        nc.tensor.matmul(PM[:, 0:D], ones[:, :], rot["k"][:, n, :, :].rearrange("p h d -> p (h d)"),
                                         start=(n == 0), stop=(n == NB - 1))
                    for n in range(NB):
                        last = nc.tensor.matmul(PM[:, D:2 * D], ones[:, :], kv[:, n, :, HD1:2 * HD1],
                                                start=(n == 0), stop=(n == NB - 1))
                    last.then_inc(s_mn, 1)
                    for k in range(TURNS):
                        if k == 0:
                            pe.wait_ge(s_st["q"], (b + 1) * 2)
                        if k == G1:
                            pe.wait_ge(s_st["k"], (b + 1) * 2)
                        if k == TURNS - 1:
                            pe.wait_ge(s_inf, b + 1)
                        wait(pe, s_to, b * TURNS + k - (1 if k else 0))
                        for n in range(NB):
                            if k == TURNS - 1:
                                src = inf[:, n, :, :].rearrange("p h d -> p (h d)")
                            else:
                                r = n * H1 + k % G1 * HG
                                src = st["qk"[k // G1]][:, r:r + HG, :, :].rearrange("p h r d -> p (h r d)")
                            last = nc.tensor.transpose(PT[k % 2][:, n * P:(n + 1) * P], src, ident[:, :])
                        last.then_inc(s_tt, 1)

                sequences(pe, seq)

            @block.scalar
            def _(a):
                def seq(b):
                    a.wait_ge(s_pq, b + 1)
                    wait(a, s_pn, b)
                    nc.scalar.activation(qT[:, :], PQ[:, :], ACT.Identity, bias=bias[:, 0:1]).then_inc(s_qT, 1)
                    a.wait_ge(s_pc, b + 1)
                    wait(a, s_kv, b)
                    nc.scalar.activation(cT[:, :], PC[0:LAT, :], ACT.Identity, bias=bias[0:LAT, 1:2]).then_inc(s_cT, 1)
                    for k in range(TURNS):
                        if k == TURNS - 1:
                            a.wait_ge(s_sc, b + 1)
                            nc.scalar.activation(gate[:, :, :], score[:, :, :], ACT.Sigmoid).then_inc(s_g, 1)
                        a.wait_ge(s_tt, b * TURNS + k + 1)
                        dst = (infT[:, bass.ds(b * T, T)] if k == TURNS - 1 else
                               (qsT, ksT)[k // G1][:, k % G1, bass.ds(b * T, T)])
                        nc.scalar.activation(dst, PT[k % 2][:, :], ACT.Copy).then_inc(s_to, 1)

                sequences(a, seq)

            @block.vector
            def _(v):
                v.wait_ge(s_w, 96)

                def seq(b):
                    v.wait_ge(s_pn, b + 1)
                    nc.vector.tensor_copy(flat(x["q"]), PN[:, :]).then_inc(s_x["q"], 1)
                    v.wait_ge(s_kv, b + 1)
                    wait(v, s_mn, b)
                    wait(v, s_v, b)
                    nc.vector.tensor_tensor(kv[:, :, :, :].rearrange("p n h d -> p n (h d)"), KV[:, :, :],
                                            bu[:, None, :].broadcast_to([P, NB, 2 * D]), ALU.add).then_inc(s_x["k"], 1)
                    rotate(v, nc.vector, "q", b)
                    v.wait_ge(s_rot["q"], (b + 1) * 2)
                    nc.vector.tensor_scalar(flat(rs), flat(rot["q"]), -HD1 ** -0.5, None, ALU.mult).then_inc(s_rs, 1)
                    v.wait_ge(s_rs, b + 1)
                    high(rs, "q", b)
                    wait(v, s_tt, b * TURNS)
                    stack(v, nc.vector, rs, "q", b)
                    v.wait_ge(s_rot["k"], (b + 1) * 2)
                    high(rot["k"], "k", b)
                    v.wait_ge(s_mn, b + 1)
                    nc.vector.tensor_tensor(prod[:, :, :, :].rearrange("p n h d -> p n (h d)"),
                                            rot["q"][:, :, :, :].rearrange("p n h d -> p n (h d)"),
                                            PM[:, None, 0:D].broadcast_to([P, NB, D]), ALU.mult).then_inc(s_pr, 1)
                    v.wait_ge(s_pr, b + 1)
                    nc.vector.tensor_reduce(score[:, :, :], prod[:, :, :, :], AX.X, ALU.add).then_inc(s_sc, 1)
                    v.wait_ge(s_g, b + 1)
                    nc.vector.tensor_scalar(gate2[:, :, :], gate[:, :, :], 0.2, None, ALU.mult).then_inc(s_g2, 1)
                    v.wait_ge(s_g2, b + 1)
                    nc.vector.tensor_tensor(inf[:, :, :, :], gate2[:, :, :, None].broadcast_to(W4),
                                            PM[:, D:2 * D].rearrange("p (h d) -> p h d", h=H1)[:, None, :, :].broadcast_to(W4),
                                            ALU.mult).then_inc(s_inf, 1)

                sequences(v, seq)

            @block.gpsimd
            def _(g):
                g.wait_ge(s_w, 96)
                x["k"] = kv

                def seq(b):
                    wait(g, s_mn, b)
                    rotate(g, nc.gpsimd, "k", b)
                    nc.gpsimd.tensor_copy(vN[:, bass.ds(b * NB, NB), :].rearrange("p n (h d) -> p n h d", h=H1),
                                          kv[:, :, :, HD1:2 * HD1]).then_inc(s_v, 1)
                    wait(g, s_tt, b * TURNS)
                    stack(g, nc.gpsimd, rot["k"], "k", b)

                sequences(g, seq)


def attention1(nc, x_nat, qsT, ksT, vN, infT, mask, ident, bias_in, Wo, bo_in):
    SL = 4 * G1
    TL = 4 * SL
    L_S, L_T, L_PV = 2, 6, 7
    with Phase(nc, "a1") as ph:
        bias = ph.sb("bias", [P, NB, T])
        QZ = ph.sb("qz", [P, 4, T], F32R)
        VZ = ph.sb("vz", [P, 2, NB, HG, RS])
        PR = ph.sb("probs", [P, 2, HG, NB, T])
        PT = ph.sb("probsT", [P, 2, HG, T])
        least = ph.sb("least", [P, 4, NB])
        first_v, first_g = ph.sb("first_v", [P, 4]), ph.sb("first_g", [P, 4])
        wog, wo, bo = ph.sb("wog", [P, G1, D]), ph.sb("wo", [P, D]), ph.sb("bo", [P, D])
        rec, wide = ph.sb("rec", [P, 2, NB, HG]), ph.sb("wide", [P, 2, NB, HG, RS])
        SC = [ph.ps(f"scores{k}", [P, T]) for k in range(3)]
        TB = [ph.ps(f"turned{k}", [P, 2, T]) for k in range(2)]
        OB = ph.ps("outT", [P, T])
        s_c, s_wo, s_z = ph.sem("constants"), ph.sem("wout"), ph.sem("zeros")
        s_qz, s_vz, s_S, s_b, s_e = (ph.sem(n) for n in ("q_in", "v_in", "scored", "biased", "exped"))
        s_T, s_ta, s_td, s_pv, s_o = (ph.sem(n) for n in ("turned_", "copied_a", "copied_d", "pv", "o_out"))
        s_fv, s_fg = ph.sem("first_v_"), ph.sem("first_g_")
        s_s, s_rc, s_w, s_sp, s_dv, s_y, s_x, s_xb = (ph.sem(n) for n in ("sums", "recip", "widened", "spread_", "divided", "y", "x", "xb"))

        def head_q(b, u):
            g, j = u // 4, u % 4
            wait(nc.gpsimd, s_fg, b * SL + u - 3)
            wait(nc.gpsimd, s_S, b * TL + 4 * u - 12)
            nc.gpsimd.tensor_tensor(first_g[:, j:j + 1], mask[:, 0:1], mask[:, 0:1], ALU.mult).then_inc(s_fg, 1)
            nc.gpsimd.tensor_tensor(QZ[:, j, :], qsT[:, g, bass.ds(b * T, T)].bitcast(F32),
                                    mask[:, j:j + 1].broadcast_to([P, T]), ALU.mult).then_inc(s_qz, 1)

        def head_v(b, u):
            g, j = u // 4, u % 4
            if j == 0:
                wait(nc.gpsimd, s_pv, b * SL + u - 4)
                src = vN[:, bass.ds(b * NB, NB), g * HG * HD1:(g + 1) * HG * HD1].rearrange("p n (h d) -> p n h d", h=HG)
                nc.gpsimd.tensor_copy(VZ[:, g % 2, :, :, 0:HD1], src).then_inc(s_vz, 1)

        def scores(b, u, pair):
            g, j = u // 4, u % 4
            if pair == 0:
                wait(nc.tensor, s_qz, b * SL + u + 1)
            for r in (2 * pair, 2 * pair + 1):
                m = 4 * u + r
                wait(nc.tensor, s_b, b * TL + m - (2 if m else 0))
                nc.tensor.matmul(SC[m % 3][:, :], QZ[:, j, r * P:(r + 1) * P], ksT[:, g, bass.ds(b * T, T)],
                                 start=True, stop=True).then_inc(s_S, 1)

        def scores_1(b, u):
            scores(b, u, 0)

        def scores_2(b, u):
            scores(b, u, 1)

        def turn(b, u, half):
            g, j = u // 4, u % 4
            wait(nc.tensor, (s_td, s_ta)[half], b * SL + u)
            for h in range(2):
                for r in range(NB):
                    last = nc.tensor.transpose(TB[half][:, h, r * P:(r + 1) * P],
                                               PR[:, g % 2, 2 * half + h, r, j * P:(j + 1) * P], ident[:, :])
            last.then_inc(s_T, 1)

        def turn_1(b, u):
            if u % 4 == 0:
                wait(nc.tensor, s_e, b * SL + u + 4)
            turn(b, u, 0)

        def turn_2(b, u):
            turn(b, u, 1)

        def pv(b, u):
            g, j = u // 4, u % 4
            wait(nc.tensor, s_ta, b * SL + u + 1)
            wait(nc.tensor, s_td, b * SL + u + 1)
            if j == 0:
                wait(nc.tensor, s_vz, b * G1 + g + 1)
                wait(nc.tensor, s_o, b * G1 + g)
            for h in range(HG):
                last = nc.tensor.matmul(OB[h * RS:(h + 1) * RS, :], VZ[:, g % 2, j, h, :], PT[:, u % 2, h, :],
                                        start=(j == 0), stop=(j == NB - 1))
            last.then_inc(s_pv, 1)

        def start_v(b, u):
            wait(nc.vector, s_fv, b * SL + u - 3)
            wait(nc.vector, s_e, b * SL + u - 3)
            if u % 4 == 0:
                wait(nc.vector, s_T, b * 2 * SL + 2 * u - 8)
            wait(nc.vector, s_S, b * TL + 4 * u + 2)
            nc.vector.tensor_copy(first_v[:, u % 4:u % 4 + 1], mask[:, 0:1]).then_inc(s_fv, 1)

        def add_bias(b, u, pair):
            g, j = u // 4, u % 4
            for r in (2 * pair, 2 * pair + 1):
                m = 4 * u + r
                nc.vector.tensor_tensor_reduce(PR[:, g % 2, j, r, :], SC[m % 3][:, :], bias[:, r, :], 1.0, 3.0e38,
                                               ALU.add, ALU.min, least[:, j, r:r + 1]).then_inc(s_b, 1)

        def add_bias_1(b, u):
            add_bias(b, u, 0)

        def await_scores_2(b, u):
            wait(nc.vector, s_S, b * TL + 4 * u + 4)

        def copy_turned_v(b, u):
            wait(nc.vector, s_T, b * 2 * SL + 2 * u + 1)
            wait(nc.vector, s_pv, b * SL + u - 1)
            nc.vector.tensor_copy(PT[:, u % 2, 0:2, :], TB[0][:, :, :]).then_inc(s_td, 1)

        def add_bias_2(b, u):
            add_bias(b, u, 1)

        def exps(b, u, tiles):
            g, j = u // 4, u % 4
            for r in tiles:
                wait(nc.scalar, s_b, b * TL + 4 * u + r + 1)
                pr = PR[:, g % 2, j, r, :]
                last = nc.scalar.activation(pr, pr, ACT.Exp, bias=least[:, j, r:r + 1], scale=-1.0)
            return last

        def exps_1(b, u):
            exps(b, u, (0, 1))

        def copy_turned_a(b, u):
            wait(nc.scalar, s_T, b * 2 * SL + 2 * u + 2)
            wait(nc.scalar, s_pv, b * SL + u - 1)
            nc.scalar.activation(PT[:, u % 2, 2:4, :], TB[1][:, :, :], ACT.Copy).then_inc(s_ta, 1)

        def exps_2(b, u):
            exps(b, u, (2, 3)).then_inc(s_e, 1)

        def o_out(b, u):
            g, j = u // 4, u % 4
            if j == 3:
                wait(nc.scalar, s_pv, b * SL + u + 1)
                nc.scalar.activation(qsT[:, g, bass.ds(b * T, T)].bitcast(F32), OB[:, :], ACT.Copy).then_inc(s_o, 1)

        with nc.Block() as block:
            @block.sync
            def _(sp):
                sp.dma_start(bias[:, :, :], bias_in).then_inc(s_c, 16)
                sp.wait_ge(s_z, 2)
                for h in range(HG):
                    sp.dma_start(wog[h * RS:h * RS + HD1, :, :],
                                 Wo.rearrange("(g h d) n -> h d g n", g=G1, h=HG)[h]).then_inc(s_wo, 16)
                sp.dma_start(wo[:, :], Wo).then_inc(s_wo, 16)
                sp.dma_start(bo[:, :], bo_in[None, :].broadcast_to([P, D])).then_inc(s_wo, 16)

            def spread(pe, n):
                wait(pe, s_dv, n - 1)
                pe.wait_ge(s_w, n + 1)
                for r in range(NB):
                    last = nc.tensor.matmul(TB[n % 2][:, 1, r * P:(r + 1) * P],
                                            wide[:, n % 2, r, :, :].rearrange("p h j -> p (h j)"),
                                            ident[:, :], start=True, stop=True)
                last.then_inc(s_sp, 1)

            @block.tensor
            def _(pe):
                pe.wait_ge(s_z, 3)
                pipeline(pe, [(scores_1, L_S), (turn_1, L_T), (scores_2, L_S), (turn_2, L_T), (pv, L_PV)], SL, B)
                pe.wait_ge(s_wo, 16 * (HG + 2))
                pe.wait_ge(s_o, B * G1)
                for t in range(NT):
                    b, at = t // NB, slice(t * P, (t + 1) * P)
                    if t % NB == 0:
                        for g in range(G1):
                            n = b * G1 + g
                            wait(pe, s_rc, n - 1)
                            for r in range(NB):
                                o = qsT[:, g, (b * NB + r) * P:(b * NB + r + 1) * P].bitcast(F32)
                                last = nc.tensor.transpose(TB[g % 2][:, 0, r * P:(r + 1) * P], o, ident[:, :])
                            last.then_inc(s_s, 1)
                            if g:
                                spread(pe, n - 1)
                        spread(pe, n)
                        pe.wait_ge(s_dv, (b + 1) * G1)
                    wait(pe, s_y, t - 1)
                    for g in range(G1):
                        nc.tensor.matmul(SC[t % 2][:, 0:D], qsT[:, g, at].bitcast(F32), wog[:, g, :], start=(g == 0), stop=False)
                    nc.tensor.matmul(SC[t % 2][:, 0:D], infT[:, at], wo[:, :], start=False, stop=True).then_inc(s_x, 1)

            @block.vector
            def _(v):
                nc.vector.memset(VZ[:, :, :, :, :], 0.0).then_inc(s_z, 1)
                nc.vector.memset(wog[:, :, :], 0.0).then_inc(s_z, 1)
                v.wait_ge(s_z, 2)
                nc.vector.memset(VZ[:, :, :, :, HD1:HD1 + 1], 1.0).then_inc(s_z, 1)
                v.wait_ge(s_c, 16)
                pipeline(v, [(start_v, L_S), (add_bias_1, L_S), (await_scores_2, L_S), (copy_turned_v, L_T),
                             (add_bias_2, L_S)], SL, B)
                v.wait_ge(s_wo, 16 * (HG + 2))
                nc.vector.tensor_tensor(x_nat[:, :, :], x_nat[:, :, :], bo[:, None, :].broadcast_to([P, NT, D]),
                                        ALU.add).then_inc(s_xb, 1)
                v.wait_ge(s_xb, 1)
                for b in range(B):
                    for g in range(G1 + 1):
                        n = b * G1 + g
                        if g < G1:
                            v.wait_ge(s_s, n + 1)
                            wait(v, s_sp, n - 1)
                            nc.vector.reciprocal(rec[:, n % 2, :, :],
                                                 TB[g % 2][:, 0, :].rearrange("p (r h j) -> p r h j", r=NB, h=HG)[:, :, :, HD1]
                                                 ).then_inc(s_rc, 1)
                        if g:
                            v.wait_ge(s_sp, n)
                            o = qsT[:, g - 1, b * T:(b + 1) * T].bitcast(F32)
                            nc.vector.tensor_tensor(o, o, TB[(n - 1) % 2][:, 1, :], ALU.mult).then_inc(s_dv, 1)
                    for t in range(b * NB, (b + 1) * NB):
                        v.wait_ge(s_x, t + 1)
                        nc.vector.tensor_tensor(x_nat[:, t, :], SC[t % 2][:, 0:D], x_nat[:, t, :], ALU.add).then_inc(s_y, 1)

            @block.scalar
            def _(a):
                pipeline(a, [(exps_1, L_S), (copy_turned_a, L_T), (exps_2, L_S), (o_out, L_PV)], SL, B)
                for n in range(B * G1):
                    a.wait_ge(s_rc, n + 1)
                    wait(a, s_sp, n - 1)
                    nc.scalar.activation(wide[:, n % 2, :, :, :], rec[:, n % 2, :, :, None].broadcast_to([P, NB, HG, RS]),
                                         ACT.Copy).then_inc(s_w, 1)

            @block.gpsimd
            def _(g):
                g.wait_ge(s_z, 3)
                pipeline(g, [(head_q, 0), (head_v, 4)], SL, B)


def gates1(nc, xT, combine, gate_w, numbers_in):
    W = [P, NT, E1]
    with Phase(nc, "g1") as ph:
        gw, num = ph.sb("gw", [P, E1]), ph.sb("num", [P, E1])
        lg, ex, pr, top = (ph.sb(n, W) for n in ("lg", "ex", "pr", "top"))
        c1, c2 = ph.sb("c1", W), ph.sb("c2", W)
        at, atf = ph.sb("at", W, U32), ph.sb("atf", W)
        mx, sm, rs, s2, r2 = (ph.sb(n, [P, NT]) for n in ("mx", "sm", "rs", "s2", "r2"))
        wt = ph.sb("wt", [P, 2, NT])
        LG = ph.ps("logits", [P, NT, E1])
        s_w, s_l, s_c, s_e, s_m = (ph.sem(n) for n in ("w", "l", "chain", "exped", "tops"))

        with nc.Block() as block:
            @block.sync
            def _(sp):
                sp.dma_start(gw[:, :], gate_w).then_inc(s_w, 16)
                sp.dma_start(num[:, :], numbers_in).then_inc(s_w, 16)

            @block.tensor
            def _(pe):
                pe.wait_ge(s_w, 32)
                for t in range(NT):
                    last = nc.tensor.matmul(LG[:, t, :], xT[:, t * P:(t + 1) * P], gw[:, :], start=True, stop=True)
                last.then_inc(s_l, 1)

            @block.scalar
            def _(a):
                a.wait_ge(s_c, 2)
                nc.scalar.activation(ex[:, :, :], lg[:, :, :], ACT.Exp).then_inc(s_e, 1)

            @block.vector
            def _(v):
                count = [0]

                def link(ins):
                    count[0] += 1
                    ins.then_inc(s_c, 1)
                    v.wait_ge(s_c, count[0])

                v.wait_ge(s_l, 1)
                v.wait_ge(s_w, 32)
                link(nc.vector.tensor_reduce(mx[:, :], LG[:, :, :], AX.X, ALU.max))
                link(nc.vector.tensor_tensor(lg[:, :, :], LG[:, :, :], mx[:, :, None].broadcast_to(W), ALU.subtract))
                v.wait_ge(s_e, 1)
                link(nc.vector.tensor_reduce(sm[:, :], ex[:, :, :], AX.X, ALU.add))
                link(nc.vector.reciprocal(rs[:, :], sm[:, :]))
                link(nc.vector.tensor_tensor(pr[:, :, :], ex[:, :, :], rs[:, :, None].broadcast_to(W), ALU.mult))
                for t in range(NT):
                    nc.vector.max(top[:, t, :], pr[:, t, :]).then_inc(s_m, 1)
                for t in range(NT):
                    v.wait_ge(s_m, t + 1)
                    last = nc.vector.max_index(at[:, t, :], top[:, t, :], pr[:, t, :])
                link(last)
                link(nc.vector.tensor_copy(atf[:, :, :], at[:, :, :]))
                link(nc.vector.tensor_tensor(s2[:, :], top[:, :, 0], top[:, :, 1], ALU.add))
                link(nc.vector.reciprocal(r2[:, :], s2[:, :]))
                link(nc.vector.tensor_tensor(wt[:, 0, :], top[:, :, 0], r2[:, :], ALU.mult))
                link(nc.vector.tensor_tensor(wt[:, 1, :], top[:, :, 1], r2[:, :], ALU.mult))
                for k, c in enumerate((c1, c2)):
                    link(nc.vector.tensor_tensor(c[:, :, :], num[:, None, :].broadcast_to(W),
                                                 atf[:, :, k:k + 1].broadcast_to(W), ALU.is_equal))
                    link(nc.vector.tensor_tensor(c[:, :, :], c[:, :, :], wt[:, k, :, None].broadcast_to(W), ALU.mult))
                link(nc.vector.tensor_tensor(combine[:, :, :], c1[:, :, :], c2[:, :, :], ALU.add))


def experts1(nc, x_nat, xT, combine, w_gate, w_up, w_down):
    PER = 2 * B
    with Phase(nc, "e1") as ph:
        wg, wu = ph.sb("wg", [P, 2, F1]), ph.sb("wu", [P, 2, F1])
        wd = ph.sb("wd", [P, 2, FT, D])
        h, hu = ph.sb("h", [P, 2, T]), ph.sb("hu", [P, 2, FT, T])
        G = [ph.ps(f"gate{k}", [P, T]) for k in range(2)]
        U = [ph.ps(f"up{k}", [P, T]) for k in range(2)]
        Y = [ph.ps(f"out{k}", [P, NB, D]) for k in range(2)]
        s_w = [ph.sem(f"weights{q}") for q in range(2)]
        s_g, s_h, s_m, s_d, s_y = (ph.sem(n) for n in ("gated", "silu", "times", "down", "added"))
        full = F1 // P
        size = [P] * full + [F1 - full * P]

        def load(sp, i, q):
            e = bass.ds(i * 2 + q, 1)
            sp.dma_start(wg[:, q, :], w_gate[e].rearrange("o d f -> d (o f)")).then_inc(s_w[q], 16)
            sp.dma_start(wu[:, q, :], w_up[e].rearrange("o d f -> d (o f)")).then_inc(s_w[q], 16)
            sp.dma_start(wd[:, q, 0:full, :],
                         w_down[e, 0:full * P].rearrange("o (k p) n -> p (o k) n", p=P)).then_inc(s_w[q], 16)
            sp.dma_start(wd[0:size[full], q, full, :], w_down[e, full * P:F1].rearrange("o p n -> p (o n)")).then_inc(s_w[q], 16)

        def gate_up(i, u):
            q, b = u // B, u % B
            if b == 0:
                wait(nc.tensor, s_w[q], (i + 1) * 64)
            for k in range(FT):
                m = u * FT + k
                wait(nc.tensor, s_m, i * PER * FT + m - 1)
                for bank, ww in ((G, wg), (U, wu)):
                    last = nc.tensor.matmul(bank[m % 2][0:size[k], :], ww[:, q, k * P:k * P + size[k]],
                                            xT[:, b * T:(b + 1) * T], start=True, stop=True)
                last.then_inc(s_g, 1)

        def down(i, u):
            q = u // B
            wait(nc.tensor, s_m, (i * PER + u + 1) * FT)
            wait(nc.tensor, s_y, i * PER + u - 1)
            for n in range(NB):
                for k in range(FT):
                    last = nc.tensor.matmul(Y[u % 2][:, n, :], hu[0:size[k], u % 2, k, n * P:(n + 1) * P],
                                            wd[0:size[k], q, k, :], start=(k == 0), stop=(k == FT - 1))
            last.then_inc(s_d, 1)

        def silu(i, u):
            for k in range(FT):
                m = u * FT + k
                wait(nc.scalar, s_g, i * PER * FT + m + 1)
                wait(nc.scalar, s_m, i * PER * FT + m - 1)
                nc.scalar.activation(h[0:size[k], m % 2, :], G[m % 2][0:size[k], :], ACT.Silu).then_inc(s_h, 1)

        def times(i, u):
            wait(nc.vector, s_d, i * PER + u - 1)
            for k in range(FT):
                m = u * FT + k
                wait(nc.vector, s_h, i * PER * FT + m + 1)
                nc.vector.tensor_tensor(hu[0:size[k], u % 2, k, :], U[m % 2][0:size[k], :], h[0:size[k], m % 2, :],
                                        ALU.mult).then_inc(s_m, 1)

        def add(i, u):
            q, b = u // B, u % B
            wait(nc.vector, s_d, i * PER + u + 1)
            wait(nc.vector, s_y, i * PER + u - B + 1)
            for n in range(NB):
                t = b * NB + n
                last = nc.vector.scalar_tensor_tensor(out=x_nat[:, t, :], in0=Y[u % 2][:, n, :],
                                                      scalar=combine[:, t, bass.ds(i * 2 + q, 1)], in1=x_nat[:, t, :],
                                                      op0=ALU.mult, op1=ALU.add)
            last.then_inc(s_y, 1)

        with nc.Block() as block:
            @block.sync
            def _(sp):
                for q in range(2):
                    load(sp, 0, q)
                with sp.Fori(1, E1 // 2) as i:
                    for q in range(2):
                        sp.wait_ge(s_d, i * PER + (q - 1) * B)
                        load(sp, i, q)

            @block.tensor
            def _(pe):
                pipeline(pe, [(gate_up, 0), (down, 1)], PER, E1 // 2)

            @block.scalar
            def _(a):
                pipeline(a, [(silu, 0)], PER, E1 // 2)

            @block.vector
            def _(v):
                pipeline(v, [(times, 0), (add, 1)], PER, E1 // 2)


def build(nc, a, out, stop=99):
    with ExitStack() as top:
        def sb(name, shape, dt=F32):
            return top.enter_context(nc.sbuf_tensor(name, shape, dt))

        x_nat, xT = sb("x_nat", [P, NT, D]), sb("xT", [P, B * T])
        ident, ones = sb("ident", [P, P]), sb("ones", [P, P])
        epsc, mask = sb("epsc", [P, 1]), sb("mask", [P, HG])
        bqkv = sb("bqkv", [P, 3 * H0])
        b1 = sb("b1", [P, 2])
        bgT, buT = sb("bgT", [P, E0 * F0 // P]), sb("buT", [P, E0 * F0 // P])
        combine = sb("combine", [P, NT, E1])

        sems = {n: Counted(top.enter_context(nc.semaphore(n))) for n in (
            "turned", "turn_copied", "stats", "mean_var", "std", "rstd", "normed", "gained", "shifted", "out")}

        s_in = top.enter_context(nc.semaphore("inputs"))
        s_one = top.enter_context(nc.semaphore("ones_set"))
        with nc.Block() as block:
            @block.sync
            def _(sp):
                sp.dma_start(x_nat[:, :, :], a["L0_attn_x"].rearrange("b (n p) d -> p (b n) d", p=P)).then_inc(s_in, 16)
                sp.dma_start(ident[:, :], a["ident"]).then_inc(s_in, 16)
                sp.dma_start(mask[:, :], a["mask"]).then_inc(s_in, 16)
                sp.wait_ge(s_in, 48)

            @block.vector
            def _(v):
                nc.vector.memset(ones[:, :], 1.0 / T).then_inc(s_one, 1)
                nc.vector.memset(epsc[:, :], EPS).then_inc(s_one, 1)

        load_columns(nc, "lc", ident, [
            ([(c * H0, half * HD0, a["L0_attn_b_qkv"].rearrange("(h c d) -> c h d", c=3, d=HD0)[c])
              for c in range(3) for half in range(2)], 3 * H0, P, bqkv),
            ([(0, 0, a["L0_ffn_bg"].rearrange("e (k p) -> (e k) p", p=P))], E0 * F0 // P, P, bgT),
            ([(0, 0, a["L0_ffn_bu"].rearrange("e (k p) -> (e k) p", p=P))], E0 * F0 // P, P, buT),
            ([(0, 0, a["L1_attn_bq"][None, :])], 1, P, b1[:, 0:1]),
            ([(0, 0, a["L1_attn_bkv_down"][None, :])], 1, LAT, b1[:, 1:2]),
        ])
        s_b8 = top.enter_context(nc.semaphore("bias_scaled"))
        with nc.Block() as block:
            @block.vector
            def _(v):
                nc.vector.tensor_scalar(bqkv[:, 0:H0], bqkv[:, 0:H0], HD0 ** -0.5, None, ALU.mult).then_inc(s_b8, 1)

        transpose_tokens(nc, "t0", sems, x_nat, xT, ident)
        if stop >= 1:
            attention0(nc, x_nat, xT, ident, a["L0_attn_w_qkv"], bqkv, a["L0_attn_w_out"], a["L0_attn_b_out"], a["posT"], a["own"])
            norm_rows(nc, "n0", sems, x_nat, x_nat, NT, epsc)
        if stop >= 2:
            with ExitStack() as mid:
                def sb2(name, shape, dt=F32):
                    return mid.enter_context(nc.sbuf_tensor(name, shape, dt))

                xn, xnT = sb2("xn", [P, NT, D]), sb2("xnT", [P, B * T])
                se, seT = sb2("se", [P, ST, D]), sb2("seT", [P, ST * P])
                rows = sb2("rows", [P, 4, D])
                sc = sb2("sc", [P, 1])
                slotsT, eout = sb2("slotsT", [P, B, ST * P]), sb2("eout", [P, ST, B, D])
                s_f = mid.enter_context(nc.semaphore("f0_in"))
                with nc.Block() as block:
                    @block.sync
                    def _(sp):
                        for k, n in enumerate(("norm_g", "norm_b", "slot_g", "slot_b")):
                            sp.dma_start(rows[:, k, :], a["L0_ffn_" + n][None, :].broadcast_to([P, D])).then_inc(s_f, 16)
                        sp.dma_start(sc[:, :], a["L0_ffn_scale"][None, :].broadcast_to([P, 1])).then_inc(s_f, 16)
                        sp.dma_start(se[:, :, :], a["L0_ffn_slot_embeds"].rearrange("(t q) s d -> (q s) t d", q=2)).then_inc(s_f, 16)
                        sp.wait_ge(s_f, 96)
                norm_rows(nc, "n1", sems, x_nat, xn, NT, epsc, rows[:, 0, :], rows[:, 1, :])
                norm_rows(nc, "n2", sems, se, se, ST, epsc, rows[:, 2, :], rows[:, 3, :], sc)
                transpose_tokens(nc, "t1", sems, xn, xnT, ident)
                transpose_tokens(nc, "t2", sems, se, seT, ident, ST)
                dispatch0(nc, xn, xnT, seT, slotsT, ident)
                experts0(nc, ident, slotsT, eout, bgT, buT, a["L0_ffn_Wg"], a["L0_ffn_Wu"], a["L0_ffn_Wd"], a["L0_ffn_bd"])
                combine0(nc, x_nat, xnT, seT, eout, ident)
            norm_rows(nc, "n3", sems, x_nat, x_nat, NT, epsc)
        if stop >= 3:
            transpose_tokens(nc, "t3", sems, x_nat, xT, ident)
            with ExitStack() as mid:
                def sb3(name, shape, dt=F32):
                    return mid.enter_context(nc.sbuf_tensor(name, shape, dt))

                qsT, ksT = sb3("qsT", [P, G1, B * T], F32R), sb3("ksT", [P, G1, B * T], F32R)
                vN, infT = sb3("vN", [P, NT, D]), sb3("infT", [P, B * T])
                prepare1(nc, xT, ident, qsT, ksT, vN, infT, b1, ones, a["L1_attn_Wq"], a["L1_attn_Wkv_down"],
                         a["L1_attn_Wkv_up"], a["L1_attn_bkv_up"], a["cos"], a["sin"])
                attention1(nc, x_nat, qsT, ksT, vN, infT, mask, ident, a["att_bias"], a["L1_attn_Wo"], a["L1_attn_bo"])
            norm_rows(nc, "n4", sems, x_nat, x_nat, NT, epsc)
        if stop >= 4:
            transpose_tokens(nc, "t4", sems, x_nat, xT, ident)
            gates1(nc, xT, combine, a["L1_ffn_gate_w"], a["numbers"])
            experts1(nc, x_nat, xT, combine, a["L1_ffn_w_gate"], a["L1_ffn_w_up"], a["L1_ffn_w_down"])
        norm_rows(nc, "n5", sems, x_nat, x_nat, NT, epsc, out=out)


_OUTS = [((B, T, D), "float32")]


def _constants():
    f = np.float32
    pos = np.arange(T, dtype=f)[:, None]
    div = np.exp(np.arange(0, HD0, 2, dtype=f) * f(-(np.log(10000.0) / HD0))).astype(f)
    ang = (pos * div).astype(f)
    pe = np.zeros((T, HD0), f)
    pe[:, 0::2], pe[:, 1::2] = np.sin(ang), np.cos(ang)
    own = np.repeat(np.tile(np.eye(GT, dtype=f), (1, GC)), H0, axis=1)
    inv = (f(1.0) / np.power(f(10000.0), np.arange(0, HD1, 2, dtype=f) / f(HD1))).astype(f)
    fr = np.outer(np.arange(T, dtype=f), inv).astype(f)
    by_block = lambda t: np.ascontiguousarray(t.reshape(NB, P, -1).transpose(1, 0, 2))
    idx = np.arange(T, dtype=f)
    dist = idx[:, None] - idx[None, :]
    decay = np.exp(-np.maximum(dist, f(0.0)) * f(0.01)).astype(f)
    bias = (f(-0.1) * np.log(np.abs(dist) + f(1.0)) + np.log(decay + f(1e-9))).astype(f)
    return {
        "ident": np.eye(P, dtype=f),
        "mask": np.kron(np.eye(HG, dtype=f), np.ones((RS, 1), f)),
        "own": np.stack([own, f(NOT_OWN) * (f(1.0) - own)]),
        "posT": np.ascontiguousarray(np.concatenate([pe.T, pe.T])),
        "cos": by_block(np.cos(fr).astype(f)), "sin": by_block(np.sin(fr).astype(f)),
        "att_bias": by_block(-bias),
        "numbers": np.tile(np.arange(E1, dtype=f), (P, 1)),
    }


def kernel(**inputs):
    import concourse.bacc as _bacc
    from concourse.bass_utils import run_bass_kernel_spmd as _run

    nc = _bacc.Bacc("TRN2", target_bir_lowering=False, num_devices=1)
    arrays, args = {}, {}
    for name, value in (*inputs.items(), *_constants().items()):
        value = np.ascontiguousarray(value)
        arrays[f"in_{name}_dram"] = value
        args[name] = nc.dram_tensor(f"in_{name}_dram", value.shape, mybir.dt.from_np(value.dtype), kind="ExternalInput").ap()
    outs = [nc.dram_tensor(f"out_{i}_dram", shape, mybir.dt.from_np(np.dtype(dtype)), kind="ExternalOutput").ap()
            for i, (shape, dtype) in enumerate(_OUTS)]
    build(nc, args, outs[0])
    r = _run(nc, [arrays], core_ids=[0])
    return r.results[0]["out_0_dram"]
```

```python
import numpy as np
from contextlib import ExitStack

import concourse.bass as bass
from concourse import mybir

F32 = mybir.dt.float32
F32R = mybir.dt.float32r
I32 = mybir.dt.int32
U32 = mybir.dt.uint32
ALU = mybir.AluOpType
ACT = mybir.ActivationFunctionType
AX = mybir.AxisListType

P = 128
B, T, D = 4, 512, 128
NB = T // P
NT = B * NB
H0, HD0 = 16, 64
E0, S0, F0 = 16, 64, 256
ST = E0 * S0 // P
H1, HD1, LAT = 16, 8, 32
G1 = 4
HG = H1 // G1
E1, F1 = 8, 352
FT = (F1 + P - 1) // P
EPS = 1e-5
SMALL1 = 9


def wait(eng, sem, value):
    if not isinstance(value, int) or value > 0:
        eng.wait_ge(sem, value)


class Counted:

    def __init__(self, sem):
        self.sem, self.base = sem, 0

    def wait(self, eng, n):
        if n > 0:
            eng.wait_ge(self.sem, self.base + n)

    def done(self, n):
        self.base += n


class Phase:

    def __init__(self, nc, tag):
        self.nc, self.tag, self.stack = nc, tag, ExitStack()

    def sb(self, name, shape, dt=F32):
        return self.stack.enter_context(self.nc.sbuf_tensor(f"{self.tag}_{name}", shape, dt))

    def ps(self, name, shape, dt=F32):
        return self.stack.enter_context(self.nc.psum_tensor(f"{self.tag}_{name}", shape, dt))

    def sem(self, name):
        return self.stack.enter_context(self.nc.semaphore(f"{self.tag}_{name}"))

    def __enter__(self):
        return self

    def __exit__(self, *a):
        return self.stack.__exit__(*a)


def pipeline(eng, stages, per, iters):
    for u in range(per):
        for stage, lag in stages:
            if u >= lag:
                stage(0, u - lag)
    with eng.Fori(1, iters) as i:
        for u in range(per):
            for stage, lag in stages:
                stage(i if u >= lag else i - 1, (u - lag) % per)
    for u in range(max(lag for _, lag in stages)):
        for stage, lag in stages:
            if u < lag:
                stage(iters - 1, per + u - lag)


def transpose_tokens(nc, tag, sems, src, dst, ident, tiles=NT):
    s_t, s_c = sems["turned"], sems["turn_copied"]
    with Phase(nc, tag) as ph:
        pt = [ph.ps(f"pt{k}", [P, T]) for k in range(2)]
        with nc.Block() as block:
            @block.tensor
            def _(pe):
                for b in range(tiles // NB):
                    s_c.wait(pe, b - 1)
                    for n in range(NB):
                        last = nc.tensor.transpose(pt[b % 2][:, n * P:(n + 1) * P], src[:, b * NB + n, :], ident[:, :])
                    last.then_inc(s_t.sem, 1)

            @block.vector
            def _(v):
                for b in range(tiles // NB):
                    s_t.wait(v, b + 1)
                    nc.vector.tensor_copy(dst[:, b * T:(b + 1) * T], pt[b % 2][:, :]).then_inc(s_c.sem, 1)
    s_t.done(tiles // NB)
    s_c.done(tiles // NB)


class Norm:

    def __init__(self, nc, ph, sems, src, dst, tiles, epsc, gain=None, shift=None, scale=None):
        self.nc, self.sems, self.src, self.dst, self.tiles, self.epsc = nc, sems, src, dst, tiles, epsc
        self.gain, self.shift, self.scale = gain, shift, scale
        self.stats, self.mv = ph.sb(f"stats{tiles}", [P, tiles, 6]), ph.sb(f"mv{tiles}", [P, tiles, 2])
        self.std, self.rstd = ph.sb(f"std{tiles}", [P, tiles]), ph.sb(f"rstd{tiles}", [P, tiles])

    def vector(self, v):
        nc, sems, src, dst, tiles, stats, mv = self.nc, self.sems, self.src, self.dst, self.tiles, self.stats, self.mv
        for t in range(tiles):
            nc.vector.bn_stats(stats[:, t, :], src[:, t, :]).then_inc(sems["stats"].sem, 1)
        for t in range(tiles):
            sems["stats"].wait(v, t + 1)
            nc.vector.bn_aggr(mv[:, t, :], stats[:, t, :]).then_inc(sems["mean_var"].sem, 1)
        sems["std"].wait(v, 1)
        nc.vector.reciprocal(self.rstd[:, :], self.std[:, :]).then_inc(sems["rstd"].sem, 1)
        sems["rstd"].wait(v, 1)
        for t in range(tiles):
            nc.vector.tensor_scalar(dst[:, t, :], src[:, t, :], mv[:, t, 0:1], self.rstd[:, t:t + 1],
                                    ALU.subtract, ALU.mult).then_inc(sems["normed"].sem, 1)
        if self.gain is not None:
            sems["normed"].wait(v, tiles)
            wide = [P, tiles, D]
            nc.vector.tensor_tensor(dst[:, :, :], dst[:, :, :], self.gain.unsqueeze(1).broadcast_to(wide),
                                    ALU.mult).then_inc(sems["gained"].sem, 1)
            sems["gained"].wait(v, 1)
            nc.vector.tensor_tensor(dst[:, :, :], dst[:, :, :], self.shift.unsqueeze(1).broadcast_to(wide),
                                    ALU.add).then_inc(sems["shifted"].sem, 1)
            if self.scale is not None:
                sems["shifted"].wait(v, 1)
                nc.vector.tensor_scalar(dst[:, :, :], dst[:, :, :], self.scale[:, 0:1], None, ALU.mult).then_inc(sems["scaled"].sem, 1)

    def scalar(self, a):
        self.sems["mean_var"].wait(a, self.tiles)
        self.nc.scalar.activation(self.std[:, :], self.mv[:, :, 1], ACT.Sqrt,
                                  bias=self.epsc[:, 0:1]).then_inc(self.sems["std"].sem, 1)

    def done(self):
        for n, count in (("stats", self.tiles), ("mean_var", self.tiles), ("std", 1), ("rstd", 1), ("normed", self.tiles),
                         ("gained", self.gain is not None), ("shifted", self.gain is not None),
                         ("scaled", self.scale is not None)):
            self.sems[n].done(int(count))


def norm_rows(nc, tag, sems, src, dst, tiles, epsc, gain=None, shift=None, out=None):
    s_x, s_out = sems["normed"], sems["out"]
    with Phase(nc, tag) as ph:
        norm = Norm(nc, ph, sems, src, dst, tiles, epsc, gain, shift)
        with nc.Block() as block:
            @block.vector
            def _(v):
                norm.vector(v)

            @block.scalar
            def _(a):
                norm.scalar(a)

            if out is not None:
                @block.sync
                def _(sp):
                    for b in range(B):
                        s_x.wait(sp, NB * (b + 1))
                        sp.dma_start(out[b].rearrange("(n p) d -> p n d", p=P),
                                     dst[:, b * NB:(b + 1) * NB, :]).then_inc(s_out.sem, 16)
                    s_out.wait(sp, 16 * B)
    norm.done()


def preamble(nc, a, sems, x_nat, xT, ident, mask, ones, epsc, jobs, rows, sc, se, seT, w, posT, posb, wo, bo, QKV, small,
             s_w, s_wo, s_own, s_1):
    with Phase(nc, "pre") as ph:
        rows_in = [ph.sb(f"rows{k}", [P, P]) for k in range(len(jobs))]
        XT = [ph.ps(f"xt{k}", [P, T]) for k in range(NB)]
        CT = [ph.ps(f"ct{k}", [P, P]) for k in range(2)]
        s_id, s_x, s_rows, s_f, s_t, s_c, s_ct, s_cc, s_set, s_b8, s_z, s_pb, s_st, s_sc = (ph.sem(n) for n in (
            "ident_in", "x_in", "rows_in_", "slots_in", "turned", "copied", "columns_", "columns_out", "set", "scaled",
            "zeros", "posb_", "slots_turned", "slots_out"))
        norm = Norm(nc, ph, sems, se, se, ST, epsc, rows[:, 2, :], rows[:, 3, :], sc)

        def key_rows(e, half):
            part = slice(half * HD0, (half + 1) * HD0)
            for k in range(2):
                h = H0 + 8 * k + 4 * half
                e.tensor_tensor(posb[part, k, :, :], posT[part, None, :].broadcast_to([HD0, 4, T]),
                                jobs[0][3][part, h:h + 4].unsqueeze(2).broadcast_to([HD0, 4, T]), ALU.add).then_inc(s_pb, 1)

        with nc.Block() as block:
            @block.sync
            def _(sp):
                sp.dma_start(ident[:, :], a["ident"]).then_inc(s_id, 16)
                for b in range(B):
                    sp.dma_start(x_nat[:, b * NB:(b + 1) * NB, :],
                                 a["L0_attn_x"][b].rearrange("(n p) d -> p n d", p=P)).then_inc(s_x, 16)
                sp.dma_start(posT[:, :], a["posT"]).then_inc(s_wo, 16)
                w_c = a["L0_attn_w_qkv"].rearrange("p (h c d) -> p c h d", h=H0, c=3)
                for c in range(3):
                    for k in range(2):
                        for half in range(2):
                            h = 8 * k + 4 * half
                            sp.dma_start(w[:, c, 4 * k:4 * k + 4, half, :], w_c[:, c, h:h + 4, :]).then_inc(s_w, 16)
                sp.dma_start(bo[:, :], a["L0_attn_b_out"][None, :].broadcast_to([P, D])).then_inc(s_wo, 16)
                sp.dma_start(wo[:, :, :], a["L0_attn_w_out"].rearrange("(k p) n -> p k n", p=P)).then_inc(s_wo, 16)
                sp.wait_ge(s_z, 2)
                for t in range(2):
                    for par in range(2):
                        sp.dma_start(QKV[t][HD0:HD0 + GT, par, :, :].rearrange("p t h -> p (t h)"), a["own"][t]).then_inc(s_own, 16)

            @block.scalar
            def _(act):
                for k, (parts, r, n, dst) in enumerate(jobs):
                    for r0, c0, src in parts:
                        act.dma_start(rows_in[k][r0:r0 + src.shape[0], c0:c0 + src.shape[1]], src).then_inc(s_rows, 16)
                act.dma_start(se[:, :, :], a["L0_ffn_slot_embeds"].rearrange("(t q) s d -> (q s) t d", q=2)).then_inc(s_f, 16)
                act.dma_start(sc[:, :], a["L0_ffn_scale"][None, :].broadcast_to([P, 1])).then_inc(s_f, 16)
                for k, n in enumerate(("norm_g", "norm_b", "slot_g", "slot_b")):
                    act.dma_start(rows[:, k, :], a["L0_ffn_" + n][None, :].broadcast_to([P, D])).then_inc(s_f, 16)
                norm.scalar(act)
                act.dma_start(mask[:, :], a["mask"]).then_inc(s_1, 16)
                for dst, src in small:
                    act.dma_start(dst, src).then_inc(s_1, 16)

            @block.gpsimd
            def _(g):
                for t in QKV:
                    nc.gpsimd.memset(t[HD0:P, :, :, :], 0.0).then_inc(s_z, 1)
                g.wait_ge(s_wo, 48)
                g.wait_ge(s_cc, 1)
                key_rows(nc.gpsimd, 1)

            @block.tensor
            def _(pe):
                pe.wait_ge(s_id, 16)
                pe.wait_ge(s_x, 16 * B)
                for b in range(B):
                    for n in range(NB):
                        last = nc.tensor.transpose(XT[b][:, n * P:(n + 1) * P], x_nat[:, b * NB + n, :], ident[:, :])
                    last.then_inc(s_t, 1)
                pe.wait_ge(s_rows, 16 * sum(len(j[0]) for j in jobs))
                for k, (parts, r, n, dst) in enumerate(jobs):
                    wait(pe, s_cc, k - 1)
                    nc.tensor.transpose(CT[k % 2][0:n, 0:r], rows_in[k][0:r, 0:n], ident[0:r, 0:r]).then_inc(s_ct, 1)
                sems["scaled"].wait(pe, 1)
                for b in range(ST // NB):
                    for n in range(NB):
                        last = nc.tensor.transpose(XT[b][:, n * P:(n + 1) * P], se[:, b * NB + n, :], ident[:, :])
                    last.then_inc(s_st, 1)

            @block.vector
            def _(v):
                nc.vector.memset(ones[:, :], 1.0 / T).then_inc(s_set, 1)
                nc.vector.memset(epsc[:, :], EPS).then_inc(s_set, 1)
                for b in range(B):
                    v.wait_ge(s_t, b + 1)
                    nc.vector.tensor_copy(xT[:, b * T:(b + 1) * T], XT[b][:, :]).then_inc(s_c, 1)
                for k, (parts, r, n, dst) in enumerate(jobs):
                    v.wait_ge(s_ct, k + 1)
                    nc.vector.tensor_copy(dst[0:n, 0:r], CT[k % 2][0:n, 0:r]).then_inc(s_cc, 1)
                bias = jobs[0][3]
                v.wait_ge(s_cc, 1)
                nc.vector.tensor_scalar(bias[:, 0:H0], bias[:, 0:H0], HD0 ** -0.5, None, ALU.mult).then_inc(s_b8, 1)
                v.wait_ge(s_wo, 48)
                key_rows(nc.vector, 0)
                nc.vector.tensor_tensor(x_nat[:, :, :], x_nat[:, :, :], bo[:, None, :].broadcast_to([P, NT, D]), ALU.add)
                v.wait_ge(s_f, 96)
                norm.vector(v)
                for b in range(ST // NB):
                    v.wait_ge(s_st, b + 1)
                    nc.vector.tensor_copy(seT[:, b * T:(b + 1) * T], XT[b][:, :]).then_inc(s_sc, 1)
    norm.done()


GT = P // H0
GC = P // GT
NOT_OWN = -2.0 ** 100


def attention0(nc, x_nat, xT, ident, w, bias, wo, posb, QKV, s_w, s_wo, s_own):
    SL = 4 * NB
    L_S, L_R, L_T, L_PV, L_O, L_Y = 4, 5, 6, 7, 8, 9
    with Phase(nc, "a0") as ph:
        V = ph.sb("vrows", [P, 8, 4, HD0])
        PR = ph.sb("probs", [P, 4, 4, P])
        PT = ph.sb("probsT", [P, 2, 4, P])
        OT = ph.sb("oT", [P, 2, P, H0 // 2])
        nmax, sums, rsum = (ph.sb(n, [P, 4, 4]) for n in ("nmax", "sums", "rsum"))
        PJ = [ph.ps(f"proj{k}", [P, 4, P]) for k in range(2)]
        SC = [ph.ps(f"scores{k}", [P, 4, P]) for k in range(2)]
        TB, VB, OB, Y = (ph.ps(n, [P, 4, P]) for n in ("turned", "vturned", "outT", "y"))
        s_pj, s_pe, s_S, s_mx, s_e, s_r, s_n = (ph.sem(n) for n in ("projected", "proj_in", "scored", "maxed", "exped", "recip", "normed"))
        s_vt, s_vc, s_T, s_tc, s_pv, s_oa, s_od, s_y, s_x = (
            ph.sem(n) for n in ("vturned_", "v_in", "turned_", "copied", "pv", "o_a", "o_d", "y_", "x"))

        def project(i, u):
            q, s = u // 4, u % 4
            if s == 3:
                return
            for k in range(2):
                m = 6 * q + 2 * s + k
                wait(nc.tensor, s_pe, 2 * (i * 24 + m - 1))
                for j in range(4):
                    last = nc.tensor.matmul(PJ[k][:, j, :], w[:, s, 4 * k + j, :, :].rearrange("p h d -> p (h d)"),
                                            xT[:, bass.ds(i * T + q * P, P)], start=True, stop=True)
                last.then_inc(s_pj, 1)

        def group(t, u, n):
            q, s = u // 4, u % 4
            at = (4 * s + n) * GT
            return t[:, q % 2, at:at + GT, :].rearrange("p t h -> p (t h)")

        def turn_v(i, u):
            q, s = u // 4, u % 4
            if s == 0:
                wait(nc.tensor, s_pe, 2 * (i * 24 + 6 * q + 6))
            wait(nc.tensor, s_vc, i * SL + u)
            for n in range(4):
                last = nc.tensor.transpose(VB[:, n, :], group(QKV[2], u, n), ident[:, :])
            last.then_inc(s_vt, 1)

        def scores(i, u):
            wait(nc.tensor, s_e, i * SL + u - 1)
            for n in range(4):
                last = nc.tensor.matmul(SC[u % 2][:, n, :], group(QKV[0], u, n), group(QKV[1], u, n), start=True, stop=True)
            last.then_inc(s_S, 1)

        def turn(i, u):
            wait(nc.tensor, s_n, i * SL + u + 1)
            wait(nc.tensor, s_tc, i * SL + u)
            for n in range(4):
                last = nc.tensor.transpose(TB[:, n, :], PR[:, u % 4, n, :], ident[:, :])
            last.then_inc(s_T, 1)

        def pv(i, u):
            wait(nc.tensor, s_tc, i * SL + u + 1)
            wait(nc.tensor, s_vc, i * SL + u + 1)
            wait(nc.tensor, s_oa, i * SL + u)
            wait(nc.tensor, s_od, i * SL + u)
            for n in range(4):
                last = nc.tensor.matmul(OB[0:HD0, n, :], V[:, u % 8, n, :], PT[:, u % 2, n, :], start=True, stop=True)
            last.then_inc(s_pv, 1)

        def out_proj(i, u):
            q, s = u // 4, u % 4
            if s < 3:
                return
            wait(nc.tensor, s_oa, i * SL + u + 1)
            wait(nc.tensor, s_od, i * SL + u + 1)
            wait(nc.tensor, s_x, i * NB + q)
            for m in range(H0 // 2):
                last = nc.tensor.matmul(Y[:, 0, :], OT[:, q % 2, :, m], wo[:, m, :], start=(m == 0), stop=(m == H0 // 2 - 1))
            last.then_inc(s_y, 1)

        def proj_in(i, u):
            q, s = u // 4, u % 4
            if s == 3:
                return
            n = i * SL + 4 * q - 4
            wait(nc.vector, s_vt if s == 2 else s_S, n)
            for k in range(2):
                wait(nc.vector, s_pj, i * 24 + 6 * q + 2 * s + k + 1)
                for half in range(2):
                    rows = slice(half * HD0, (half + 1) * HD0)
                    h = 8 * k + 4 * half
                    out = QKV[s][0:HD0, q % 2, :, h:h + 4].rearrange("p t h -> p h t")
                    if s == 1:
                        last = nc.vector.tensor_tensor(out, PJ[k][rows, :, :], posb[rows, k, :, q * P:(q + 1) * P], ALU.add)
                    else:
                        last = nc.vector.scalar_tensor_tensor(
                            out=out, in0=PJ[k][rows, :, :], scalar=HD0 ** -0.5 if s == 0 else 1.0,
                            in1=bias[rows, s * H0 + h:s * H0 + h + 4].unsqueeze(2).broadcast_to([HD0, 4, P]),
                            op0=ALU.mult, op1=ALU.add)
                    last.then_inc(s_pe, 1)

        def neg_max(i, u):
            wait(nc.vector, s_S, i * SL + u + 1)
            wait(nc.vector, s_e, i * SL + u - 3)
            nc.vector.tensor_reduce(nmax[:, u % 4, :], SC[u % 2][:, :, :], AX.X, ALU.max, negate=True).then_inc(s_mx, 1)

        def recip(i, u):
            wait(nc.vector, s_e, i * SL + u + 1)
            wait(nc.vector, s_n, i * SL + u - 3)
            nc.vector.reciprocal(rsum[:, u % 4, :], sums[:, u % 4, :]).then_inc(s_r, 1)

        def o_rows(u, par):
            q, s = u // 4, u % 4
            dst = OT[par * HD0:(par + 1) * HD0, q % 2, 4 * s * GT:(4 * s + 4) * GT, :]
            src = OB[0:HD0, :, :].rearrange("p n (t m r) -> p (n t) m r", t=GT, r=2)[:, :, :, par]
            return dst, src

        def o_free(eng, i, u):
            q, s = u // 4, u % 4
            if s == 0:
                wait(eng, s_y, i * NB + q - 1)

        def o_out_v(i, u):
            wait(nc.vector, s_pv, i * SL + u + 1)
            wait(nc.vector, s_oa, i * SL + u + 1)
            dst, src = o_rows(u, 1)
            o_free(nc.vector, i, u)
            nc.vector.tensor_copy(dst, src).then_inc(s_od, 1)

        def add(i, u):
            q, s = u // 4, u % 4
            if s < 3:
                return
            wait(nc.vector, s_y, i * NB + q + 1)
            x = x_nat[:, bass.ds(i * NB + q, 1), :].rearrange("p o d -> p (o d)")
            nc.vector.tensor_tensor(x, Y[:, 0, :], x, ALU.add).then_inc(s_x, 1)

        def exps(i, u):
            wait(nc.scalar, s_mx, i * SL + u + 1)
            wait(nc.scalar, s_r, i * SL + u - 3)
            wait(nc.scalar, s_T, i * SL + u - 3)
            for n in range(4):
                last = nc.scalar.activation(PR[:, u % 4, n, :], SC[u % 2][:, n, :], ACT.Exp,
                                            bias=nmax[:, u % 4, n:n + 1], accum_out=sums[:, u % 4, n:n + 1])
            last.then_inc(s_e, 1)

        def v_in(i, u):
            wait(nc.scalar, s_vt, i * SL + u + 1)
            wait(nc.scalar, s_pv, i * SL + u - 7)
            nc.scalar.activation(V[:, u % 8, :, :], VB[:, :, 0:HD0], ACT.Copy).then_inc(s_vc, 1)

        def copy_turned(i, u):
            wait(nc.scalar, s_T, i * SL + u + 1)
            wait(nc.scalar, s_pv, i * SL + u - 1)
            nc.scalar.activation(PT[:, u % 2, :, :], TB[:, :, :], ACT.Copy).then_inc(s_tc, 1)

        def o_out_a(i, u):
            wait(nc.scalar, s_pv, i * SL + u + 1)
            dst, src = o_rows(u, 0)
            o_free(nc.scalar, i, u)
            nc.scalar.activation(dst, src, ACT.Copy).then_inc(s_oa, 1)

        def normalise(i, u):
            wait(nc.gpsimd, s_r, i * SL + u + 1)
            pr = PR[:, u % 4, :, :]
            nc.gpsimd.tensor_tensor(pr, pr, rsum[:, u % 4, :].unsqueeze(2).broadcast_to([P, 4, P]), ALU.mult).then_inc(s_n, 1)

        with nc.Block() as block:
            @block.tensor
            def _(pe):
                pe.wait_ge(s_w, 16 * 12)
                pe.wait_ge(s_own, 16 * 4)
                pe.wait_ge(s_wo, 48)
                pipeline(pe, [(turn_v, L_S), (scores, L_S), (turn, L_T), (project, 0), (pv, L_PV), (out_proj, L_Y)], SL, B)

            @block.vector
            def _(v):
                pipeline(v, [(o_out_v, L_O), (neg_max, L_S), (recip, L_R), (proj_in, 0), (add, L_Y)], SL, B)

            @block.scalar
            def _(a):
                pipeline(a, [(o_out_a, L_O), (v_in, L_S), (exps, L_S), (copy_turned, L_T)], SL, B)

            @block.gpsimd
            def _(g):
                pipeline(g, [(normalise, L_R)], SL, B)


def dispatch0(nc, xn, xnT, seT, slotsT, ident):
    L_T, L_M = 2, 3
    with Phase(nc, "d0") as ph:
        xs = ph.sb("xs", [P, 2, NB, D])
        DI = ph.sb("dispatch", [P, 2, T])
        DT = ph.sb("dispatchT", [P, 2, NB, P])
        nmax, sums, rsum = (ph.sb(n, [P, 2, 1]) for n in ("nmax", "sums", "rsum"))
        LG = [ph.ps(f"logits{k}", [P, T]) for k in range(2)]
        TB = [ph.ps(f"turned{k}", [P, NB, P]) for k in range(2)]
        SB_ = [ph.ps(f"slots{k}", [P, T]) for k in range(2)]
        s_xs, s_l, s_mx, s_e, s_r, s_n, s_T, s_t, s_m, s_o = (
            ph.sem(n) for n in ("xs_in", "logits_", "maxed", "exped", "recip", "normed", "turned_", "copied", "mixed", "out"))

        def logits(b, u):
            wait(nc.tensor, s_e, b * ST + u - 1)
            nc.tensor.matmul(LG[u % 2][:, :], seT[:, u * P:(u + 1) * P], xnT[:, bass.ds(b * T, T)],
                             start=True, stop=True).then_inc(s_l, 1)

        def turn(b, u):
            wait(nc.tensor, s_n, b * ST + u + 1)
            wait(nc.tensor, s_t, b * ST + u - 1)
            for n in range(NB):
                last = nc.tensor.transpose(TB[u % 2][:, n, :], DI[:, u % 2, n * P:(n + 1) * P], ident[:, :])
            last.then_inc(s_T, 1)

        def mix(b, u):
            wait(nc.tensor, s_t, b * ST + u + 1)
            if u == 0:
                wait(nc.tensor, s_xs, b + 1)
            wait(nc.tensor, s_o, b * ST + u - 1)
            for n in range(NB):
                last = nc.tensor.matmul(SB_[u % 2][:, 0:P], xs[:, 0, n, :], DT[:, u % 2, n, :],
                                        start=(n == 0), stop=(n == NB - 1))
            last.then_inc(s_m, 1)

        def neg_max(b, u):
            wait(nc.vector, s_l, b * ST + u + 1)
            wait(nc.vector, s_e, b * ST + u - 1)
            nc.vector.tensor_reduce(nmax[:, u % 2, :], LG[u % 2][:, :], AX.X, ALU.max, negate=True).then_inc(s_mx, 1)

        def recip(b, u):
            wait(nc.vector, s_e, b * ST + u + 1)
            wait(nc.vector, s_n, b * ST + u - 1)
            nc.vector.reciprocal(rsum[:, u % 2, :], sums[:, u % 2, :]).then_inc(s_r, 1)

        def copy_turned(b, u):
            wait(nc.vector, s_T, b * ST + u + 1)
            wait(nc.vector, s_m, b * ST + u - 1)
            nc.vector.tensor_copy(DT[:, u % 2, :, :], TB[u % 2][:, :, :]).then_inc(s_t, 1)

        def exps(b, u):
            wait(nc.scalar, s_mx, b * ST + u + 1)
            wait(nc.scalar, s_r, b * ST + u - 1)
            wait(nc.scalar, s_T, b * ST + u - 1)
            nc.scalar.activation(DI[:, u % 2, :], LG[u % 2][:, :], ACT.Exp, bias=nmax[:, u % 2, :],
                                 accum_out=sums[:, u % 2, :]).then_inc(s_e, 1)

        def slots_out(b, u):
            wait(nc.scalar, s_m, b * ST + u + 1)
            nc.scalar.activation(slotsT[:, bass.ds(b, 1), u * P:(u + 1) * P].rearrange("p o s -> p (o s)"),
                                 SB_[u % 2][:, 0:P], ACT.Copy).then_inc(s_o, 1)

        def stage_x(b, u):
            if u == 0:
                wait(nc.gpsimd, s_m, b * ST)
                nc.gpsimd.tensor_copy(xs[:, 0, :, :], xn[:, bass.ds(b * NB, NB), :]).then_inc(s_xs, 1)

        def normalise(b, u):
            wait(nc.gpsimd, s_r, b * ST + u + 1)
            nc.gpsimd.tensor_tensor(DI[:, u % 2, :], DI[:, u % 2, :], rsum[:, u % 2, :].broadcast_to([P, T]),
                                    ALU.mult).then_inc(s_n, 1)

        with nc.Block() as block:
            @block.tensor
            def _(pe):
                pipeline(pe, [(logits, 0), (turn, L_T), (mix, L_M)], ST, B)

            @block.vector
            def _(v):
                pipeline(v, [(neg_max, 0), (recip, 1), (copy_turned, L_T)], ST, B)

            @block.scalar
            def _(a):
                pipeline(a, [(exps, 0), (slots_out, L_M)], ST, B)

            @block.gpsimd
            def _(g):
                pipeline(g, [(normalise, 1), (stage_x, L_M)], ST, B)


def experts0(nc, ident, slotsT, eout, bgT, buT, Wg, Wu, Wd, bd):
    R, C = 4, B * S0
    KF = F0 // P
    with Phase(nc, "e0") as ph:
        wg, wu = ph.sb("wg", [P, R, F0]), ph.sb("wu", [P, R, F0])
        wd = ph.sb("wd", [P, R, KF, D])
        bdb = ph.sb("bd", [P, ST, D])
        h, hu = ph.sb("h", [P, 2, KF, C]), ph.sb("hu", [P, 2, KF, C])
        G = [ph.ps(f"gate{k}", [P, KF, C]) for k in range(2)]
        U = [ph.ps(f"up{k}", [P, KF, C]) for k in range(2)]
        EO = [ph.ps(f"out{k}", [P, B, D]) for k in range(2)]
        s_w = [ph.sem(f"weights{q}") for q in range(R)]
        s_bd, s_g, s_h, s_m, s_d, s_o = (ph.sem(n) for n in ("bd_in", "gated", "gelu", "times", "down", "out_"))

        def load(sp, i, q):
            e = i * R + q
            sp.dma_start(wg[:, q, :], Wg[bass.ds(e, 1)].rearrange("o d f -> d (o f)")).then_inc(s_w[q], 16)
            sp.dma_start(wu[:, q, :], Wu[bass.ds(e, 1)].rearrange("o d f -> d (o f)")).then_inc(s_w[q], 16)
            sp.dma_start(wd[:, q, :, :], Wd[bass.ds(e, 1)].rearrange("o (k p) n -> p (o k) n", p=P)).then_inc(s_w[q], 16)

        def gate_up(i, u):
            n = i * R + u
            wait(nc.tensor, s_w[u], (i + 1) * 48)
            wait(nc.tensor, s_m, n - 1)
            for bank, ww in ((G, wg), (U, wu)):
                for k in range(KF):
                    last = nc.tensor.matmul(bank[u % 2][:, k, :].rearrange("p (b s) -> p b s", b=B),
                                            ww[:, u, k * P:(k + 1) * P],
                                            slotsT[:, :, bass.ds(n * S0, S0)], start=True, stop=True)
            last.then_inc(s_g, 1)

        def down(i, u):
            n = i * R + u
            wait(nc.tensor, s_m, n + 1)
            wait(nc.tensor, s_o, i * (R // 2) + u // 2 - 1)
            for b in range(B):
                for k in range(KF):
                    last = nc.tensor.matmul(EO[u // 2][(u % 2) * S0:(u % 2 + 1) * S0, b, :],
                                            hu[:, u % 2, k, b * S0:(b + 1) * S0], wd[:, u, k, :],
                                            start=(k == 0), stop=(k == KF - 1))
            last.then_inc(s_d, 1)

        def gelu(i, u):
            n = i * R + u
            wait(nc.scalar, s_g, n + 1)
            wait(nc.scalar, s_m, n - 1)
            for k in range(KF):
                last = nc.scalar.activation(h[:, u % 2, k, :], G[u % 2][:, k, :], ACT.Gelu,
                                            bias=bgT[:, bass.ds(n * KF + k, 1)])
            last.then_inc(s_h, 1)

        def times(i, u):
            n = i * R + u
            wait(nc.vector, s_h, n + 1)
            wait(nc.vector, s_d, n - 1)
            for k in range(KF):
                last = nc.vector.scalar_tensor_tensor(out=hu[:, u % 2, k, :], in0=U[u % 2][:, k, :],
                                                      scalar=buT[:, bass.ds(n * KF + k, 1)], in1=h[:, u % 2, k, :],
                                                      op0=ALU.add, op1=ALU.mult)
            last.then_inc(s_m, 1)

        def out(i, u):
            if u % 2 == 1:
                n = i * R + u
                wait(nc.vector, s_d, n + 1)
                st = i * (R // 2) + u // 2
                nc.vector.tensor_tensor(eout[:, bass.ds(st, 1), :, :].rearrange("p o b d -> p (o b) d"), EO[u // 2][:, :, :],
                                        bdb[:, bass.ds(st, 1), :].broadcast_to([P, B, D]),
                                        ALU.add).then_inc(s_o, 1)

        with nc.Block() as block:
            @block.sync
            def _(sp):
                for q in range(2):
                    src = bd.rearrange("(t q) d -> q t d", q=2)[q:q + 1]
                    sp.dma_start(bdb[q * S0:(q + 1) * S0, :, :], src.broadcast_to([S0, ST, D])).then_inc(s_bd, 16)
                for q in range(R):
                    load(sp, 0, q)
                with sp.Fori(1, E0 // R) as i:
                    for q in range(R):
                        sp.wait_ge(s_d, i * R + q - R + 1)
                        load(sp, i, q)

            @block.tensor
            def _(pe):
                pipeline(pe, [(gate_up, 0), (down, 1)], R, E0 // R)

            @block.scalar
            def _(a):
                pipeline(a, [(gelu, 0)], R, E0 // R)

            @block.vector
            def _(v):
                v.wait_ge(s_bd, 32)
                pipeline(v, [(times, 0), (out, 1)], R, E0 // R)


def combine0(nc, x_nat, xnT, seT, eout, ident):
    L_T, L_Y = 1, 2
    with Phase(nc, "c0") as ph:
        xs = ph.sb("xs", [P, T])
        CO = ph.sb("combine", [P, 2, ST * P])
        CT = ph.sb("combineT", [P, 2, ST, P])
        nmax = ph.sb("nmax", [P, 2, 1])
        sums, rsum = ph.sb("sums", [P, 4, 1]), ph.sb("rsum", [P, 4, 1])
        LG = [ph.ps(f"logits{k}", [P, ST * P]) for k in range(2)]
        TB = ph.ps("turned", [P, ST, P])
        Y = [ph.ps(f"y{k}", [P, T]) for k in range(2)]
        s_xs, s_l, s_mx, s_e, s_r, s_T, s_ta, s_td, s_y, s_o = (
            ph.sem(n) for n in ("xs_in", "logits_", "maxed", "exped", "recip", "turned_", "copied_a", "copied_d", "mixed", "out"))
        HS = ST // 2

        def logits(b, u):
            if u == 0:
                wait(nc.tensor, s_xs, b + 1)
            wait(nc.tensor, s_e, b * NB + u - 1)
            for k in range(2):
                last = nc.tensor.matmul(LG[u % 2][:, k * T:(k + 1) * T], xs[:, u * P:(u + 1) * P],
                                        seT[:, k * T:(k + 1) * T], start=True, stop=True)
            last.then_inc(s_l, 1)

        def turn(b, u):
            wait(nc.tensor, s_e, b * NB + u + 1)
            wait(nc.tensor, s_ta, b * NB + u)
            wait(nc.tensor, s_td, b * NB + u)
            for k in range(ST):
                last = nc.tensor.transpose(TB[:, k, :], CO[:, u % 2, k * P:(k + 1) * P], ident[:, :])
            last.then_inc(s_T, 1)

        def mix(b, u):
            wait(nc.tensor, s_ta, b * NB + u + 1)
            wait(nc.tensor, s_td, b * NB + u + 1)
            wait(nc.tensor, s_o, b * NB + u - 1)
            for k in range(ST):
                last = nc.tensor.matmul(Y[u % 2][:, 0:D], CT[:, u % 2, k, :],
                                        eout[:, k, bass.ds(b, 1), :].rearrange("p o d -> p (o d)"),
                                        start=(k == 0), stop=(k == ST - 1))
            last.then_inc(s_y, 1)

        def neg_max(b, u):
            wait(nc.vector, s_l, b * NB + u + 1)
            wait(nc.vector, s_e, b * NB + u - 1)
            nc.vector.tensor_reduce(nmax[:, u % 2, :], LG[u % 2][:, :], AX.X, ALU.max, negate=True).then_inc(s_mx, 1)

        def recip(b, u):
            wait(nc.vector, s_e, b * NB + u + 1)
            wait(nc.vector, s_o, b * NB + u - 3)
            nc.vector.reciprocal(rsum[:, u % 4, :], sums[:, u % 4, :]).then_inc(s_r, 1)

        def copy_turned_v(b, u):
            wait(nc.vector, s_T, b * NB + u + 1)
            wait(nc.vector, s_y, b * NB + u - 1)
            nc.vector.tensor_copy(CT[:, u % 2, 0:HS, :], TB[:, 0:HS, :]).then_inc(s_td, 1)

        def add(b, u):
            wait(nc.vector, s_y, b * NB + u + 1)
            wait(nc.vector, s_r, b * NB + u + 1)
            x = x_nat[:, bass.ds(b * NB + u, 1), :].rearrange("p o d -> p (o d)")
            nc.vector.scalar_tensor_tensor(out=x, in0=Y[u % 2][:, 0:D], scalar=rsum[:, u % 4, :], in1=x,
                                           op0=ALU.mult, op1=ALU.add).then_inc(s_o, 1)

        def exps(b, u):
            wait(nc.scalar, s_mx, b * NB + u + 1)
            wait(nc.scalar, s_r, b * NB + u - 3)
            wait(nc.scalar, s_T, b * NB + u - 1)
            nc.scalar.activation(CO[:, u % 2, :], LG[u % 2][:, :], ACT.Exp, bias=nmax[:, u % 2, :],
                                 accum_out=sums[:, u % 4, :]).then_inc(s_e, 1)

        def copy_turned_a(b, u):
            wait(nc.scalar, s_T, b * NB + u + 1)
            wait(nc.scalar, s_y, b * NB + u - 1)
            nc.scalar.activation(CT[:, u % 2, HS:ST, :], TB[:, HS:ST, :], ACT.Copy).then_inc(s_ta, 1)

        with nc.Block() as block:
            @block.gpsimd
            def _(g):
                nc.gpsimd.tensor_copy(xs[:, :], xnT[:, 0:T]).then_inc(s_xs, 1)
                with g.Fori(1, B) as b:
                    g.wait_ge(s_l, b * NB)
                    nc.gpsimd.tensor_copy(xs[:, :], xnT[:, bass.ds(b * T, T)]).then_inc(s_xs, 1)

            @block.tensor
            def _(pe):
                pipeline(pe, [(logits, 0), (turn, L_T), (mix, L_Y)], NB, B)

            @block.vector
            def _(v):
                pipeline(v, [(neg_max, 0), (recip, 1), (copy_turned_v, L_T), (add, L_Y)], NB, B)

            @block.scalar
            def _(a):
                pipeline(a, [(exps, 0), (copy_turned_a, L_T)], NB, B)


RS = 4 * HD1


def prepare1(nc, xT, ident, qsT, ksT, vN, infT, bias, ones, wq, wd, wu, bu, cos, sin, s_w):
    W4, HALF = [P, NB, H1, HD1], HD1 // 2
    PER = 2
    TURNS = 2 * G1 + 1
    with Phase(nc, "p1") as ph:
        qT, cT = ph.sb("qT", [P, T]), ph.sb("cT", [LAT, T])
        q = [ph.sb(f"q{u}", W4) for u in range(PER)]
        kv = [ph.sb(f"kv{u}", [P, NB, H1, 2 * HD1]) for u in range(PER)]
        rot = {s: [ph.sb(f"rot_{s}{u}", W4) for u in range(PER)] for s in "qk"}
        hi = {s: [ph.sb(f"high_{s}{u}", W4) for u in range(PER)] for s in "qk"}
        st = {s: [ph.sb(f"stack_{s}{u}", [P, NB * H1, 4, HD1]) for u in range(PER)] for s in "qk"}
        tt = {s: [ph.sb(f"t{k}{s}", [P, NB, H1, HALF]) for k in range(4)] for s in "qk"}
        rs = ph.sb("rs", W4)
        prod, inf = ph.sb("prod", W4), ph.sb("inf", W4)
        score, gate, gate2 = (ph.sb(n, [P, NB, H1]) for n in ("score", "gate", "gate2"))
        PQ, PN, PC = ph.ps("pq", [P, T]), ph.ps("pn", [P, T]), ph.ps("pc", [P, T])
        KV = ph.ps("pkv", [P, NB, 2 * D])
        PM = ph.ps("pmean", [P, T])
        PT = [ph.ps(f"turned{k}", [P, T]) for k in range(2)]
        s_pq, s_qT, s_pc, s_cT, s_pn, s_kv = (ph.sem(n) for n in ("pq_", "qT_", "pc_", "cT_", "pn_", "pkv_"))
        s_x = {s: ph.sem("x_" + s) for s in "qk"}
        s_t = {s: ph.sem("products_" + s) for s in "qk"}
        s_rot = {s: ph.sem("rotated_" + s) for s in "qk"}
        s_hi = {s: ph.sem("high_" + s) for s in "qk"}
        s_st = {s: ph.sem("stacked_" + s) for s in "qk"}
        s_sh = {s: ph.sem("stacked_high_" + s) for s in "qk"}
        s_sc, s_rs, s_v, s_mn, s_pr, s_g, s_g2, s_inf, s_tt, s_to = (
            ph.sem(n) for n in ("score_", "scaled", "v_", "mean", "prod_", "gate_", "gate2_", "inf_", "tt", "to"))

        def flat(t):
            return t[:, :, :, :].rearrange("p n h d -> p (n h d)")

        def rotate(eng, e, s, n, src, dst):
            c4, s4 = (t[:, :, None, :].broadcast_to([P, NB, H1, HALF]) for t in (cos, sin))
            x1, x2 = src[:, :, :, 0:HALF], src[:, :, :, HALF:HD1]
            t = tt[s]
            wait(eng, s_rot[s], 2 * n)
            wait(eng, s_x[s], n + 1)
            for k, (i0, i1) in enumerate(((x1, c4), (x2, s4), (x1, s4), (x2, c4))):
                e.tensor_tensor(t[k][:, :, :, :], i0, i1, ALU.mult).then_inc(s_t[s], 1)
            wait(eng, s_t[s], (n + 1) * 4)
            e.tensor_tensor(dst[:, :, :, 0:HALF], t[0][:, :, :, :], t[1][:, :, :, :], ALU.subtract).then_inc(s_rot[s], 1)
            e.tensor_tensor(dst[:, :, :, HALF:HD1], t[2][:, :, :, :], t[3][:, :, :, :], ALU.add).then_inc(s_rot[s], 1)

        def high(src, s, u):
            nc.vector.tensor_scalar(flat(hi[s][u]).bitcast(I32), flat(src).bitcast(I32), -4096, None,
                                    ALU.bitwise_and).then_inc(s_hi[s], 1)

        SETS = {"q": (slice(0, 2), slice(2, 4)), "k": (slice(0, 4, 2), slice(1, 4, 2))}

        def row_sets(t):
            return t[:, :, :, :].rearrange("p n h d -> p (n h) d")[:, :, None, :].broadcast_to([P, NB * H1, 2, HD1])

        def stack_rest(e, src, s, u):
            e.tensor_tensor(st[s][u][:, :, SETS[s][1], :], row_sets(src), row_sets(hi[s][u]), ALU.subtract).then_inc(s_st[s], 1)

        def project(i, u):
            b = i * PER + u
            x = xT[:, bass.ds(b * T, T)]
            wait(nc.tensor, s_qT, b)
            wait(nc.tensor, s_cT, b)
            nc.tensor.matmul(PQ[:, :], wq[:, :], x, start=True, stop=True).then_inc(s_pq, 1)
            nc.tensor.matmul(PC[0:LAT, :], wd[:, :], x, start=True, stop=True).then_inc(s_pc, 1)
            wait(nc.tensor, s_qT, b + 1)
            wait(nc.tensor, s_x["q"], b)
            for n in range(NB):
                last = nc.tensor.transpose(PN[:, n * P:(n + 1) * P], qT[:, n * P:(n + 1) * P], ident[:, :])
            last.then_inc(s_pn, 1)
            wait(nc.tensor, s_cT, b + 1)
            wait(nc.tensor, s_x["k"], b)
            for n in range(NB):
                last = nc.tensor.matmul(KV[:, n, :], cT[:, n * P:(n + 1) * P], wu[:, :], start=True, stop=True)
            last.then_inc(s_kv, 1)

        def means(i, u):
            b = i * PER + u
            wait(nc.tensor, s_rot["k"], (b + 1) * 2)
            wait(nc.tensor, s_inf, b)
            for n in range(NB):
                nc.tensor.matmul(PM[:, 0:D], ones[:, :], rot["k"][u][:, n, :, :].rearrange("p h d -> p (h d)"),
                                 start=(n == 0), stop=(n == NB - 1))
            for n in range(NB):
                last = nc.tensor.matmul(PM[:, D:2 * D], ones[:, :], kv[u][:, n, :, HD1:2 * HD1],
                                        start=(n == 0), stop=(n == NB - 1))
            last.then_inc(s_mn, 1)

        def turns(i, u):
            b = i * PER + u
            for k in range(TURNS):
                if k in (0, G1):
                    s = "qk"[k // G1]
                    wait(nc.tensor, s_sh[s], b + 1)
                    wait(nc.tensor, s_st[s], b + 1)
                if k == TURNS - 1:
                    wait(nc.tensor, s_inf, b + 1)
                wait(nc.tensor, s_to, b * TURNS + k - (1 if k else 0))
                for n in range(NB):
                    if k == TURNS - 1:
                        src = inf[:, n, :, :].rearrange("p h d -> p (h d)")
                    else:
                        r = n * H1 + k % G1 * HG
                        src = st["qk"[k // G1]][u][:, r:r + HG, :, :].rearrange("p h r d -> p (h r d)")
                    last = nc.tensor.transpose(PT[k % 2][:, n * P:(n + 1) * P], src, ident[:, :])
                last.then_inc(s_tt, 1)

        def biased(i, u):
            b = i * PER + u
            wait(nc.scalar, s_pq, b + 1)
            wait(nc.scalar, s_pn, b)
            nc.scalar.activation(qT[:, :], PQ[:, :], ACT.Identity, bias=bias[:, 0:1]).then_inc(s_qT, 1)
            wait(nc.scalar, s_pc, b + 1)
            wait(nc.scalar, s_kv, b)
            nc.scalar.activation(cT[:, :], PC[0:LAT, :], ACT.Identity, bias=bias[0:LAT, 1:2]).then_inc(s_cT, 1)

        def stack_high(i, u):
            b = i * PER + u
            for s in "qk":
                wait(nc.scalar, s_hi[s], b + 1)
                wait(nc.scalar, s_tt, (b - 1) * TURNS)
                nc.scalar.activation(st[s][u][:, :, SETS[s][0], :], row_sets(hi[s][u]), ACT.Copy).then_inc(s_sh[s], 1)

        def v_rows(i, u):
            b = i * PER + u
            wait(nc.scalar, s_x["k"], b + 1)
            nc.scalar.activation(vN[:, bass.ds(b * NB, NB), :].rearrange("p n (h d) -> p n h d", h=H1),
                                 kv[u][:, :, :, HD1:2 * HD1], ACT.Copy).then_inc(s_v, 1)

        def turned_out(i, u):
            b = i * PER + u
            for k in range(TURNS):
                wait(nc.scalar, s_tt, b * TURNS + k + 1)
                dst = (infT[:, bass.ds(b * T, T)] if k == TURNS - 1 else
                       (qsT, ksT)[k // G1][:, k % G1, bass.ds(b * T, T)])
                nc.scalar.activation(dst, PT[k % 2][:, :], ACT.Copy).then_inc(s_to, 1)

        def gates(i, u):
            b = i * PER + u
            wait(nc.scalar, s_sc, b + 1)
            nc.scalar.activation(gate[:, :, :], score[:, :, :], ACT.Sigmoid).then_inc(s_g, 1)

        def take(i, u):
            b = i * PER + u
            wait(nc.vector, s_pn, b + 1)
            nc.vector.tensor_copy(flat(q[u]), PN[:, :]).then_inc(s_x["q"], 1)
            wait(nc.vector, s_kv, b + 1)
            wait(nc.vector, s_mn, b - 1)
            wait(nc.vector, s_v, b - 1)
            nc.vector.tensor_tensor(kv[u][:, :, :, :].rearrange("p n h d -> p n (h d)"), KV[:, :, :],
                                    bu[:, None, :].broadcast_to([P, NB, 2 * D]), ALU.add).then_inc(s_x["k"], 1)

        def q_rows(i, u):
            b = i * PER + u
            rotate(nc.vector, nc.vector, "q", b, q[u], rot["q"][u])
            wait(nc.vector, s_rot["q"], (b + 1) * 2)
            nc.vector.tensor_scalar(flat(rs), flat(rot["q"][u]), -HD1 ** -0.5, None, ALU.mult).then_inc(s_rs, 1)
            wait(nc.vector, s_rs, b + 1)
            wait(nc.vector, s_sh["q"], b - 1)
            high(rs, "q", u)
            wait(nc.vector, s_hi["q"], b + 1)
            wait(nc.vector, s_tt, (b - 1) * TURNS)
            stack_rest(nc.vector, rs, "q", u)
            wait(nc.vector, s_rot["k"], (b + 1) * 2)
            wait(nc.vector, s_sh["k"], b - 1)
            wait(nc.vector, s_st["k"], b - 1)
            high(rot["k"][u], "k", u)

        def memory(i, u):
            b = i * PER + u
            wait(nc.vector, s_mn, b + 1)
            nc.vector.tensor_tensor(prod[:, :, :, :].rearrange("p n h d -> p n (h d)"),
                                    rot["q"][u][:, :, :, :].rearrange("p n h d -> p n (h d)"),
                                    PM[:, None, 0:D].broadcast_to([P, NB, D]), ALU.mult).then_inc(s_pr, 1)
            wait(nc.vector, s_pr, b + 1)
            nc.vector.tensor_reduce(score[:, :, :], prod[:, :, :, :], AX.X, ALU.add).then_inc(s_sc, 1)
            wait(nc.vector, s_g, b + 1)
            nc.vector.tensor_scalar(gate2[:, :, :], gate[:, :, :], 0.2, None, ALU.mult).then_inc(s_g2, 1)
            wait(nc.vector, s_g2, b + 1)
            wait(nc.vector, s_tt, b * TURNS)
            nc.vector.tensor_tensor(inf[:, :, :, :], gate2[:, :, :, None].broadcast_to(W4),
                                    PM[:, D:2 * D].rearrange("p (h d) -> p h d", h=H1)[:, None, :, :].broadcast_to(W4),
                                    ALU.mult).then_inc(s_inf, 1)

        def k_rows(i, u):
            b = i * PER + u
            wait(nc.gpsimd, s_mn, b - 1)
            rotate(nc.gpsimd, nc.gpsimd, "k", b, kv[u], rot["k"][u])
            wait(nc.gpsimd, s_tt, (b - 1) * TURNS)
            wait(nc.gpsimd, s_hi["k"], b + 1)
            stack_rest(nc.gpsimd, rot["k"][u], "k", u)

        with nc.Block() as block:
            @block.tensor
            def _(pe):
                pe.wait_ge(s_w, SMALL1 * 16)
                pipeline(pe, [(project, 0), (turns, 2), (means, 1)], PER, B // PER)

            @block.scalar
            def _(a):
                pipeline(a, [(biased, 0), (turned_out, 2), (v_rows, 1), (stack_high, 1), (gates, 1)], PER, B // PER)

            @block.vector
            def _(v):
                v.wait_ge(s_w, SMALL1 * 16)
                pipeline(v, [(take, 0), (q_rows, 1), (memory, 1)], PER, B // PER)

            @block.gpsimd
            def _(g):
                g.wait_ge(s_w, SMALL1 * 16)
                pipeline(g, [(k_rows, 1)], PER, B // PER)


def attention1(nc, x_nat, xT, qsT, ksT, vN, infT, mask, ident, bias, Wo, bo_in, s_c):
    SL = 4 * G1
    TL = 4 * SL
    L_S, L_T, L_PV = 2, 6, 7
    with Phase(nc, "a1") as ph:
        QZ = ph.sb("qz", [P, 4, T], F32R)
        VZ = ph.sb("vz", [P, 2, NB, HG, RS])
        PR = ph.sb("probs", [P, 2, HG, NB, T])
        PT = ph.sb("probsT", [P, 2, HG, T])
        least = ph.sb("least", [P, 4, NB])
        first_v, first_g = ph.sb("first_v", [P, 4]), ph.sb("first_g", [P, 4])
        wog, wo, bo = ph.sb("wog", [P, G1, D]), ph.sb("wo", [P, D]), ph.sb("bo", [P, D])
        rec = ph.sb("rec", [P, 2, NB, HG])
        wide = xT[:, 0:2 * T].rearrange("p (u r h j) -> p u r h j", u=2, r=NB, h=HG)
        SC = [ph.ps(f"scores{k}", [P, T]) for k in range(3)]
        TB = [ph.ps(f"turned{k}", [P, 2, T]) for k in range(2)]
        OB = ph.ps("outT", [P, T])
        s_wo, s_z = ph.sem("wout"), ph.sem("zeros")
        s_qz, s_vz, s_S, s_b, s_e = (ph.sem(n) for n in ("q_in", "v_in", "scored", "biased", "exped"))
        s_T, s_ta, s_td, s_pv, s_o = (ph.sem(n) for n in ("turned_", "copied_a", "copied_d", "pv", "o_out"))
        s_fv, s_fg = ph.sem("first_v_"), ph.sem("first_g_")
        s_s, s_rc, s_w, s_sp, s_dv, s_y, s_x, s_xb = (ph.sem(n) for n in ("sums", "recip", "widened", "spread_", "divided", "y", "x", "xb"))

        def head_q(b, u):
            g, j = u // 4, u % 4
            wait(nc.gpsimd, s_fg, b * SL + u - 3)
            wait(nc.gpsimd, s_S, b * TL + 4 * u - 12)
            nc.gpsimd.tensor_tensor(first_g[:, j:j + 1], mask[:, 0:1], mask[:, 0:1], ALU.mult).then_inc(s_fg, 1)
            nc.gpsimd.tensor_tensor(QZ[:, j, :], qsT[:, g, bass.ds(b * T, T)].bitcast(F32),
                                    mask[:, j:j + 1].broadcast_to([P, T]), ALU.mult).then_inc(s_qz, 1)

        def head_v(b, u):
            g, j = u // 4, u % 4
            if j == 0:
                wait(nc.gpsimd, s_pv, b * SL + u - 4)
                src = vN[:, bass.ds(b * NB, NB), g * HG * HD1:(g + 1) * HG * HD1].rearrange("p n (h d) -> p n h d", h=HG)
                nc.gpsimd.tensor_copy(VZ[:, g % 2, :, :, 0:HD1], src).then_inc(s_vz, 1)

        def scores(b, u, pair):
            g, j = u // 4, u % 4
            if pair == 0:
                wait(nc.tensor, s_qz, b * SL + u + 1)
            for r in (2 * pair, 2 * pair + 1):
                m = 4 * u + r
                wait(nc.tensor, s_b, b * TL + m - (2 if m else 0))
                nc.tensor.matmul(SC[m % 3][:, :], QZ[:, j, r * P:(r + 1) * P], ksT[:, g, bass.ds(b * T, T)],
                                 start=True, stop=True).then_inc(s_S, 1)

        def scores_1(b, u):
            scores(b, u, 0)

        def scores_2(b, u):
            scores(b, u, 1)

        def turn(b, u, half):
            g, j = u // 4, u % 4
            wait(nc.tensor, (s_td, s_ta)[half], b * SL + u)
            for h in range(2):
                for r in range(NB):
                    last = nc.tensor.transpose(TB[half][:, h, r * P:(r + 1) * P],
                                               PR[:, g % 2, 2 * half + h, r, j * P:(j + 1) * P], ident[:, :])
            last.then_inc(s_T, 1)

        def turn_1(b, u):
            if u % 4 == 0:
                wait(nc.tensor, s_e, b * SL + u + 4)
            turn(b, u, 0)

        def turn_2(b, u):
            turn(b, u, 1)

        def pv(b, u):
            g, j = u // 4, u % 4
            wait(nc.tensor, s_ta, b * SL + u + 1)
            wait(nc.tensor, s_td, b * SL + u + 1)
            if j == 0:
                wait(nc.tensor, s_vz, b * G1 + g + 1)
                wait(nc.tensor, s_o, b * G1 + g)
            for h in range(HG):
                last = nc.tensor.matmul(OB[h * RS:(h + 1) * RS, :], VZ[:, g % 2, j, h, :], PT[:, u % 2, h, :],
                                        start=(j == 0), stop=(j == NB - 1))
            last.then_inc(s_pv, 1)

        def start_v(b, u):
            wait(nc.vector, s_fv, b * SL + u - 3)
            wait(nc.vector, s_e, b * SL + u - 3)
            if u % 4 == 0:
                wait(nc.vector, s_T, b * 2 * SL + 2 * u - 8)
            wait(nc.vector, s_S, b * TL + 4 * u + 2)
            nc.vector.tensor_copy(first_v[:, u % 4:u % 4 + 1], mask[:, 0:1]).then_inc(s_fv, 1)

        def add_bias(b, u, pair):
            g, j = u // 4, u % 4
            for r in (2 * pair, 2 * pair + 1):
                m = 4 * u + r
                nc.vector.tensor_tensor_reduce(PR[:, g % 2, j, r, :], SC[m % 3][:, :], bias[:, r, :], 1.0, 3.0e38,
                                               ALU.add, ALU.min, least[:, j, r:r + 1]).then_inc(s_b, 1)

        def add_bias_1(b, u):
            add_bias(b, u, 0)

        def await_scores_2(b, u):
            wait(nc.vector, s_S, b * TL + 4 * u + 4)

        def copy_turned_v(b, u):
            wait(nc.vector, s_T, b * 2 * SL + 2 * u + 1)
            wait(nc.vector, s_pv, b * SL + u - 1)
            nc.vector.tensor_copy(PT[:, u % 2, 0:2, :], TB[0][:, :, :]).then_inc(s_td, 1)

        def add_bias_2(b, u):
            add_bias(b, u, 1)

        def exps(b, u, tiles):
            g, j = u // 4, u % 4
            for r in tiles:
                wait(nc.scalar, s_b, b * TL + 4 * u + r + 1)
                pr = PR[:, g % 2, j, r, :]
                last = nc.scalar.activation(pr, pr, ACT.Exp, bias=least[:, j, r:r + 1], scale=-1.0)
            return last

        def exps_1(b, u):
            exps(b, u, (0, 1))

        def copy_turned_a(b, u):
            wait(nc.scalar, s_T, b * 2 * SL + 2 * u + 2)
            wait(nc.scalar, s_pv, b * SL + u - 1)
            nc.scalar.activation(PT[:, u % 2, 2:4, :], TB[1][:, :, :], ACT.Copy).then_inc(s_ta, 1)

        def exps_2(b, u):
            exps(b, u, (2, 3)).then_inc(s_e, 1)

        def o_out(b, u):
            g, j = u // 4, u % 4
            if j == 3:
                wait(nc.scalar, s_pv, b * SL + u + 1)
                nc.scalar.activation(qsT[:, g, bass.ds(b * T, T)].bitcast(F32), OB[:, :], ACT.Copy).then_inc(s_o, 1)

        with nc.Block() as block:
            @block.sync
            def _(sp):
                sp.wait_ge(s_z, 2)
                for h in range(HG):
                    sp.dma_start(wog[h * RS:h * RS + HD1, :, :],
                                 Wo.rearrange("(g h d) n -> h d g n", g=G1, h=HG)[h]).then_inc(s_wo, 16)
                sp.dma_start(wo[:, :], Wo).then_inc(s_wo, 16)
                sp.dma_start(bo[:, :], bo_in[None, :].broadcast_to([P, D])).then_inc(s_wo, 16)

            def spread(pe, n):
                wait(pe, s_dv, n - 1)
                pe.wait_ge(s_w, n + 1)
                for r in range(NB):
                    last = nc.tensor.matmul(TB[n % 2][:, 1, r * P:(r + 1) * P],
                                            wide[:, n % 2, r, :, :].rearrange("p h j -> p (h j)"),
                                            ident[:, :], start=True, stop=True)
                last.then_inc(s_sp, 1)

            @block.tensor
            def _(pe):
                pe.wait_ge(s_z, 3)
                pipeline(pe, [(scores_1, L_S), (turn_1, L_T), (scores_2, L_S), (turn_2, L_T), (pv, L_PV)], SL, B)
                pe.wait_ge(s_wo, 16 * (HG + 2))
                pe.wait_ge(s_o, B * G1)
                for t in range(NT):
                    b, at = t // NB, slice(t * P, (t + 1) * P)
                    if t % NB == 0:
                        for g in range(G1):
                            n = b * G1 + g
                            wait(pe, s_rc, n - 1)
                            for r in range(NB):
                                o = qsT[:, g, (b * NB + r) * P:(b * NB + r + 1) * P].bitcast(F32)
                                last = nc.tensor.transpose(TB[g % 2][:, 0, r * P:(r + 1) * P], o, ident[:, :])
                            last.then_inc(s_s, 1)
                            if g:
                                spread(pe, n - 1)
                        spread(pe, n)
                        pe.wait_ge(s_dv, (b + 1) * G1)
                    wait(pe, s_y, t - 1)
                    for g in range(G1):
                        nc.tensor.matmul(SC[t % 2][:, 0:D], qsT[:, g, at].bitcast(F32), wog[:, g, :], start=(g == 0), stop=False)
                    nc.tensor.matmul(SC[t % 2][:, 0:D], infT[:, at], wo[:, :], start=False, stop=True).then_inc(s_x, 1)

            @block.vector
            def _(v):
                nc.vector.memset(VZ[:, :, :, :, :], 0.0).then_inc(s_z, 1)
                nc.vector.memset(wog[:, :, :], 0.0).then_inc(s_z, 1)
                v.wait_ge(s_z, 2)
                nc.vector.memset(VZ[:, :, :, :, HD1:HD1 + 1], 1.0).then_inc(s_z, 1)
                v.wait_ge(s_c, 16)
                pipeline(v, [(start_v, L_S), (add_bias_1, L_S), (await_scores_2, L_S), (copy_turned_v, L_T),
                             (add_bias_2, L_S)], SL, B)
                v.wait_ge(s_wo, 16 * (HG + 2))
                nc.vector.tensor_tensor(x_nat[:, :, :], x_nat[:, :, :], bo[:, None, :].broadcast_to([P, NT, D]),
                                        ALU.add).then_inc(s_xb, 1)
                v.wait_ge(s_xb, 1)
                for b in range(B):
                    for g in range(G1 + 1):
                        n = b * G1 + g
                        if g < G1:
                            v.wait_ge(s_s, n + 1)
                            wait(v, s_sp, n - 1)
                            nc.vector.reciprocal(rec[:, n % 2, :, :],
                                                 TB[g % 2][:, 0, :].rearrange("p (r h j) -> p r h j", r=NB, h=HG)[:, :, :, HD1]
                                                 ).then_inc(s_rc, 1)
                        if g:
                            v.wait_ge(s_sp, n)
                            o = qsT[:, g - 1, b * T:(b + 1) * T].bitcast(F32)
                            nc.vector.tensor_tensor(o, o, TB[(n - 1) % 2][:, 1, :], ALU.mult).then_inc(s_dv, 1)
                    for t in range(b * NB, (b + 1) * NB):
                        v.wait_ge(s_x, t + 1)
                        nc.vector.tensor_tensor(x_nat[:, t, :], SC[t % 2][:, 0:D], x_nat[:, t, :], ALU.add).then_inc(s_y, 1)

            @block.scalar
            def _(a):
                pipeline(a, [(exps_1, L_S), (copy_turned_a, L_T), (exps_2, L_S), (o_out, L_PV)], SL, B)
                for n in range(B * G1):
                    a.wait_ge(s_rc, n + 1)
                    wait(a, s_sp, n - 1)
                    nc.scalar.activation(wide[:, n % 2, :, :, :], rec[:, n % 2, :, :, None].broadcast_to([P, NB, HG, RS]),
                                         ACT.Copy).then_inc(s_w, 1)

            @block.gpsimd
            def _(g):
                g.wait_ge(s_z, 3)
                pipeline(g, [(head_q, 0), (head_v, 4)], SL, B)


def gates1(nc, xT, combine, gw, num, s_w):
    W = [P, NT, E1]
    with Phase(nc, "g1") as ph:
        lg, ex, pr, top = (ph.sb(n, W) for n in ("lg", "ex", "pr", "top"))
        c1, c2 = ph.sb("c1", W), ph.sb("c2", W)
        at, atf = ph.sb("at", W, U32), ph.sb("atf", W)
        mx, sm, rs, s2, r2 = (ph.sb(n, [P, NT]) for n in ("mx", "sm", "rs", "s2", "r2"))
        wt = ph.sb("wt", [P, 2, NT])
        LG = ph.ps("logits", [P, NT, E1])
        s_l, s_c, s_e, s_m = (ph.sem(n) for n in ("l", "chain", "exped", "tops"))

        with nc.Block() as block:
            @block.tensor
            def _(pe):
                pe.wait_ge(s_w, SMALL1 * 16)
                for t in range(NT):
                    last = nc.tensor.matmul(LG[:, t, :], xT[:, t * P:(t + 1) * P], gw[:, :], start=True, stop=True)
                last.then_inc(s_l, 1)

            @block.scalar
            def _(a):
                a.wait_ge(s_c, 2)
                nc.scalar.activation(ex[:, :, :], lg[:, :, :], ACT.Exp).then_inc(s_e, 1)

            @block.vector
            def _(v):
                count = [0]

                def link(ins):
                    count[0] += 1
                    ins.then_inc(s_c, 1)
                    v.wait_ge(s_c, count[0])

                v.wait_ge(s_l, 1)
                v.wait_ge(s_w, SMALL1 * 16)
                link(nc.vector.tensor_reduce(mx[:, :], LG[:, :, :], AX.X, ALU.max))
                link(nc.vector.tensor_tensor(lg[:, :, :], LG[:, :, :], mx[:, :, None].broadcast_to(W), ALU.subtract))
                v.wait_ge(s_e, 1)
                link(nc.vector.tensor_reduce(sm[:, :], ex[:, :, :], AX.X, ALU.add))
                link(nc.vector.reciprocal(rs[:, :], sm[:, :]))
                link(nc.vector.tensor_tensor(pr[:, :, :], ex[:, :, :], rs[:, :, None].broadcast_to(W), ALU.mult))
                for t in range(NT):
                    nc.vector.max(top[:, t, :], pr[:, t, :]).then_inc(s_m, 1)
                for t in range(NT):
                    v.wait_ge(s_m, t + 1)
                    last = nc.vector.max_index(at[:, t, :], top[:, t, :], pr[:, t, :])
                link(last)
                link(nc.vector.tensor_copy(atf[:, :, :], at[:, :, :]))
                link(nc.vector.tensor_tensor(s2[:, :], top[:, :, 0], top[:, :, 1], ALU.add))
                link(nc.vector.reciprocal(r2[:, :], s2[:, :]))
                link(nc.vector.tensor_tensor(wt[:, 0, :], top[:, :, 0], r2[:, :], ALU.mult))
                link(nc.vector.tensor_tensor(wt[:, 1, :], top[:, :, 1], r2[:, :], ALU.mult))
                for k, c in enumerate((c1, c2)):
                    link(nc.vector.tensor_tensor(c[:, :, :], num[:, None, :].broadcast_to(W),
                                                 atf[:, :, k:k + 1].broadcast_to(W), ALU.is_equal))
                    link(nc.vector.tensor_tensor(c[:, :, :], c[:, :, :], wt[:, k, :, None].broadcast_to(W), ALU.mult))
                link(nc.vector.tensor_tensor(combine[:, :, :], c1[:, :, :], c2[:, :, :], ALU.add))


def experts1(nc, x_nat, xT, combine, w_gate, w_up, w_down):
    PER = 2 * B
    L_G, L_D = 2, 3
    with Phase(nc, "e1") as ph:
        wgu = ph.sb("wgu", [P, 2, 2, F1])
        wH, wL = ph.sb("w_high", [P, 2, 2, F1], F32R), ph.sb("w_rest", [P, 2, 2, F1], F32R)
        xH, xL = ph.sb("x_high", [P, B * T], F32R), ph.sb("x_rest", [P, B * T], F32R)
        w32, x32 = ph.sb("w_high32", [P, 2, 2, F1]), ph.sb("x_high32", [P, B * T])
        wd = ph.sb("wd", [P, 2, FT, D])
        h, hu = ph.sb("h", [P, 2, T]), ph.sb("hu", [P, 2, FT, T])
        G = [ph.ps(f"gate{k}", [P, T]) for k in range(2)]
        U = [ph.ps(f"up{k}", [P, T]) for k in range(2)]
        Y = [ph.ps(f"out{k}", [P, NB, D]) for k in range(2)]
        s_w = [ph.sem(f"weights{q}") for q in range(2)]
        s_xh, s_xc, s_xl, s_wh, s_wc, s_wl = (ph.sem(n) for n in (
            "x_high32_", "x_high_", "x_rest_", "w_high32_", "w_high_", "w_rest_"))
        s_g, s_h, s_m, s_d, s_y = (ph.sem(n) for n in ("gated", "silu", "times", "down", "added"))
        full = F1 // P
        size = [P] * full + [F1 - full * P]

        def load(sp, i, q):
            e = bass.ds(i * 2 + q, 1)
            sp.dma_start(wgu[:, q, 0, :], w_gate[e].rearrange("o d f -> d (o f)")).then_inc(s_w[q], 16)
            sp.dma_start(wgu[:, q, 1, :], w_up[e].rearrange("o d f -> d (o f)")).then_inc(s_w[q], 16)
            sp.dma_start(wd[:, q, 0:full, :],
                         w_down[e, 0:full * P].rearrange("o (k p) n -> p (o k) n", p=P)).then_inc(s_w[q], 16)
            sp.dma_start(wd[0:size[full], q, full, :], w_down[e, full * P:F1].rearrange("o p n -> p (o n)")).then_inc(s_w[q], 16)

        def gate_up(i, u):
            q, b = u // B, u % B
            if b == 0:
                wait(nc.tensor, s_wc, i * 2 + q + 1)
                wait(nc.tensor, s_wl, i * 2 + q + 1)
            if isinstance(i, int) and q == 0:
                wait(nc.tensor, s_xc, b + 1)
                wait(nc.tensor, s_xl, b + 1)
            for k in range(FT):
                m = u * FT + k
                wait(nc.tensor, s_m, i * PER * FT + m - 1)
                for n, bank in enumerate((G, U)):
                    for p, (ww, xx) in enumerate(((wH, xH), (wH, xL), (wL, xH))):
                        last = nc.tensor.matmul(bank[m % 2][0:size[k], :], ww[:, q, n, k * P:k * P + size[k]],
                                                xx[:, b * T:(b + 1) * T], start=(p == 0), stop=(p == 2))
                last.then_inc(s_g, 1)

        def down(i, u):
            q = u // B
            wait(nc.tensor, s_m, (i * PER + u + 1) * FT)
            wait(nc.tensor, s_y, i * PER + u - 1)
            for n in range(NB):
                for k in range(FT):
                    last = nc.tensor.matmul(Y[u % 2][:, n, :], hu[0:size[k], u % 2, k, n * P:(n + 1) * P],
                                            wd[0:size[k], q, k, :], start=(k == 0), stop=(k == FT - 1))
            last.then_inc(s_d, 1)

        def high(dst, src):
            return nc.vector.tensor_scalar(dst.bitcast(I32), src.bitcast(I32), -4096, None, ALU.bitwise_and)

        def split_high(i, u):
            q, b = u // B, u % B
            if b == 0:
                wait(nc.vector, s_w[q], (i + 1) * 64)
                wait(nc.vector, s_d, (i * 2 + q - 1) * B)
                high(w32[:, q, :, :], wgu[:, q, :, :]).then_inc(s_wh, 1)

        def split_rest(i, u):
            q, b = u // B, u % B
            if b == 0:
                wait(nc.gpsimd, s_wh, i * 2 + q + 1)
                nc.gpsimd.tensor_tensor(wL[:, q, :, :], wgu[:, q, :, :], w32[:, q, :, :],
                                        ALU.subtract).then_inc(s_wl, 1)

        def keep_high(i, u):
            q, b = u // B, u % B
            if b == 0:
                wait(nc.scalar, s_wh, i * 2 + q + 1)
                nc.scalar.activation(wH[:, q, :, :], w32[:, q, :, :], ACT.Copy).then_inc(s_wc, 1)

        def silu(i, u):
            for k in range(FT):
                m = u * FT + k
                wait(nc.scalar, s_g, i * PER * FT + m + 1)
                wait(nc.scalar, s_m, i * PER * FT + m - 1)
                nc.scalar.activation(h[0:size[k], m % 2, :], G[m % 2][0:size[k], :], ACT.Silu).then_inc(s_h, 1)

        def times(i, u):
            wait(nc.vector, s_d, i * PER + u - 1)
            for k in range(FT):
                m = u * FT + k
                wait(nc.vector, s_h, i * PER * FT + m + 1)
                nc.vector.tensor_tensor(hu[0:size[k], u % 2, k, :], U[m % 2][0:size[k], :], h[0:size[k], m % 2, :],
                                        ALU.mult).then_inc(s_m, 1)

        def add(i, u):
            q, b = u // B, u % B
            wait(nc.vector, s_d, i * PER + u + 1)
            wait(nc.vector, s_y, i * PER + u - B + 1)
            for n in range(NB):
                t = b * NB + n
                last = nc.vector.scalar_tensor_tensor(out=x_nat[:, t, :], in0=Y[u % 2][:, n, :],
                                                      scalar=combine[:, t, bass.ds(i * 2 + q, 1)], in1=x_nat[:, t, :],
                                                      op0=ALU.mult, op1=ALU.add)
            last.then_inc(s_y, 1)

        with nc.Block() as block:
            @block.sync
            def _(sp):
                for q in range(2):
                    load(sp, 0, q)
                with sp.Fori(1, E1 // 2) as i:
                    for q in range(2):
                        sp.wait_ge(s_d, i * PER + (q - 1) * B)
                        load(sp, i, q)

            @block.tensor
            def _(pe):
                pipeline(pe, [(gate_up, L_G), (down, L_D)], PER, E1 // 2)

            @block.scalar
            def _(a):
                for b in range(B):
                    at = slice(b * T, (b + 1) * T)
                    a.wait_ge(s_xh, b + 1)
                    nc.scalar.activation(xH[:, at], x32[:, at], ACT.Copy).then_inc(s_xc, 1)
                pipeline(a, [(keep_high, 0), (silu, L_G)], PER, E1 // 2)

            @block.vector
            def _(v):
                for b in range(B):
                    at = slice(b * T, (b + 1) * T)
                    high(x32[:, at], xT[:, at]).then_inc(s_xh, 1)
                pipeline(v, [(split_high, 0), (times, L_G), (add, L_D)], PER, E1 // 2)

            @block.gpsimd
            def _(g):
                for b in range(B):
                    at = slice(b * T, (b + 1) * T)
                    g.wait_ge(s_xh, b + 1)
                    nc.gpsimd.tensor_tensor(xL[:, at], xT[:, at], x32[:, at], ALU.subtract).then_inc(s_xl, 1)
                pipeline(g, [(split_rest, 0)], PER, E1 // 2)


def build(nc, a, out, stop=99):
    with ExitStack() as top:
        def sb(name, shape, dt=F32):
            return top.enter_context(nc.sbuf_tensor(name, shape, dt))

        x_nat, xT = sb("x_nat", [P, NT, D]), sb("xT", [P, B * T])
        ident, ones = sb("ident", [P, P]), sb("ones", [P, P])
        epsc, mask = sb("epsc", [P, 1]), sb("mask", [P, HG])
        bqkv = sb("bqkv", [P, 3 * H0])
        b1 = sb("b1", [P, 2])
        bgT, buT = sb("bgT", [P, E0 * F0 // P]), sb("buT", [P, E0 * F0 // P])
        combine = sb("combine", [P, NT, E1])

        sems = {n: Counted(top.enter_context(nc.semaphore(n))) for n in (
            "turned", "turn_copied", "stats", "mean_var", "std", "rstd", "normed", "gained", "shifted", "scaled", "out")}

        wq, wd, wu, bu = sb("wq", [P, D]), sb("wd", [P, LAT]), sb("wu", [LAT, 2 * D]), sb("bu", [P, 2 * D])
        cos, sin = sb("cos", [P, NB, HD1 // 2]), sb("sin", [P, NB, HD1 // 2])
        gw, num = sb("gw", [P, E1]), sb("num", [P, E1])

        s_w, s_wo, s_own, s_1 = (top.enter_context(nc.semaphore(n)) for n in ("w_qkv_in", "w_out_in", "own_in", "small_1"))
        early = top.enter_context(ExitStack())

        def sb1(name, shape):
            return early.enter_context(nc.sbuf_tensor(name, shape, F32))

        rows, sc, se, seT = sb1("rows", [P, 4, D]), sb1("sc", [P, 1]), sb1("se", [P, ST, D]), sb1("seT", [P, ST * P])
        with ExitStack() as first:
            def sb0(name, shape):
                return first.enter_context(nc.sbuf_tensor(name, shape, F32))

            w = sb0("w_qkv", [P, 3, H0 // 2, 2, HD0])
            posT, wo, bo = sb0("posT", [P, T]), sb0("wo0", [P, H0 // 2, D]), sb0("bo0", [P, D])
            posb = sb0("posb", [P, 2, 4, T])
            QKV = [sb0(n, [P, 2, P, H0]) for n in ("q_cols", "k_cols", "v_cols")]
            b_qkv = a["L0_attn_b_qkv"].rearrange("(h c d) -> c h d", c=3, d=HD0)
            preamble(nc, a, sems, x_nat, xT, ident, mask, ones, epsc, [
                ([(c * H0, half * HD0, b_qkv[c]) for c in range(3) for half in range(2)], 3 * H0, P, bqkv),
                ([(0, 0, a["L0_ffn_bg"].rearrange("e (k p) -> (e k) p", p=P))], E0 * F0 // P, P, bgT),
                ([(0, 0, a["L0_ffn_bu"].rearrange("e (k p) -> (e k) p", p=P))], E0 * F0 // P, P, buT),
                ([(0, 0, a["L1_attn_bq"][None, :])], 1, P, b1[:, 0:1]),
                ([(0, 0, a["L1_attn_bkv_down"][None, :])], 1, LAT, b1[:, 1:2]),
            ], rows, sc, se, seT, w, posT, posb, wo, bo, QKV, (
                (wq[:, :], a["L1_attn_Wq"]), (wd[:, :], a["L1_attn_Wkv_down"]), (wu[:, :], a["L1_attn_Wkv_up"]),
                (bu[:, :], a["L1_attn_bkv_up"][None, :].broadcast_to([P, 2 * D])),
                (cos[:, :, :], a["cos"]), (sin[:, :, :], a["sin"]),
                (gw[:, :], a["L1_ffn_gate_w"]), (num[:, :], a["numbers"])), s_w, s_wo, s_own, s_1)
            if stop >= 1:
                attention0(nc, x_nat, xT, ident, w, bqkv, wo, posb, QKV, s_w, s_wo, s_own)
                norm_rows(nc, "n0", sems, x_nat, x_nat, NT, epsc)
        if stop >= 2:
            with ExitStack() as mid:
                def sb2(name, shape, dt=F32):
                    return mid.enter_context(nc.sbuf_tensor(name, shape, dt))

                xn, xnT = sb2("xn", [P, NT, D]), sb2("xnT", [P, B * T])
                slotsT, eout = sb2("slotsT", [P, B, ST * P]), sb2("eout", [P, ST, B, D])
                norm_rows(nc, "n1", sems, x_nat, xn, NT, epsc, rows[:, 0, :], rows[:, 1, :])
                transpose_tokens(nc, "t1", sems, xn, xnT, ident)
                dispatch0(nc, xn, xnT, seT, slotsT, ident)
                experts0(nc, ident, slotsT, eout, bgT, buT, a["L0_ffn_Wg"], a["L0_ffn_Wu"], a["L0_ffn_Wd"], a["L0_ffn_bd"])
                combine0(nc, x_nat, xnT, seT, eout, ident)
            early.close()
            norm_rows(nc, "n3", sems, x_nat, x_nat, NT, epsc)
        if stop >= 3:
            transpose_tokens(nc, "t3", sems, x_nat, xT, ident)
            with ExitStack() as mid:
                def sb3(name, shape, dt=F32):
                    return mid.enter_context(nc.sbuf_tensor(name, shape, dt))

                qsT, ksT = sb3("qsT", [P, G1, B * T], F32R), sb3("ksT", [P, G1, B * T], F32R)
                vN, infT = sb3("vN", [P, NT, D]), sb3("infT", [P, B * T])
                bias = sb3("bias", [P, NB, T])
                s_bias = mid.enter_context(nc.semaphore("att_bias_in"))
                with nc.Block() as block:
                    @block.sync
                    def _(sp):
                        sp.dma_start(bias[:, :, :], a["att_bias"]).then_inc(s_bias, 16)
                prepare1(nc, xT, ident, qsT, ksT, vN, infT, b1, ones, wq, wd, wu, bu, cos, sin, s_1)
                attention1(nc, x_nat, xT, qsT, ksT, vN, infT, mask, ident, bias, a["L1_attn_Wo"], a["L1_attn_bo"], s_bias)
            norm_rows(nc, "n4", sems, x_nat, x_nat, NT, epsc)
        if stop >= 4:
            transpose_tokens(nc, "t4", sems, x_nat, xT, ident)
            gates1(nc, xT, combine, gw, num, s_1)
            experts1(nc, x_nat, xT, combine, a["L1_ffn_w_gate"], a["L1_ffn_w_up"], a["L1_ffn_w_down"])
        norm_rows(nc, "n5", sems, x_nat, x_nat, NT, epsc, out=out)


_OUTS = [((B, T, D), "float32")]


def _constants():
    f = np.float32
    pos = np.arange(T, dtype=f)[:, None]
    div = np.exp(np.arange(0, HD0, 2, dtype=f) * f(-(np.log(10000.0) / HD0))).astype(f)
    ang = (pos * div).astype(f)
    pe = np.zeros((T, HD0), f)
    pe[:, 0::2], pe[:, 1::2] = np.sin(ang), np.cos(ang)
    own = np.repeat(np.tile(np.eye(GT, dtype=f), (1, GC)), H0, axis=1)
    inv = (f(1.0) / np.power(f(10000.0), np.arange(0, HD1, 2, dtype=f) / f(HD1))).astype(f)
    fr = np.outer(np.arange(T, dtype=f), inv).astype(f)
    by_block = lambda t: np.ascontiguousarray(t.reshape(NB, P, -1).transpose(1, 0, 2))
    idx = np.arange(T, dtype=f)
    dist = idx[:, None] - idx[None, :]
    decay = np.exp(-np.maximum(dist, f(0.0)) * f(0.01)).astype(f)
    bias = (f(-0.1) * np.log(np.abs(dist) + f(1.0)) + np.log(decay + f(1e-9))).astype(f)
    return {
        "ident": np.eye(P, dtype=f),
        "mask": np.kron(np.eye(HG, dtype=f), np.ones((RS, 1), f)),
        "own": np.stack([own, f(NOT_OWN) * (f(1.0) - own)]),
        "posT": np.ascontiguousarray(np.concatenate([pe.T, pe.T])),
        "cos": by_block(np.cos(fr).astype(f)), "sin": by_block(np.sin(fr).astype(f)),
        "att_bias": by_block(-bias),
        "numbers": np.tile(np.arange(E1, dtype=f), (P, 1)),
    }


def kernel(**inputs):
    import concourse.bacc as _bacc
    from concourse.bass_utils import run_bass_kernel_spmd as _run

    nc = _bacc.Bacc("TRN2", target_bir_lowering=False, num_devices=1)
    arrays, args = {}, {}
    for name, value in (*inputs.items(), *_constants().items()):
        value = np.ascontiguousarray(value)
        arrays[f"in_{name}_dram"] = value
        args[name] = nc.dram_tensor(f"in_{name}_dram", value.shape, mybir.dt.from_np(value.dtype), kind="ExternalInput").ap()
    outs = [nc.dram_tensor(f"out_{i}_dram", shape, mybir.dt.from_np(np.dtype(dtype)), kind="ExternalOutput").ap()
            for i, (shape, dtype) in enumerate(_OUTS)]
    build(nc, args, outs[0])
    r = _run(nc, [arrays], core_ids=[0])
    return r.results[0]["out_0_dram"]
```

```python
import numpy as np
from contextlib import ExitStack

import concourse.bass as bass
from concourse import mybir

F32 = mybir.dt.float32
F32R = mybir.dt.float32r
I32 = mybir.dt.int32
U32 = mybir.dt.uint32
ALU = mybir.AluOpType
ACT = mybir.ActivationFunctionType
AX = mybir.AxisListType

P = 128
B, T, D = 4, 512, 128
NB = T // P
NT = B * NB
H0, HD0 = 16, 64
E0, S0, F0 = 16, 64, 256
ST = E0 * S0 // P
H1, HD1, LAT = 16, 8, 32
G1 = 4
HG = H1 // G1
E1, F1 = 8, 352
FT = (F1 + P - 1) // P
EPS = 1e-5
SMALL1 = 9


def wait(eng, sem, value):
    if not isinstance(value, int) or value > 0:
        eng.wait_ge(sem, value)


class Counted:

    def __init__(self, sem):
        self.sem, self.base = sem, 0

    def wait(self, eng, n):
        if n > 0:
            eng.wait_ge(self.sem, self.base + n)

    def done(self, n):
        self.base += n


class Phase:

    def __init__(self, nc, tag):
        self.nc, self.tag, self.stack = nc, tag, ExitStack()

    def sb(self, name, shape, dt=F32):
        return self.stack.enter_context(self.nc.sbuf_tensor(f"{self.tag}_{name}", shape, dt))

    def ps(self, name, shape, dt=F32):
        return self.stack.enter_context(self.nc.psum_tensor(f"{self.tag}_{name}", shape, dt))

    def sem(self, name):
        return self.stack.enter_context(self.nc.semaphore(f"{self.tag}_{name}"))

    def __enter__(self):
        return self

    def __exit__(self, *a):
        return self.stack.__exit__(*a)


def pipeline(eng, stages, per, iters):
    for u in range(per):
        for stage, lag in stages:
            if u >= lag:
                stage(0, u - lag)
    with eng.Fori(1, iters) as i:
        for u in range(per):
            for stage, lag in stages:
                stage(i if u >= lag else i - 1, (u - lag) % per)
    for u in range(max(lag for _, lag in stages)):
        for stage, lag in stages:
            if u < lag:
                stage(iters - 1, per + u - lag)


class Norm:

    def __init__(self, nc, ph, sems, src, dst, tiles, epsc, gain=None, shift=None, scale=None):
        self.nc, self.sems, self.src, self.dst, self.tiles, self.epsc = nc, sems, src, dst, tiles, epsc
        self.gain, self.shift, self.scale = gain, shift, scale
        self.stats, self.mv = ph.sb(f"stats{tiles}", [P, tiles, 6]), ph.sb(f"mv{tiles}", [P, tiles, 2])
        self.std, self.rstd = ph.sb(f"std{tiles}", [P, tiles]), ph.sb(f"rstd{tiles}", [P, tiles])
        self.off = ph.sb(f"off{tiles}", [P, tiles])
        self.quads = tiles // 4

    def vector(self, v):
        nc, sems, src, dst, tiles, stats, mv = self.nc, self.sems, self.src, self.dst, self.tiles, self.stats, self.mv
        for t in range(tiles):
            nc.vector.bn_stats(stats[:, t, :], src[:, t, :]).then_inc(sems["stats"].sem, 1)
        for t in range(tiles):
            sems["stats"].wait(v, t + 1)
            nc.vector.bn_aggr(mv[:, t, :], stats[:, t, :]).then_inc(sems["mean_var"].sem, 1)
        sems["std"].wait(v, 1)
        nc.vector.reciprocal(self.rstd[:, :], self.std[:, :]).then_inc(sems["rstd"].sem, 1)
        sems["rstd"].wait(v, 1)
        nc.vector.scalar_tensor_tensor(out=self.off[:, :], in0=mv[:, :, 0], scalar=-1.0, in1=self.rstd[:, :],
                                       op0=ALU.mult, op1=ALU.mult).then_inc(sems["off"].sem, 1)
        for q in range(self.quads):
            for t in (4 * q, 4 * q + 1):
                last = nc.vector.tensor_scalar(dst[:, t, :], src[:, t, :], mv[:, t, 0:1], self.rstd[:, t:t + 1],
                                               ALU.subtract, ALU.mult)
            last.then_inc(sems["normed_v"].sem, 1)
            if self.gain is not None and q:
                self.affine(v, q - 1)
        if self.gain is not None:
            self.affine(v, self.quads - 1)

    def affine(self, v, q):
        nc, sems, wide = self.nc, self.sems, [P, 4, D]
        d = self.dst[:, 4 * q:4 * q + 4, :]
        sems["normed_v"].wait(v, q + 1)
        sems["normed_a"].wait(v, q + 1)
        nc.vector.tensor_tensor(d, d, self.gain.unsqueeze(1).broadcast_to(wide), ALU.mult).then_inc(sems["gained"].sem, 1)
        sems["gained"].wait(v, q + 1)
        nc.vector.tensor_tensor(d, d, self.shift.unsqueeze(1).broadcast_to(wide), ALU.add).then_inc(sems["shifted"].sem, 1)
        if self.scale is not None:
            sems["shifted"].wait(v, q + 1)
            nc.vector.tensor_scalar(d, d, self.scale[:, 0:1], None, ALU.mult).then_inc(sems["scaled"].sem, 1)

    def ready(self, eng, q):
        if self.scale is not None:
            self.sems["scaled"].wait(eng, q + 1)
        elif self.gain is not None:
            self.sems["shifted"].wait(eng, q + 1)
        else:
            self.sems["normed_v"].wait(eng, q + 1)
            self.sems["normed_a"].wait(eng, q + 1)

    def scalar(self, a, between=None):
        nc, sems = self.nc, self.sems
        sems["mean_var"].wait(a, self.tiles)
        nc.scalar.activation(self.std[:, :], self.mv[:, :, 1], ACT.Sqrt, bias=self.epsc[:, 0:1]).then_inc(sems["std"].sem, 1)
        sems["off"].wait(a, 1)
        for q in range(self.quads):
            for t in (4 * q + 2, 4 * q + 3):
                last = nc.scalar.activation(self.dst[:, t, :], self.src[:, t, :], ACT.Identity,
                                            bias=self.off[:, t:t + 1], scale=self.rstd[:, t:t + 1])
            last.then_inc(sems["normed_a"].sem, 1)
            if between is not None and q:
                between(a, q - 1)
        if between is not None:
            between(a, self.quads - 1)

    def done(self):
        for n, count in (("stats", self.tiles), ("mean_var", self.tiles), ("std", 1), ("rstd", 1), ("off", 1),
                         ("normed_v", self.quads), ("normed_a", self.quads),
                         ("gained", self.quads * (self.gain is not None)), ("shifted", self.quads * (self.gain is not None)),
                         ("scaled", self.quads * (self.scale is not None))):
            self.sems[n].done(count)


def norm_rows(nc, tag, sems, src, dst, epsc, gain=None, shift=None, turned=None, ident=None, out=None, loads=None):
    with Phase(nc, tag) as ph:
        norm = Norm(nc, ph, sems, src, dst, NT, epsc, gain, shift)
        pt = [ph.ps(f"pt{k}", [P, T]) for k in range(B)]
        s_t, s_c, s_out = sems["turned"], sems["turn_copied"], sems["out"]

        def copy_turned(a, b):
            s_t.wait(a, b + 1)
            nc.scalar.activation(turned[:, b * T:(b + 1) * T], pt[b][:, :], ACT.Copy).then_inc(s_c.sem, 1)

        with nc.Block() as block:
            @block.vector
            def _(v):
                norm.vector(v)

            @block.scalar
            def _(a):
                norm.scalar(a, copy_turned if turned is not None else None)

            if turned is not None:
                @block.tensor
                def _(pe):
                    for b in range(B):
                        norm.ready(pe, b)
                        for n in range(NB):
                            last = nc.tensor.transpose(pt[b][:, n * P:(n + 1) * P], dst[:, b * NB + n, :], ident[:, :])
                        last.then_inc(s_t.sem, 1)

            if loads is not None:
                @block.sync
                def _(sp):
                    loads(sp)

            if out is not None:
                @block.sync
                def _(sp):
                    for b in range(B):
                        norm.ready(sp, b)
                        sp.dma_start(out[b].rearrange("(n p) d -> p n d", p=P),
                                     dst[:, b * NB:(b + 1) * NB, :]).then_inc(s_out.sem, 16)
                    s_out.wait(sp, 16 * B)
    norm.done()
    if turned is not None:
        s_t.done(B)
        s_c.done(B)


def preamble(nc, a, sems, x_nat, xT, ident, mask, ones, epsc, jobs, rows, sc, se, seT, w, posT, posb, wo, bo, QKV, small,
             s_w, s_wo, s_own, s_1):
    with Phase(nc, "pre") as ph:
        rows_in = [ph.sb(f"rows{k}", [P, P]) for k in range(len(jobs))]
        XT = [ph.ps(f"xt{k}", [P, T]) for k in range(NB)]
        CT = [ph.ps(f"ct{k}", [P, P]) for k in range(2)]
        s_id, s_x, s_rows, s_f, s_t, s_c, s_ct, s_cc, s_set, s_b8, s_z, s_pb, s_st, s_sc, s_pos = (ph.sem(n) for n in (
            "ident_in", "x_in", "rows_in_", "slots_in", "turned", "copied", "columns_", "columns_out", "set", "scaled",
            "zeros", "posb_", "slots_turned", "slots_out", "positions"))
        norm = Norm(nc, ph, sems, se, se, ST, epsc, rows[:, 2, :], rows[:, 3, :], sc)

        def key_rows(e, half):
            part = slice(half * HD0, (half + 1) * HD0)
            for k in range(2):
                h = H0 + 8 * k + 4 * half
                e.tensor_tensor(posb[part, k, :, :], posT[part, None, :].broadcast_to([HD0, 4, T]),
                                jobs[0][3][part, h:h + 4].unsqueeze(2).broadcast_to([HD0, 4, T]), ALU.add).then_inc(s_pb, 1)

        with nc.Block() as block:
            @block.sync
            def _(sp):
                sp.dma_start(ident[:, :], a["ident"]).then_inc(s_id, 16)
                for b in range(B):
                    sp.dma_start(x_nat[:, b * NB:(b + 1) * NB, :],
                                 a["L0_attn_x"][b].rearrange("(n p) d -> p n d", p=P)).then_inc(s_x, 16)
                sp.dma_start(posT[:, :], a["posT"]).then_inc(s_pos, 16)
                sp.dma_start(bo[:, :], a["L0_attn_b_out"][None, :].broadcast_to([P, D])).then_inc(s_pos, 16)
                w_c = a["L0_attn_w_qkv"].rearrange("p (h c d) -> p c h d", h=H0, c=3)
                for c in range(3):
                    for k in range(2):
                        for half in range(2):
                            h = 8 * k + 4 * half
                            sp.dma_start(w[:, c, 4 * k:4 * k + 4, half, :], w_c[:, c, h:h + 4, :]).then_inc(s_w, 16)
                sp.dma_start(wo[:, :, :], a["L0_attn_w_out"].rearrange("(k p) n -> p k n", p=P)).then_inc(s_wo, 16)
                sp.wait_ge(s_z, 2)
                for t in range(2):
                    for par in range(2):
                        sp.dma_start(QKV[t][HD0:HD0 + GT, par, :, :].rearrange("p t h -> p (t h)"), a["own"][t]).then_inc(s_own, 16)

            @block.scalar
            def _(act):
                for k, (parts, r, n, dst) in enumerate(jobs):
                    for r0, c0, src in parts:
                        act.dma_start(rows_in[k][r0:r0 + src.shape[0], c0:c0 + src.shape[1]], src).then_inc(s_rows, 16)
                act.dma_start(se[:, :, :], a["L0_ffn_slot_embeds"].rearrange("(t q) s d -> (q s) t d", q=2)).then_inc(s_f, 16)
                act.dma_start(sc[:, :], a["L0_ffn_scale"][None, :].broadcast_to([P, 1])).then_inc(s_f, 16)
                for k, n in enumerate(("norm_g", "norm_b", "slot_g", "slot_b")):
                    act.dma_start(rows[:, k, :], a["L0_ffn_" + n][None, :].broadcast_to([P, D])).then_inc(s_f, 16)
                norm.scalar(act)
                act.dma_start(mask[:, :], a["mask"]).then_inc(s_1, 16)
                for dst, src in small:
                    act.dma_start(dst, src).then_inc(s_1, 16)

            @block.gpsimd
            def _(g):
                for t in QKV[0:2]:
                    nc.gpsimd.memset(t[HD0:P, :, :, :], 0.0).then_inc(s_z, 1)
                g.wait_ge(s_pos, 32)
                g.wait_ge(s_cc, 1)
                key_rows(nc.gpsimd, 1)

            @block.tensor
            def _(pe):
                pe.wait_ge(s_id, 16)
                pe.wait_ge(s_x, 16 * B)
                for b in range(B):
                    for n in range(NB):
                        last = nc.tensor.transpose(XT[b][:, n * P:(n + 1) * P], x_nat[:, b * NB + n, :], ident[:, :])
                    last.then_inc(s_t, 1)
                pe.wait_ge(s_rows, 16 * sum(len(j[0]) for j in jobs))
                for k, (parts, r, n, dst) in enumerate(jobs):
                    wait(pe, s_cc, k - 1)
                    nc.tensor.transpose(CT[k % 2][0:n, 0:r], rows_in[k][0:r, 0:n], ident[0:r, 0:r]).then_inc(s_ct, 1)
                for b in range(ST // NB):
                    norm.ready(pe, b)
                    for n in range(NB):
                        last = nc.tensor.transpose(XT[b][:, n * P:(n + 1) * P], se[:, b * NB + n, :], ident[:, :])
                    last.then_inc(s_st, 1)

            @block.vector
            def _(v):
                nc.vector.memset(ones[:, :], 1.0 / T).then_inc(s_set, 1)
                nc.vector.memset(epsc[:, :], EPS).then_inc(s_set, 1)
                for b in range(B):
                    v.wait_ge(s_t, b + 1)
                    nc.vector.tensor_copy(xT[:, b * T:(b + 1) * T], XT[b][:, :]).then_inc(s_c, 1)
                for k, (parts, r, n, dst) in enumerate(jobs):
                    v.wait_ge(s_ct, k + 1)
                    nc.vector.tensor_copy(dst[0:n, 0:r], CT[k % 2][0:n, 0:r]).then_inc(s_cc, 1)
                bias = jobs[0][3]
                v.wait_ge(s_cc, 1)
                nc.vector.tensor_scalar(bias[:, 0:H0], bias[:, 0:H0], HD0 ** -0.5, None, ALU.mult).then_inc(s_b8, 1)
                v.wait_ge(s_pos, 32)
                key_rows(nc.vector, 0)
                nc.vector.tensor_tensor(x_nat[:, :, :], x_nat[:, :, :], bo[:, None, :].broadcast_to([P, NT, D]), ALU.add)
                v.wait_ge(s_f, 96)
                norm.vector(v)
                for b in range(ST // NB):
                    v.wait_ge(s_st, b + 1)
                    nc.vector.tensor_copy(seT[:, b * T:(b + 1) * T], XT[b][:, :]).then_inc(s_sc, 1)
    norm.done()


GT = P // H0
GC = P // GT
NOT_OWN = -2.0 ** 100


def attention0(nc, x_nat, xT, ident, w, bias, wo, posb, QKV, s_w, s_wo, s_own):
    SL = 4 * NB
    L_S, L_R, L_T, L_PV, L_O, L_Y = 4, 5, 6, 7, 8, 9
    with Phase(nc, "a0") as ph:
        V = ph.sb("vrows", [P, 8, 4, HD0])
        PR = ph.sb("probs", [P, 4, 4, P])
        PT = ph.sb("probsT", [P, 2, 4, P])
        OT = ph.sb("oT", [P, 2, P, H0 // 2])
        nmax, sums, rsum = (ph.sb(n, [P, 4, 4]) for n in ("nmax", "sums", "rsum"))
        PJ = [ph.ps(f"proj{k}", [P, 4, P]) for k in range(2)]
        SC = [ph.ps(f"scores{k}", [P, 4, P]) for k in range(2)]
        TB, Y = ph.ps("turned", [P, 4, P]), ph.ps("y", [P, 4, P])
        VB, OB = ph.ps("vturned", [P, 2, P]), ph.ps("outT", [P, 2, P])
        s_pj, s_pe, s_S, s_mx, s_e, s_r, s_n = (ph.sem(n) for n in ("projected", "proj_in", "scored", "maxed", "exped", "recip", "normed"))
        s_vt, s_vc, s_T, s_tc, s_pv, s_oa, s_od, s_y, s_x = (
            ph.sem(n) for n in ("vturned_", "v_in", "turned_", "copied", "pv", "o_a", "o_d", "y_", "x"))

        def project(i, u):
            q, s = u // 4, u % 4
            if s == 3:
                return
            for k in range(2):
                m = 6 * q + 2 * s + k
                wait(nc.tensor, s_pe, i * 24 + m - 1)
                for j in range(4):
                    last = nc.tensor.matmul(PJ[k][:, j, :], w[:, s, 4 * k + j, :, :].rearrange("p h d -> p (h d)"),
                                            xT[:, bass.ds(i * T + q * P, P)], start=True, stop=True)
                last.then_inc(s_pj, 1)

        def group(t, u, n):
            q, s = u // 4, u % 4
            at = (4 * s + n) * GT
            return t[:, q % 2, at:at + GT, :].rearrange("p t h -> p (t h)")

        def turn_v(i, u):
            q, s = u // 4, u % 4
            if s == 0:
                wait(nc.tensor, s_pe, i * 24 + 6 * q + 6)
            wait(nc.tensor, s_vc, i * SL + u)
            for n in range(2):
                at = (2 * s + n) * GT
                last = nc.tensor.transpose(VB[:, n, :], QKV[2][:, q % 2, at:at + GT, :].rearrange("p t h -> p (t h)"), ident[:, :])
            last.then_inc(s_vt, 1)

        def scores(i, u):
            wait(nc.tensor, s_e, i * SL + u - 1)
            for n in range(4):
                last = nc.tensor.matmul(SC[u % 2][:, n, :], group(QKV[0], u, n), group(QKV[1], u, n), start=True, stop=True)
            last.then_inc(s_S, 1)

        def turn(i, u):
            wait(nc.tensor, s_n, i * SL + u + 1)
            wait(nc.tensor, s_tc, i * SL + u)
            for n in range(4):
                last = nc.tensor.transpose(TB[:, n, :], PR[:, u % 4, n, :], ident[:, :])
            last.then_inc(s_T, 1)

        def pv(i, u):
            wait(nc.tensor, s_tc, i * SL + u + 1)
            wait(nc.tensor, s_vc, i * SL + u + 1)
            wait(nc.tensor, s_oa, i * SL + u)
            wait(nc.tensor, s_od, i * SL + u)
            for n in range(4):
                last = nc.tensor.matmul(OB[n % 2 * HD0:(n % 2 + 1) * HD0, n // 2, :], V[:, u % 8, n, :], PT[:, u % 2, n, :],
                                        start=True, stop=True)
            last.then_inc(s_pv, 1)

        def out_proj(i, u):
            q, s = u // 4, u % 4
            if s < 3:
                return
            wait(nc.tensor, s_oa, i * SL + u + 1)
            wait(nc.tensor, s_od, i * SL + u + 1)
            wait(nc.tensor, s_x, i * NB + q)
            for m in range(H0 // 2):
                last = nc.tensor.matmul(Y[:, 0, :], OT[:, q % 2, :, m], wo[:, m, :], start=(m == 0), stop=(m == H0 // 2 - 1))
            last.then_inc(s_y, 1)

        def proj_in(i, u):
            q, s = u // 4, u % 4
            if s == 3:
                return
            n = i * SL + 4 * q - 4
            wait(nc.vector, s_vt if s == 2 else s_S, n)
            for k in range(2):
                wait(nc.vector, s_pj, i * 24 + 6 * q + 2 * s + k + 1)
                for half in range(2):
                    rows = slice(half * HD0, (half + 1) * HD0)
                    h = 8 * k + 4 * half
                    b4 = bias[rows, s * H0 + h:s * H0 + h + 4].unsqueeze(2)
                    if s == 2:
                        wide = [HD0, 4, P // (2 * GT), GT]
                        for e in range(2):
                            src = PJ[k][rows, :, :].rearrange("p h (m e t) -> p h m e t", e=2, t=GT)[:, :, :, e, :]
                            out = QKV[2][e * HD0:(e + 1) * HD0, q % 2, :, h:h + 4].rearrange("p (m t) h -> p h m t", t=GT)
                            last = nc.vector.tensor_tensor(out, src, b4.unsqueeze(3).broadcast_to(wide), ALU.add)
                        continue
                    out = QKV[s][0:HD0, q % 2, :, h:h + 4].rearrange("p t h -> p h t")
                    if s == 1:
                        last = nc.vector.tensor_tensor(out, PJ[k][rows, :, :], posb[rows, k, :, q * P:(q + 1) * P], ALU.add)
                    else:
                        last = nc.vector.scalar_tensor_tensor(out=out, in0=PJ[k][rows, :, :], scalar=HD0 ** -0.5,
                                                              in1=b4.broadcast_to([HD0, 4, P]), op0=ALU.mult, op1=ALU.add)
                last.then_inc(s_pe, 1)

        def neg_max(i, u):
            wait(nc.vector, s_S, i * SL + u + 1)
            wait(nc.vector, s_e, i * SL + u - 3)
            nc.vector.tensor_reduce(nmax[:, u % 4, :], SC[u % 2][:, :, :], AX.X, ALU.max, negate=True).then_inc(s_mx, 1)

        def recip(i, u):
            wait(nc.vector, s_e, i * SL + u + 1)
            wait(nc.vector, s_n, i * SL + u - 3)
            nc.vector.reciprocal(rsum[:, u % 4, :], sums[:, u % 4, :]).then_inc(s_r, 1)

        def o_rows(u, par):
            q, s = u // 4, u % 4
            for e in range(2):
                at = OT[par * HD0:(par + 1) * HD0, q % 2, 4 * s * GT:(4 * s + 4) * GT, :]
                yield (at.rearrange("p (n e t) m -> p n e t m", e=2, t=GT)[:, :, e, :, :],
                       OB[e * HD0:(e + 1) * HD0, :, :].rearrange("p n (t m r) -> p n t m r", t=GT, r=2)[:, :, :, :, par])

        def o_free(eng, i, u):
            q, s = u // 4, u % 4
            if s == 0:
                wait(eng, s_y, i * NB + q - 1)

        def o_out_v(i, u):
            wait(nc.vector, s_pv, i * SL + u + 1)
            wait(nc.vector, s_oa, i * SL + u + 1)
            o_free(nc.vector, i, u)
            for dst, src in o_rows(u, 1):
                last = nc.vector.tensor_copy(dst, src)
            last.then_inc(s_od, 1)

        def add(i, u):
            q, s = u // 4, u % 4
            if s < 3:
                return
            wait(nc.vector, s_y, i * NB + q + 1)
            x = x_nat[:, bass.ds(i * NB + q, 1), :].rearrange("p o d -> p (o d)")
            nc.vector.tensor_tensor(x, Y[:, 0, :], x, ALU.add).then_inc(s_x, 1)

        def exps(i, u):
            wait(nc.scalar, s_mx, i * SL + u + 1)
            wait(nc.scalar, s_r, i * SL + u - 3)
            wait(nc.scalar, s_T, i * SL + u - 3)
            for n in range(4):
                last = nc.scalar.activation(PR[:, u % 4, n, :], SC[u % 2][:, n, :], ACT.Exp,
                                            bias=nmax[:, u % 4, n:n + 1], accum_out=sums[:, u % 4, n:n + 1])
            last.then_inc(s_e, 1)

        def v_in(i, u):
            wait(nc.scalar, s_vt, i * SL + u + 1)
            wait(nc.scalar, s_pv, i * SL + u - 7)
            nc.scalar.activation(V[:, u % 8, :, :].rearrange("p n d -> p (n d)"), VB[:, :, :].rearrange("p n c -> p (n c)"), ACT.Copy).then_inc(s_vc, 1)

        def copy_turned(i, u):
            wait(nc.scalar, s_T, i * SL + u + 1)
            wait(nc.scalar, s_pv, i * SL + u - 1)
            nc.scalar.activation(PT[:, u % 2, :, :], TB[:, :, :], ACT.Copy).then_inc(s_tc, 1)

        def o_out_a(i, u):
            wait(nc.scalar, s_pv, i * SL + u + 1)
            o_free(nc.scalar, i, u)
            for dst, src in o_rows(u, 0):
                last = nc.scalar.activation(dst, src, ACT.Copy)
            last.then_inc(s_oa, 1)

        def normalise(i, u):
            wait(nc.gpsimd, s_r, i * SL + u + 1)
            pr = PR[:, u % 4, :, :]
            nc.gpsimd.tensor_tensor(pr, pr, rsum[:, u % 4, :].unsqueeze(2).broadcast_to([P, 4, P]), ALU.mult).then_inc(s_n, 1)

        with nc.Block() as block:
            @block.tensor
            def _(pe):
                pe.wait_ge(s_w, 16 * 12)
                pe.wait_ge(s_own, 16 * 4)
                pe.wait_ge(s_wo, 16)
                pipeline(pe, [(turn_v, L_S), (scores, L_S), (turn, L_T), (project, 0), (pv, L_PV), (out_proj, L_Y)], SL, B)

            @block.vector
            def _(v):
                pipeline(v, [(o_out_v, L_O), (neg_max, L_S), (recip, L_R), (proj_in, 0), (add, L_Y)], SL, B)

            @block.scalar
            def _(a):
                pipeline(a, [(o_out_a, L_O), (v_in, L_S), (copy_turned, L_T), (exps, L_S)], SL, B)

            @block.gpsimd
            def _(g):
                pipeline(g, [(normalise, L_R)], SL, B)


def dispatch0(nc, xn, xnT, seT, LT, slotsT, ident, loads):
    L_T, L_M = 2, 3
    PER = 2 * ST
    with Phase(nc, "d0") as ph:
        xs = ph.sb("xs", [P, 2, NB, D])
        DI = ph.sb("dispatch", [P, 2, T])
        DT = ph.sb("dispatchT", [P, 2, NB, P])
        nmax, sums, rsum = (ph.sb(n, [P, 2, 1]) for n in ("nmax", "sums", "rsum"))
        LG = [ph.ps(f"logits{k}", [P, T]) for k in range(2)]
        TB = [ph.ps(f"turned{k}", [P, NB, P]) for k in range(2)]
        SB_ = [ph.ps(f"slots{k}", [P, T]) for k in range(2)]
        s_xs, s_l, s_mx, s_e, s_r, s_n, s_T, s_t, s_m, s_o, s_k = (
            ph.sem(n) for n in ("xs_in", "logits_", "maxed", "exped", "recip", "normed", "turned_", "copied", "mixed", "out", "kept"))

        def logits(i, u):
            wait(nc.tensor, s_e, i * PER + u - 1)
            wait(nc.tensor, s_k, i * PER + u - 1)
            nc.tensor.matmul(LG[u % 2][:, :], seT[:, u % ST * P:(u % ST + 1) * P], xnT[:, bass.ds((i * 2 + u // ST) * T, T)],
                             start=True, stop=True).then_inc(s_l, 1)

        def turn(i, u):
            wait(nc.tensor, s_n, i * PER + u + 1)
            wait(nc.tensor, s_t, i * PER + u - 1)
            for n in range(NB):
                last = nc.tensor.transpose(TB[u % 2][:, n, :], DI[:, u % 2, n * P:(n + 1) * P], ident[:, :])
            last.then_inc(s_T, 1)

        def mix(i, u):
            wait(nc.tensor, s_t, i * PER + u + 1)
            if u % ST == 0:
                wait(nc.tensor, s_xs, i * 2 + u // ST + 1)
            wait(nc.tensor, s_o, i * PER + u - 1)
            for n in range(NB):
                last = nc.tensor.matmul(SB_[u % 2][:, 0:P], xs[:, u // ST, n, :], DT[:, u % 2, n, :],
                                        start=(n == 0), stop=(n == NB - 1))
            last.then_inc(s_m, 1)

        def neg_max(i, u):
            wait(nc.vector, s_l, i * PER + u + 1)
            wait(nc.vector, s_e, i * PER + u - 1)
            nc.vector.tensor_reduce(nmax[:, u % 2, :], LG[u % 2][:, :], AX.X, ALU.max, negate=True).then_inc(s_mx, 1)

        def recip(i, u):
            wait(nc.vector, s_e, i * PER + u + 1)
            wait(nc.vector, s_n, i * PER + u - 1)
            nc.vector.reciprocal(rsum[:, u % 2, :], sums[:, u % 2, :]).then_inc(s_r, 1)

        def copy_turned(i, u):
            wait(nc.vector, s_T, i * PER + u + 1)
            wait(nc.vector, s_m, i * PER + u - 1)
            nc.vector.tensor_copy(DT[:, u % 2, :, :], TB[u % 2][:, :, :]).then_inc(s_t, 1)

        def exps(i, u):
            wait(nc.scalar, s_mx, i * PER + u + 1)
            wait(nc.scalar, s_r, i * PER + u - 1)
            wait(nc.scalar, s_T, i * PER + u - 1)
            nc.scalar.activation(DI[:, u % 2, :], LG[u % 2][:, :], ACT.Exp, bias=nmax[:, u % 2, :],
                                 accum_out=sums[:, u % 2, :]).then_inc(s_e, 1)

        def keep(i, u):
            wait(nc.scalar, s_mx, i * PER + u + 1)
            nc.scalar.activation(LT[:, bass.ds(i * PER + u, 1), :].rearrange("p o t -> p (o t)"), LG[u % 2][:, :],
                                 ACT.Copy).then_inc(s_k, 1)

        def slots_out(i, u):
            wait(nc.scalar, s_m, i * PER + u + 1)
            nc.scalar.activation(slotsT[:, bass.ds(i * 2 + u // ST, 1), u % ST * P:(u % ST + 1) * P].rearrange("p o s -> p (o s)"),
                                 SB_[u % 2][:, 0:P], ACT.Copy).then_inc(s_o, 1)

        def stage_x(i, u):
            if u % ST == 0:
                wait(nc.gpsimd, s_m, i * PER + u - ST)
                nc.gpsimd.tensor_copy(xs[:, u // ST, :, :], xn[:, bass.ds((i * 2 + u // ST) * NB, NB), :]).then_inc(s_xs, 1)

        def normalise(i, u):
            wait(nc.gpsimd, s_r, i * PER + u + 1)
            nc.gpsimd.tensor_tensor(DI[:, u % 2, :], DI[:, u % 2, :], rsum[:, u % 2, :].broadcast_to([P, T]),
                                    ALU.mult).then_inc(s_n, 1)

        with nc.Block() as block:
            @block.sync
            def _(sp):
                loads(sp)

            @block.tensor
            def _(pe):
                pipeline(pe, [(logits, 0), (turn, L_T), (mix, L_M)], PER, B // 2)

            @block.vector
            def _(v):
                pipeline(v, [(neg_max, 0), (recip, 1), (copy_turned, L_T)], PER, B // 2)

            @block.scalar
            def _(a):
                pipeline(a, [(exps, 0), (keep, 0), (slots_out, L_M)], PER, B // 2)

            @block.gpsimd
            def _(g):
                pipeline(g, [(normalise, 1), (stage_x, 0)], PER, B // 2)


R0 = 4


def load_expert0(sp, bufs, Wg, Wu, Wd, s_w, i, q):
    wg, wu, wd = bufs
    e = i * R0 + q
    sp.dma_start(wg[:, q, :], Wg[bass.ds(e, 1)].rearrange("o d f -> d (o f)")).then_inc(s_w[q], 16)
    sp.dma_start(wu[:, q, :], Wu[bass.ds(e, 1)].rearrange("o d f -> d (o f)")).then_inc(s_w[q], 16)
    sp.dma_start(wd[:, q, :, :], Wd[bass.ds(e, 1)].rearrange("o (k p) n -> p (o k) n", p=P)).then_inc(s_w[q], 16)


def experts0(nc, slotsT, eout, bgT, buT, bufs, bdb, s_w, s_bd, Wg, Wu, Wd):
    R, C = R0, B * S0
    KF = F0 // P
    with Phase(nc, "e0") as ph:
        wg, wu, wd = bufs
        h, hu = ph.sb("h", [P, 2, KF, C]), ph.sb("hu", [P, 2, KF, C])
        G = [ph.ps(f"gate{k}", [P, KF, C]) for k in range(2)]
        U = [ph.ps(f"up{k}", [P, KF, C]) for k in range(2)]
        EO = [ph.ps(f"out{k}", [P, B // 2, D]) for k in range(2)]
        s_g, s_h, s_m, s_d, s_o = (ph.sem(n) for n in ("gated", "gelu", "times", "down", "out_"))

        def gate_up(i, u):
            n = i * R + u
            wait(nc.tensor, s_w[u], (i + 1) * 48)
            wait(nc.tensor, s_m, n - 1)
            for bank, ww in ((G, wg), (U, wu)):
                for k in range(KF):
                    last = nc.tensor.matmul(bank[u % 2][:, k, :].rearrange("p (b s) -> p b s", b=B),
                                            ww[:, u, k * P:(k + 1) * P],
                                            slotsT[:, :, bass.ds(n * S0, S0)], start=True, stop=True)
            last.then_inc(s_g, 1)

        def down(i, u):
            n = i * R + u
            wait(nc.tensor, s_m, n + 1)
            wait(nc.tensor, s_o, n - 1)
            for c in range(B // 2):
                for k in range(KF):
                    for e in range(2):
                        b = 2 * c + e
                        last = nc.tensor.matmul(EO[u % 2][e * S0:(e + 1) * S0, c, :],
                                                hu[:, u % 2, k, b * S0:(b + 1) * S0], wd[:, u, k, :],
                                                start=(k == 0), stop=(k == KF - 1))
            last.then_inc(s_d, 1)

        def gelu(i, u):
            n = i * R + u
            wait(nc.scalar, s_g, n + 1)
            wait(nc.scalar, s_m, n - 1)
            for k in range(KF):
                last = nc.scalar.activation(h[:, u % 2, k, :], G[u % 2][:, k, :], ACT.Gelu,
                                            bias=bgT[:, bass.ds(n * KF + k, 1)])
            last.then_inc(s_h, 1)

        def times(i, u):
            n = i * R + u
            wait(nc.vector, s_h, n + 1)
            wait(nc.vector, s_d, n - 1)
            for k in range(KF):
                last = nc.vector.scalar_tensor_tensor(out=hu[:, u % 2, k, :], in0=U[u % 2][:, k, :],
                                                      scalar=buT[:, bass.ds(n * KF + k, 1)], in1=h[:, u % 2, k, :],
                                                      op0=ALU.add, op1=ALU.mult)
            last.then_inc(s_m, 1)

        def out(i, u):
            n = i * R + u
            wait(nc.vector, s_d, n + 1)
            st = i * (R // 2) + u // 2
            for e in range(2):
                rows = slice(e * S0, (e + 1) * S0)
                dst = eout[u % 2 * S0:(u % 2 + 1) * S0, bass.ds(st, 1), e:B:2, :].rearrange("p o b d -> p (o b) d")
                last = nc.vector.tensor_tensor(dst, EO[u % 2][rows, :, :],
                                               bdb[rows, bass.ds(n, 1), :].broadcast_to([S0, B // 2, D]), ALU.add)
            last.then_inc(s_o, 1)

        with nc.Block() as block:
            @block.sync
            def _(sp):
                with sp.Fori(1, E0 // R) as i:
                    for q in range(R):
                        sp.wait_ge(s_d, i * R + q - R + 1)
                        load_expert0(sp, bufs, Wg, Wu, Wd, s_w, i, q)

            @block.tensor
            def _(pe):
                pipeline(pe, [(gate_up, 0), (down, 1)], R, E0 // R)

            @block.scalar
            def _(a):
                pipeline(a, [(gelu, 0)], R, E0 // R)

            @block.vector
            def _(v):
                v.wait_ge(s_bd, 16)
                pipeline(v, [(times, 0), (out, 1)], R, E0 // R)


def combine0(nc, x_nat, LT, eout, ident):
    L_L, L_T, L_Y = 1, 2, 3
    with Phase(nc, "c0") as ph:
        ls = ph.sb("ls", [P, 2, ST, P])
        CO = ph.sb("combine", [P, 2, ST * P])
        CT = ph.sb("combineT", [P, 2, ST, P])
        nmax = ph.sb("nmax", [P, 2, 1])
        sums, rsum = ph.sb("sums", [P, 4, 1]), ph.sb("rsum", [P, 4, 1])
        LG = [ph.ps(f"logits{k}", [P, ST * P]) for k in range(2)]
        TB = ph.ps("turned", [P, ST, P])
        Y = [ph.ps(f"y{k}", [P, T]) for k in range(2)]
        s_xs, s_l, s_mx, s_e, s_r, s_T, s_ta, s_td, s_y, s_o = (
            ph.sem(n) for n in ("xs_in", "logits_", "maxed", "exped", "recip", "turned_", "copied_a", "copied_d", "mixed", "out"))
        HS = ST // 2

        def logits(b, u):
            wait(nc.tensor, s_xs, b * NB + u + 1)
            wait(nc.tensor, s_e, b * NB + u - 1)
            for k in range(ST):
                last = nc.tensor.transpose(LG[u % 2][:, k * P:(k + 1) * P], ls[:, u % 2, k, :], ident[:, :])
            last.then_inc(s_l, 1)

        def turn(b, u):
            wait(nc.tensor, s_e, b * NB + u + 1)
            wait(nc.tensor, s_ta, b * NB + u)
            wait(nc.tensor, s_td, b * NB + u)
            for k in range(ST):
                last = nc.tensor.transpose(TB[:, k, :], CO[:, u % 2, k * P:(k + 1) * P], ident[:, :])
            last.then_inc(s_T, 1)

        def mix(b, u):
            wait(nc.tensor, s_ta, b * NB + u + 1)
            wait(nc.tensor, s_td, b * NB + u + 1)
            wait(nc.tensor, s_o, b * NB + u - 1)
            for k in range(ST):
                last = nc.tensor.matmul(Y[u % 2][:, 0:D], CT[:, u % 2, k, :],
                                        eout[:, k, bass.ds(b, 1), :].rearrange("p o d -> p (o d)"),
                                        start=(k == 0), stop=(k == ST - 1))
            last.then_inc(s_y, 1)

        def stage(b, u):
            wait(nc.vector, s_l, b * NB + u - 1)
            nc.vector.tensor_scalar(ls[:, u % 2, :, :], LT[:, bass.ds(b * ST, ST), u * P:(u + 1) * P], 1.0, None,
                                    ALU.mult).then_inc(s_xs, 1)

        def neg_max(b, u):
            wait(nc.vector, s_l, b * NB + u + 1)
            wait(nc.vector, s_e, b * NB + u - 1)
            nc.vector.tensor_reduce(nmax[:, u % 2, :], LG[u % 2][:, :], AX.X, ALU.max, negate=True).then_inc(s_mx, 1)

        def recip(b, u):
            wait(nc.vector, s_e, b * NB + u + 1)
            wait(nc.vector, s_o, b * NB + u - 2)
            nc.vector.reciprocal(rsum[:, u % 4, :], sums[:, u % 4, :]).then_inc(s_r, 1)

        def copy_turned_v(b, u):
            wait(nc.vector, s_T, b * NB + u + 1)
            wait(nc.vector, s_y, b * NB + u - 1)
            nc.vector.tensor_copy(CT[:, u % 2, 0:HS, :], TB[:, 0:HS, :]).then_inc(s_td, 1)

        def add(b, u):
            wait(nc.vector, s_y, b * NB + u + 1)
            wait(nc.vector, s_r, b * NB + u + 1)
            x = x_nat[:, bass.ds(b * NB + u, 1), :].rearrange("p o d -> p (o d)")
            nc.vector.scalar_tensor_tensor(out=x, in0=Y[u % 2][:, 0:D], scalar=rsum[:, u % 4, :], in1=x,
                                           op0=ALU.mult, op1=ALU.add).then_inc(s_o, 1)

        def exps(b, u):
            wait(nc.scalar, s_mx, b * NB + u + 1)
            wait(nc.scalar, s_r, b * NB + u - 3)
            wait(nc.scalar, s_T, b * NB + u - 1)
            nc.scalar.activation(CO[:, u % 2, :], LG[u % 2][:, :], ACT.Exp, bias=nmax[:, u % 2, :],
                                 accum_out=sums[:, u % 4, :]).then_inc(s_e, 1)

        def copy_turned_a(b, u):
            wait(nc.scalar, s_T, b * NB + u + 1)
            wait(nc.scalar, s_y, b * NB + u - 1)
            nc.scalar.activation(CT[:, u % 2, HS:ST, :], TB[:, HS:ST, :], ACT.Copy).then_inc(s_ta, 1)

        with nc.Block() as block:
            @block.tensor
            def _(pe):
                pipeline(pe, [(logits, L_L), (turn, L_T), (mix, L_Y)], NB, B)

            @block.vector
            def _(v):
                pipeline(v, [(stage, 0), (neg_max, L_L), (recip, L_T), (copy_turned_v, L_T), (add, L_Y)], NB, B)

            @block.scalar
            def _(a):
                pipeline(a, [(exps, L_L), (copy_turned_a, L_T)], NB, B)


RS = 4 * HD1


def prepare1(nc, xT, ident, qsT, ksT, vN, inf, bias, ones, wq, wd, wu, bu, cos, sin, s_w):
    W4, HALF = [P, NB, H1, HD1], HD1 // 2
    PER = 2
    TURNS = 2 * G1
    with Phase(nc, "p1") as ph:
        qT, cT = ph.sb("qT", [P, T]), ph.sb("cT", [LAT, T])
        q = [ph.sb(f"q{u}", W4) for u in range(PER)]
        kv = [ph.sb(f"kv{u}", [P, NB, H1, 2 * HD1]) for u in range(PER)]
        rot = {s: [ph.sb(f"rot_{s}{u}", W4) for u in range(PER)] for s in "qk"}
        hi = {s: [ph.sb(f"high_{s}{u}", W4) for u in range(PER)] for s in "qk"}
        st = {s: [ph.sb(f"stack_{s}{u}", [P, NB * H1, 4, HD1]) for u in range(PER)] for s in "qk"}
        tt = {s: [ph.sb(f"t{k}{s}", [P, NB, H1, HALF]) for k in range(4)] for s in "qk"}
        rs = ph.sb("rs", W4)
        prod = ph.sb("prod", W4)
        score, gate, gate2 = (ph.sb(n, [P, NB, H1]) for n in ("score", "gate", "gate2"))
        PQ, PN, PC = ph.ps("pq", [P, T]), ph.ps("pn", [P, T]), ph.ps("pc", [P, T])
        KV = ph.ps("pkv", [P, NB, 2 * D])
        PM = ph.ps("pmean", [P, T])
        PT = [ph.ps(f"turned{k}", [P, T]) for k in range(2)]
        s_pq, s_qT, s_pc, s_cT, s_pn, s_kv = (ph.sem(n) for n in ("pq_", "qT_", "pc_", "cT_", "pn_", "pkv_"))
        s_x = {s: ph.sem("x_" + s) for s in "qk"}
        s_t = {s: ph.sem("products_" + s) for s in "qk"}
        s_rot = {s: ph.sem("rotated_" + s) for s in "qk"}
        s_hi = {s: ph.sem("high_" + s) for s in "qk"}
        s_st = {s: ph.sem("stacked_" + s) for s in "qk"}
        s_sh = {s: ph.sem("stacked_high_" + s) for s in "qk"}
        s_sc, s_rs, s_v, s_mn, s_pr, s_g, s_g2, s_inf, s_tt, s_to = (
            ph.sem(n) for n in ("score_", "scaled", "v_", "mean", "prod_", "gate_", "gate2_", "inf_", "tt", "to"))

        def flat(t):
            return t[:, :, :, :].rearrange("p n h d -> p (n h d)")

        def rotate(eng, e, s, n, src, dst):
            c4, s4 = (t[:, :, None, :].broadcast_to([P, NB, H1, HALF]) for t in (cos, sin))
            x1, x2 = src[:, :, :, 0:HALF], src[:, :, :, HALF:HD1]
            t = tt[s]
            wait(eng, s_rot[s], 2 * n)
            wait(eng, s_x[s], n + 1)
            for k, (i0, i1) in enumerate(((x1, c4), (x2, s4), (x1, s4), (x2, c4))):
                e.tensor_tensor(t[k][:, :, :, :], i0, i1, ALU.mult).then_inc(s_t[s], 1)
            wait(eng, s_t[s], (n + 1) * 4)
            e.tensor_tensor(dst[:, :, :, 0:HALF], t[0][:, :, :, :], t[1][:, :, :, :], ALU.subtract).then_inc(s_rot[s], 1)
            e.tensor_tensor(dst[:, :, :, HALF:HD1], t[2][:, :, :, :], t[3][:, :, :, :], ALU.add).then_inc(s_rot[s], 1)

        def high(src, s, u):
            nc.vector.tensor_scalar(flat(hi[s][u]).bitcast(I32), flat(src).bitcast(I32), -4096, None,
                                    ALU.bitwise_and).then_inc(s_hi[s], 1)

        SETS = {"q": (slice(0, 2), slice(2, 4)), "k": (slice(0, 4, 2), slice(1, 4, 2))}

        def row_sets(t):
            return t[:, :, :, :].rearrange("p n h d -> p (n h) d")[:, :, None, :].broadcast_to([P, NB * H1, 2, HD1])

        def stack_rest(e, src, s, u):
            e.tensor_tensor(st[s][u][:, :, SETS[s][1], :], row_sets(src), row_sets(hi[s][u]), ALU.subtract).then_inc(s_st[s], 1)

        def project(i, u):
            b = i * PER + u
            x = xT[:, bass.ds(b * T, T)]
            wait(nc.tensor, s_qT, b)
            wait(nc.tensor, s_cT, b)
            nc.tensor.matmul(PQ[:, :], wq[:, :], x, start=True, stop=True).then_inc(s_pq, 1)
            nc.tensor.matmul(PC[0:LAT, :], wd[:, :], x, start=True, stop=True).then_inc(s_pc, 1)
            wait(nc.tensor, s_qT, b + 1)
            wait(nc.tensor, s_x["q"], b)
            for n in range(NB):
                last = nc.tensor.transpose(PN[:, n * P:(n + 1) * P], qT[:, n * P:(n + 1) * P], ident[:, :])
            last.then_inc(s_pn, 1)
            wait(nc.tensor, s_cT, b + 1)
            wait(nc.tensor, s_x["k"], b)
            for n in range(NB):
                last = nc.tensor.matmul(KV[:, n, :], cT[:, n * P:(n + 1) * P], wu[:, :], start=True, stop=True)
            last.then_inc(s_kv, 1)

        def means(i, u):
            b = i * PER + u
            wait(nc.tensor, s_rot["k"], (b + 1) * 2)
            wait(nc.tensor, s_inf, b)
            for n in range(NB):
                nc.tensor.matmul(PM[:, 0:D], ones[:, :], rot["k"][u][:, n, :, :].rearrange("p h d -> p (h d)"),
                                 start=(n == 0), stop=(n == NB - 1))
            for n in range(NB):
                last = nc.tensor.matmul(PM[:, D:2 * D], ones[:, :], kv[u][:, n, :, HD1:2 * HD1],
                                        start=(n == 0), stop=(n == NB - 1))
            last.then_inc(s_mn, 1)

        def turns(i, u):
            b = i * PER + u
            for k in range(TURNS):
                if k in (0, G1):
                    s = "qk"[k // G1]
                    wait(nc.tensor, s_sh[s], b + 1)
                    wait(nc.tensor, s_st[s], b + 1)
                wait(nc.tensor, s_to, b * TURNS + k - 1)
                for n in range(NB):
                    r = n * H1 + k % G1 * HG
                    src = st["qk"[k // G1]][u][:, r:r + HG, :, :].rearrange("p h r d -> p (h r d)")
                    last = nc.tensor.transpose(PT[k % 2][:, n * P:(n + 1) * P], src, ident[:, :])
                last.then_inc(s_tt, 1)

        def biased(i, u):
            b = i * PER + u
            wait(nc.scalar, s_pq, b + 1)
            wait(nc.scalar, s_pn, b)
            nc.scalar.activation(qT[:, :], PQ[:, :], ACT.Identity, bias=bias[:, 0:1]).then_inc(s_qT, 1)
            wait(nc.scalar, s_pc, b + 1)
            wait(nc.scalar, s_kv, b)
            nc.scalar.activation(cT[:, :], PC[0:LAT, :], ACT.Identity, bias=bias[0:LAT, 1:2]).then_inc(s_cT, 1)

        def stack_high(i, u):
            b = i * PER + u
            for s in "qk":
                wait(nc.scalar, s_hi[s], b + 1)
                wait(nc.scalar, s_tt, (b - 1) * TURNS)
                nc.scalar.activation(st[s][u][:, :, SETS[s][0], :], row_sets(hi[s][u]), ACT.Copy).then_inc(s_sh[s], 1)

        def v_rows(i, u):
            b = i * PER + u
            wait(nc.scalar, s_x["k"], b + 1)
            nc.scalar.activation(vN[:, bass.ds(b * NB, NB), :].rearrange("p n (h d) -> p n h d", h=H1),
                                 kv[u][:, :, :, HD1:2 * HD1], ACT.Copy).then_inc(s_v, 1)

        def turned_out(i, u):
            b = i * PER + u
            for k in range(TURNS):
                wait(nc.scalar, s_tt, b * TURNS + k + 1)
                dst = (qsT, ksT)[k // G1][:, k % G1, bass.ds(b * T, T)]
                nc.scalar.activation(dst, PT[k % 2][:, :], ACT.Copy).then_inc(s_to, 1)

        def gates(i, u):
            b = i * PER + u
            wait(nc.scalar, s_sc, b + 1)
            nc.scalar.activation(gate[:, :, :], score[:, :, :], ACT.Sigmoid).then_inc(s_g, 1)

        def take(i, u):
            b = i * PER + u
            wait(nc.vector, s_pn, b + 1)
            nc.vector.tensor_copy(flat(q[u]), PN[:, :]).then_inc(s_x["q"], 1)
            wait(nc.vector, s_kv, b + 1)
            wait(nc.vector, s_mn, b - 1)
            wait(nc.vector, s_v, b - 1)
            nc.vector.tensor_tensor(kv[u][:, :, :, :].rearrange("p n h d -> p n (h d)"), KV[:, :, :],
                                    bu[:, None, :].broadcast_to([P, NB, 2 * D]), ALU.add).then_inc(s_x["k"], 1)

        def q_rows(i, u):
            b = i * PER + u
            rotate(nc.vector, nc.vector, "q", b, q[u], rot["q"][u])
            wait(nc.vector, s_rot["q"], (b + 1) * 2)
            nc.vector.tensor_scalar(flat(rs), flat(rot["q"][u]), -HD1 ** -0.5, None, ALU.mult).then_inc(s_rs, 1)
            wait(nc.vector, s_rs, b + 1)
            wait(nc.vector, s_sh["q"], b - 1)
            high(rs, "q", u)
            wait(nc.vector, s_hi["q"], b + 1)
            wait(nc.vector, s_tt, (b - 1) * TURNS)
            stack_rest(nc.vector, rs, "q", u)
            wait(nc.vector, s_rot["k"], (b + 1) * 2)
            wait(nc.vector, s_sh["k"], b - 1)
            wait(nc.vector, s_st["k"], b - 1)
            high(rot["k"][u], "k", u)

        def memory(i, u):
            b = i * PER + u
            wait(nc.vector, s_mn, b + 1)
            nc.vector.tensor_tensor(prod[:, :, :, :].rearrange("p n h d -> p n (h d)"),
                                    rot["q"][u][:, :, :, :].rearrange("p n h d -> p n (h d)"),
                                    PM[:, None, 0:D].broadcast_to([P, NB, D]), ALU.mult).then_inc(s_pr, 1)
            wait(nc.vector, s_pr, b + 1)
            nc.vector.tensor_reduce(score[:, :, :], prod[:, :, :, :], AX.X, ALU.add).then_inc(s_sc, 1)
            wait(nc.vector, s_g, b + 1)
            nc.vector.tensor_scalar(gate2[:, :, :], gate[:, :, :], 0.2, None, ALU.mult).then_inc(s_g2, 1)
            wait(nc.vector, s_g2, b + 1)
            nc.vector.tensor_tensor(inf[:, bass.ds(b * NB, NB), :].rearrange("p n (h d) -> p n h d", h=H1), gate2[:, :, :, None].broadcast_to(W4),
                                    PM[:, D:2 * D].rearrange("p (h d) -> p h d", h=H1)[:, None, :, :].broadcast_to(W4),
                                    ALU.mult).then_inc(s_inf, 1)

        def k_rows(i, u):
            b = i * PER + u
            wait(nc.gpsimd, s_mn, b - 1)
            rotate(nc.gpsimd, nc.gpsimd, "k", b, kv[u], rot["k"][u])
            wait(nc.gpsimd, s_tt, (b - 1) * TURNS)
            wait(nc.gpsimd, s_hi["k"], b + 1)
            stack_rest(nc.gpsimd, rot["k"][u], "k", u)

        with nc.Block() as block:
            @block.tensor
            def _(pe):
                pe.wait_ge(s_w, SMALL1 * 16)
                pipeline(pe, [(project, 0), (turns, 2), (means, 1)], PER, B // PER)

            @block.scalar
            def _(a):
                pipeline(a, [(biased, 0), (turned_out, 2), (v_rows, 1), (stack_high, 1), (gates, 1)], PER, B // PER)

            @block.vector
            def _(v):
                v.wait_ge(s_w, SMALL1 * 16)
                pipeline(v, [(take, 0), (q_rows, 1), (memory, 1)], PER, B // PER)

            @block.gpsimd
            def _(g):
                g.wait_ge(s_w, SMALL1 * 16)
                pipeline(g, [(k_rows, 1)], PER, B // PER)


def attention1(nc, x_nat, xT, qsT, ksT, vN, inf, mask, ident, bias, Wo, bo_in, s_c):
    SL = 4 * G1
    TL = 4 * SL
    L_S, L_T, L_PV = 2, 6, 7
    with Phase(nc, "a1") as ph:
        QZ = ph.sb("qz", [P, 4, T], F32R)
        VZ = ph.sb("vz", [P, 2, NB, HG, RS])
        PR = ph.sb("probs", [P, 2, HG, NB, T])
        PT = ph.sb("probsT", [P, 2, HG, T])
        least = ph.sb("least", [P, 4, NB])
        first_v, first_g = ph.sb("first_v", [P, 4]), ph.sb("first_g", [P, 4])
        rec = ph.sb("rec", [P, 2, NB, HG])
        wo, bo = ph.sb("wo", [P, D]), ph.sb("bo", [P, D])
        on = xT[:, :].rearrange("p (b r d) -> p b r d", b=B, r=NB)
        onT = ph.sb("onT", [P, 2, T])
        SC = [ph.ps(f"scores{k}", [P, T]) for k in range(3)]
        TB = [ph.ps(f"turned{k}", [P, 2, T]) for k in range(2)]
        OB = ph.ps("outT", [P, T])
        s_wo, s_z = ph.sem("wout"), ph.sem("zeros")
        s_qz, s_vz, s_S, s_b, s_e = (ph.sem(n) for n in ("q_in", "v_in", "scored", "biased", "exped"))
        s_T, s_ta, s_td, s_pv, s_o = (ph.sem(n) for n in ("turned_", "copied_a", "copied_d", "pv", "o_out"))
        s_fv, s_fg = ph.sem("first_v_"), ph.sem("first_g_")
        s_s, s_rc, s_dv, s_m, s_n, s_nc, s_y, s_x, s_xb = (ph.sem(n) for n in (
            "rows", "recip", "divided", "memory", "back", "back_out", "y", "x", "xb"))

        def head_q(b, u):
            g, j = u // 4, u % 4
            wait(nc.gpsimd, s_fg, b * SL + u - 3)
            wait(nc.gpsimd, s_S, b * TL + 4 * u - 12)
            nc.gpsimd.tensor_tensor(first_g[:, j:j + 1], mask[:, 0:1], mask[:, 0:1], ALU.mult).then_inc(s_fg, 1)
            nc.gpsimd.tensor_tensor(QZ[:, j, :], qsT[:, g, bass.ds(b * T, T)].bitcast(F32),
                                    mask[:, j:j + 1].broadcast_to([P, T]), ALU.mult).then_inc(s_qz, 1)

        def head_v(b, u):
            g, j = u // 4, u % 4
            if j == 0:
                wait(nc.gpsimd, s_pv, b * SL + u - 4)
                src = vN[:, bass.ds(b * NB, NB), g * HG * HD1:(g + 1) * HG * HD1].rearrange("p n (h d) -> p n h d", h=HG)
                nc.gpsimd.tensor_copy(VZ[:, g % 2, :, :, 0:HD1], src).then_inc(s_vz, 1)

        def scores(b, u, pair):
            g, j = u // 4, u % 4
            if pair == 0:
                wait(nc.tensor, s_qz, b * SL + u + 1)
            for r in (2 * pair, 2 * pair + 1):
                m = 4 * u + r
                wait(nc.tensor, s_b, b * TL + m - (2 if m else 0))
                nc.tensor.matmul(SC[m % 3][:, :], QZ[:, j, r * P:(r + 1) * P], ksT[:, g, bass.ds(b * T, T)],
                                 start=True, stop=True).then_inc(s_S, 1)

        def scores_1(b, u):
            scores(b, u, 0)

        def scores_2(b, u):
            scores(b, u, 1)

        def turn(b, u, half):
            g, j = u // 4, u % 4
            wait(nc.tensor, (s_td, s_ta)[half], b * SL + u)
            for h in range(2):
                for r in range(NB):
                    last = nc.tensor.transpose(TB[half][:, h, r * P:(r + 1) * P],
                                               PR[:, g % 2, 2 * half + h, r, j * P:(j + 1) * P], ident[:, :])
            last.then_inc(s_T, 1)

        def turn_1(b, u):
            if u % 4 == 0:
                wait(nc.tensor, s_e, b * SL + u + 4)
            turn(b, u, 0)

        def turn_2(b, u):
            turn(b, u, 1)

        def pv(b, u):
            g, j = u // 4, u % 4
            wait(nc.tensor, s_ta, b * SL + u + 1)
            wait(nc.tensor, s_td, b * SL + u + 1)
            if j == 0:
                wait(nc.tensor, s_vz, b * G1 + g + 1)
                wait(nc.tensor, s_o, b * G1 + g)
            for h in range(HG):
                last = nc.tensor.matmul(OB[h * RS:(h + 1) * RS, :], VZ[:, g % 2, j, h, :], PT[:, u % 2, h, :],
                                        start=(j == 0), stop=(j == NB - 1))
            last.then_inc(s_pv, 1)

        def start_v(b, u):
            wait(nc.vector, s_fv, b * SL + u - 3)
            wait(nc.vector, s_e, b * SL + u - 3)
            if u % 4 == 0:
                wait(nc.vector, s_T, b * 2 * SL + 2 * u - 8)
            wait(nc.vector, s_S, b * TL + 4 * u + 2)
            nc.vector.tensor_copy(first_v[:, u % 4:u % 4 + 1], mask[:, 0:1]).then_inc(s_fv, 1)

        def add_bias(b, u, pair):
            g, j = u // 4, u % 4
            for r in (2 * pair, 2 * pair + 1):
                m = 4 * u + r
                nc.vector.tensor_tensor_reduce(PR[:, g % 2, j, r, :], SC[m % 3][:, :], bias[:, r, :], 1.0, 3.0e38,
                                               ALU.add, ALU.min, least[:, j, r:r + 1]).then_inc(s_b, 1)

        def add_bias_1(b, u):
            add_bias(b, u, 0)

        def await_scores_2(b, u):
            wait(nc.vector, s_S, b * TL + 4 * u + 4)

        def copy_turned_v(b, u):
            wait(nc.vector, s_T, b * 2 * SL + 2 * u + 1)
            wait(nc.vector, s_pv, b * SL + u - 1)
            nc.vector.tensor_copy(PT[:, u % 2, 0:2, :], TB[0][:, :, :]).then_inc(s_td, 1)

        def add_bias_2(b, u):
            add_bias(b, u, 1)

        def exps(b, u, tiles):
            g, j = u // 4, u % 4
            for r in tiles:
                wait(nc.scalar, s_b, b * TL + 4 * u + r + 1)
                pr = PR[:, g % 2, j, r, :]
                last = nc.scalar.activation(pr, pr, ACT.Exp, bias=least[:, j, r:r + 1], scale=-1.0)
            return last

        def exps_1(b, u):
            exps(b, u, (0, 1))

        def copy_turned_a(b, u):
            wait(nc.scalar, s_T, b * 2 * SL + 2 * u + 2)
            wait(nc.scalar, s_pv, b * SL + u - 1)
            nc.scalar.activation(PT[:, u % 2, 2:4, :], TB[1][:, :, :], ACT.Copy).then_inc(s_ta, 1)

        def exps_2(b, u):
            exps(b, u, (2, 3)).then_inc(s_e, 1)

        def o_out(b, u):
            g, j = u // 4, u % 4
            if j == 3:
                wait(nc.scalar, s_pv, b * SL + u + 1)
                nc.scalar.activation(qsT[:, g, bass.ds(b * T, T)].bitcast(F32), OB[:, :], ACT.Copy).then_inc(s_o, 1)

        with nc.Block() as block:
            @block.sync
            def _(sp):
                sp.dma_start(wo[:, :], Wo).then_inc(s_wo, 16)
                sp.dma_start(bo[:, :], bo_in[None, :].broadcast_to([P, D])).then_inc(s_wo, 16)

            def out_proj(pe, b):
                pe.wait_ge(s_m, b + 1)
                wait(pe, s_nc, b)
                for r in range(NB):
                    last = nc.tensor.transpose(TB[1][:, 0, r * P:(r + 1) * P], on[:, b, r, :], ident[:, :])
                last.then_inc(s_n, 1)
                pe.wait_ge(s_nc, b + 1)
                pe.wait_ge(s_wo, 32)
                wait(pe, s_y, b)
                for r in range(NB):
                    last = nc.tensor.matmul(TB[1][:, 1, r * P:(r + 1) * P], onT[:, b % 2, r * P:(r + 1) * P], wo[:, :],
                                            start=True, stop=True)
                last.then_inc(s_x, 1)

            @block.tensor
            def _(pe):
                pe.wait_ge(s_z, 2)
                pipeline(pe, [(scores_1, L_S), (turn_1, L_T), (scores_2, L_S), (turn_2, L_T), (pv, L_PV)], SL, B)
                pe.wait_ge(s_o, B * G1)
                for b in range(B + 1):
                    for g in range(G1 if b < B else 0):
                        n = b * G1 + g
                        wait(pe, s_dv, n - 1)
                        for r in range(NB):
                            o = qsT[:, g, (b * NB + r) * P:(b * NB + r + 1) * P].bitcast(F32)
                            last = nc.tensor.transpose(TB[0][:, n % 2, r * P:(r + 1) * P], o, ident[:, :])
                        last.then_inc(s_s, 1)
                    if b:
                        out_proj(pe, b - 1)

            @block.vector
            def _(v):
                nc.vector.memset(VZ[:, :, :, :, :], 0.0).then_inc(s_z, 1)
                v.wait_ge(s_z, 1)
                nc.vector.memset(VZ[:, :, :, :, HD1:HD1 + 1], 1.0).then_inc(s_z, 1)
                v.wait_ge(s_c, 16)
                pipeline(v, [(start_v, L_S), (add_bias_1, L_S), (await_scores_2, L_S), (copy_turned_v, L_T),
                             (add_bias_2, L_S)], SL, B)
                v.wait_ge(s_wo, 32)
                nc.vector.tensor_tensor(x_nat[:, :, :], x_nat[:, :, :], bo[:, None, :].broadcast_to([P, NT, D]),
                                        ALU.add).then_inc(s_xb, 1)
                v.wait_ge(s_xb, 1)
                for b in range(B + 1):
                    for g in range(G1 if b < B else 0):
                        n = b * G1 + g
                        v.wait_ge(s_s, n + 1)
                        wait(v, s_dv, n - 1)
                        o = TB[0][:, n % 2, :].rearrange("p (r h j) -> p r h j", r=NB, h=HG)
                        nc.vector.reciprocal(rec[:, n % 2, :, :], o[:, :, :, HD1]).then_inc(s_rc, 1)
                        v.wait_ge(s_rc, n + 1)
                        nc.vector.tensor_tensor(on[:, b, :, g * HG * HD1:(g + 1) * HG * HD1].rearrange("p r (h d) -> p r h d", h=HG),
                                                o[:, :, :, 0:HD1], rec[:, n % 2, :, :, None].broadcast_to([P, NB, HG, HD1]),
                                                ALU.mult).then_inc(s_dv, 1)
                    if b:
                        v.wait_ge(s_x, b)
                        x = x_nat[:, (b - 1) * NB:b * NB, :].rearrange("p n d -> p (n d)")
                        nc.vector.tensor_tensor(x, TB[1][:, 1, :], x, ALU.add).then_inc(s_y, 1)

            @block.scalar
            def _(a):
                pipeline(a, [(exps_1, L_S), (copy_turned_a, L_T), (exps_2, L_S), (o_out, L_PV)], SL, B)
                for b in range(B):
                    a.wait_ge(s_n, b + 1)
                    wait(a, s_x, b - 1)
                    nc.scalar.activation(onT[:, b % 2, :], TB[1][:, 0, :], ACT.Copy).then_inc(s_nc, 1)

            @block.gpsimd
            def _(g):
                g.wait_ge(s_z, 2)
                pipeline(g, [(head_q, 0), (head_v, 4)], SL, B)
                for b in range(B):
                    g.wait_ge(s_dv, (b + 1) * G1)
                    nc.gpsimd.tensor_tensor(on[:, b, :, :], on[:, b, :, :], inf[:, b * NB:(b + 1) * NB, :], ALU.add).then_inc(s_m, 1)


class Gates:

    def __init__(self, nc, ph, xT, combine, gw, num, s_w):
        self.nc, self.ph, self.xT, self.combine, self.gw, self.num, self.s_w = nc, ph, xT, combine, gw, num, s_w
        W = self.W = [P, NT, E1]
        self.lg, self.ex, self.pr, self.top = (ph.sb(n, W) for n in ("lg", "ex", "pr", "top"))
        self.c = ph.sb("c1", W), ph.sb("c2", W)
        self.at, self.atf = ph.sb("at", W, U32), ph.sb("atf", W)
        self.mx, self.sm, self.rs, self.s2, self.r2 = (ph.sb(n, [P, NT]) for n in ("mx", "sm", "rs", "s2", "r2"))
        self.wt = ph.sb("wt", [P, 2, NT])
        self.count = 0
        self.LG = ph.ps("logits", W)
        self.s_l, self.s_c, self.s_e, self.s_m = (ph.sem(n) for n in ("logits_", "chain", "exped", "tops"))

    def tensor(self, pe):
        pe.wait_ge(self.s_w, SMALL1 * 16)
        for t in range(NT):
            last = self.nc.tensor.matmul(self.LG[:, t, :], self.xT[:, t * P:(t + 1) * P], self.gw[:, :], start=True, stop=True)
        last.then_inc(self.s_l, 1)

    def scalar(self, a):
        a.wait_ge(self.s_c, 2)
        self.nc.scalar.activation(self.ex[:, :, :], self.lg[:, :, :], ACT.Exp).then_inc(self.s_e, 1)

    def link(self, v, ins):
        self.count += 1
        ins.then_inc(self.s_c, 1)
        v.wait_ge(self.s_c, self.count)

    def probabilities(self, v):
        nc, W, lg, ex, pr = self.nc, self.W, self.lg, self.ex, self.pr
        v.wait_ge(self.s_l, 1)
        self.link(v, nc.vector.tensor_reduce(self.mx[:, :], self.LG[:, :, :], AX.X, ALU.max))
        self.link(v, nc.vector.tensor_tensor(lg[:, :, :], self.LG[:, :, :], self.mx[:, :, None].broadcast_to(W), ALU.subtract))
        v.wait_ge(self.s_e, 1)
        self.link(v, nc.vector.tensor_reduce(self.sm[:, :], ex[:, :, :], AX.X, ALU.add))
        self.link(v, nc.vector.reciprocal(self.rs[:, :], self.sm[:, :]))
        self.link(v, nc.vector.tensor_tensor(pr[:, :, :], ex[:, :, :], self.rs[:, :, None].broadcast_to(W), ALU.mult))
        for t in range(NT):
            nc.vector.max(self.top[:, t, :], pr[:, t, :]).then_inc(self.s_m, 1)

    def two_largest(self, v):
        nc, top, at, atf, wt = self.nc, self.top, self.at, self.atf, self.wt
        for t in range(NT):
            v.wait_ge(self.s_m, t + 1)
            last = nc.vector.max_index(at[:, t, :], top[:, t, :], self.pr[:, t, :])
        self.link(v, last)
        self.link(v, nc.vector.tensor_copy(atf[:, :, :], at[:, :, :]))
        self.link(v, nc.vector.tensor_tensor(self.s2[:, :], top[:, :, 0], top[:, :, 1], ALU.add))
        self.link(v, nc.vector.reciprocal(self.r2[:, :], self.s2[:, :]))
        self.link(v, nc.vector.tensor_tensor(wt[:, 0, :], top[:, :, 0], self.r2[:, :], ALU.mult))
        self.link(v, nc.vector.tensor_tensor(wt[:, 1, :], top[:, :, 1], self.r2[:, :], ALU.mult))

    def weights(self, v):
        nc, W = self.nc, self.W
        v.wait_ge(self.s_w, SMALL1 * 16)
        for k, c in enumerate(self.c):
            self.link(v, nc.vector.tensor_tensor(c[:, :, :], self.num[:, None, :].broadcast_to(W),
                                                 self.atf[:, :, k:k + 1].broadcast_to(W), ALU.is_equal))
            self.link(v, nc.vector.tensor_tensor(c[:, :, :], c[:, :, :], self.wt[:, k, :, None].broadcast_to(W), ALU.mult))
        self.link(v, nc.vector.tensor_tensor(self.combine[:, :, :], self.c[0][:, :, :], self.c[1][:, :, :], ALU.add))


def load_expert1(sp, bufs, w_gate, w_up, w_down, s_w, i, q):
    wgu, wd = bufs
    e, full = bass.ds(i * 2 + q, 1), F1 // P
    sp.dma_start(wgu[:, q, 0, :], w_gate[e].rearrange("o d f -> d (o f)")).then_inc(s_w[q], 16)
    sp.dma_start(wgu[:, q, 1, :], w_up[e].rearrange("o d f -> d (o f)")).then_inc(s_w[q], 16)
    sp.dma_start(wd[:, q, 0:full, :],
                 w_down[e, 0:full * P].rearrange("o (k p) n -> p (o k) n", p=P)).then_inc(s_w[q], 16)
    sp.dma_start(wd[0:F1 - full * P, q, full, :], w_down[e, full * P:F1].rearrange("o p n -> p (o n)")).then_inc(s_w[q], 16)


def experts1(nc, x_nat, xT, combine, gw, num, s_small, bufs, s_w, w_gate, w_up, w_down):
    PER = 2 * B
    L_G, L_D = 2, 3
    with Phase(nc, "e1") as ph:
        wgu, wd = bufs
        gates = Gates(nc, ph, xT, combine, gw, num, s_small)
        wH, wL = ph.sb("w_high", [P, 2, 2, F1], F32R), ph.sb("w_rest", [P, 2, 2, F1], F32R)
        xH, xL = ph.sb("x_high", [P, B * T], F32R), ph.sb("x_rest", [P, B * T], F32R)
        w32, x32 = ph.sb("w_high32", [P, 2, 2, F1]), ph.sb("x_high32", [P, B * T])
        h, hu = ph.sb("h", [P, 2, T]), ph.sb("hu", [P, 2, FT, T])
        G = [ph.ps(f"gate{k}", [P, T]) for k in range(2)]
        U = [ph.ps(f"up{k}", [P, T]) for k in range(2)]
        Y = [ph.ps(f"out{k}", [P, NB, D]) for k in range(2)]
        s_xh, s_xc, s_xl, s_wh, s_wc, s_wl = (ph.sem(n) for n in (
            "x_high32_", "x_high_", "x_rest_", "w_high32_", "w_high_", "w_rest_"))
        s_g, s_h, s_m, s_d, s_y = (ph.sem(n) for n in ("gated", "silu", "times", "down", "added"))
        full = F1 // P
        size = [P] * full + [F1 - full * P]

        def gate_up(i, u, tiles):
            q, b = u // B, u % B
            if b == 0 and tiles[0] == 0:
                wait(nc.tensor, s_wc, i * 2 + q + 1)
                wait(nc.tensor, s_wl, i * 2 + q + 1)
            if isinstance(i, int) and q == 0:
                wait(nc.tensor, s_xc, b + 1)
                wait(nc.tensor, s_xl, b + 1)
            for k in tiles:
                m = u * FT + k
                wait(nc.tensor, s_m, i * PER * FT + m - 1)
                for n, bank in enumerate((G, U)):
                    for p, (ww, xx) in enumerate(((wH, xH), (wH, xL), (wL, xH))):
                        last = nc.tensor.matmul(bank[m % 2][0:size[k], :], ww[:, q, n, k * P:k * P + size[k]],
                                                xx[:, b * T:(b + 1) * T], start=(p == 0), stop=(p == 2))
                last.then_inc(s_g, 1)

        def gate_up_1(i, u):
            gate_up(i, u, (0, 1))

        def gate_up_2(i, u):
            gate_up(i, u, (2,))

        def down(i, u):
            q = u // B
            wait(nc.tensor, s_m, (i * PER + u + 1) * FT)
            wait(nc.tensor, s_y, i * PER + u - 1)
            for n in range(NB):
                for k in range(FT):
                    last = nc.tensor.matmul(Y[u % 2][:, n, :], hu[0:size[k], u % 2, k, n * P:(n + 1) * P],
                                            wd[0:size[k], q, k, :], start=(k == 0), stop=(k == FT - 1))
            last.then_inc(s_d, 1)

        def high(dst, src):
            return nc.vector.tensor_scalar(dst.bitcast(I32), src.bitcast(I32), -4096, None, ALU.bitwise_and)

        def split_high(i, u):
            q, b = u // B, u % B
            if b == 0:
                wait(nc.vector, s_w[q], (i + 1) * 64)
                wait(nc.vector, s_d, (i * 2 + q - 1) * B)
                high(w32[:, q, :, :], wgu[:, q, :, :]).then_inc(s_wh, 1)

        def gate_chain(i, u):
            if isinstance(i, int) and i == 0 and u < 3:
                (gates.probabilities, gates.two_largest, gates.weights)[u](nc.vector)

        def split_rest(i, u):
            q, b = u // B, u % B
            if b == 0:
                wait(nc.gpsimd, s_wh, i * 2 + q + 1)
                nc.gpsimd.tensor_tensor(wL[:, q, :, :], wgu[:, q, :, :], w32[:, q, :, :],
                                        ALU.subtract).then_inc(s_wl, 1)

        def keep_high(i, u):
            q, b = u // B, u % B
            if b == 0:
                wait(nc.scalar, s_wh, i * 2 + q + 1)
                nc.scalar.activation(wH[:, q, :, :], w32[:, q, :, :], ACT.Copy).then_inc(s_wc, 1)
            if isinstance(i, int) and i == 0 and u == 0:
                gates.scalar(nc.scalar)

        def silu(i, u):
            for k in range(FT):
                m = u * FT + k
                wait(nc.scalar, s_g, i * PER * FT + m + 1)
                wait(nc.scalar, s_m, i * PER * FT + m - 1)
                nc.scalar.activation(h[0:size[k], m % 2, :], G[m % 2][0:size[k], :], ACT.Silu).then_inc(s_h, 1)

        def times(i, u, tiles):
            if tiles[0] == 0:
                wait(nc.vector, s_d, i * PER + u - 1)
            for k in tiles:
                m = u * FT + k
                wait(nc.vector, s_h, i * PER * FT + m + 1)
                nc.vector.tensor_tensor(hu[0:size[k], u % 2, k, :], U[m % 2][0:size[k], :], h[0:size[k], m % 2, :],
                                        ALU.mult).then_inc(s_m, 1)

        def times_1(i, u):
            times(i, u, (0, 1))

        def times_2(i, u):
            times(i, u, (2,))

        def add(i, u):
            q, b = u // B, u % B
            wait(nc.vector, s_d, i * PER + u + 1)
            wait(nc.vector, s_y, i * PER + u - B + 1)
            for n in range(NB):
                t = b * NB + n
                last = nc.vector.scalar_tensor_tensor(out=x_nat[:, t, :], in0=Y[u % 2][:, n, :],
                                                      scalar=combine[:, t, bass.ds(i * 2 + q, 1)], in1=x_nat[:, t, :],
                                                      op0=ALU.mult, op1=ALU.add)
            last.then_inc(s_y, 1)

        with nc.Block() as block:
            @block.sync
            def _(sp):
                with sp.Fori(1, E1 // 2) as i:
                    for q in range(2):
                        sp.wait_ge(s_d, i * PER + (q - 1) * B)
                        load_expert1(sp, bufs, w_gate, w_up, w_down, s_w, i, q)

            @block.tensor
            def _(pe):
                gates.tensor(pe)
                pipeline(pe, [(gate_up_1, L_G), (down, L_D), (gate_up_2, L_G)], PER, E1 // 2)

            @block.scalar
            def _(a):
                for b in range(B):
                    at = slice(b * T, (b + 1) * T)
                    a.wait_ge(s_xh, b + 1)
                    nc.scalar.activation(xH[:, at], x32[:, at], ACT.Copy).then_inc(s_xc, 1)
                pipeline(a, [(keep_high, 0), (silu, L_G)], PER, E1 // 2)

            @block.vector
            def _(v):
                for b in range(B):
                    at = slice(b * T, (b + 1) * T)
                    high(x32[:, at], xT[:, at]).then_inc(s_xh, 1)
                for b in range(B):
                    at = slice(b * T, (b + 1) * T)
                    v.wait_ge(s_xh, b + 1)
                    nc.vector.tensor_tensor(xL[:, at], xT[:, at], x32[:, at], ALU.subtract).then_inc(s_xl, 1)
                pipeline(v, [(split_high, 0), (times_1, L_G), (add, L_D), (times_2, L_G), (gate_chain, 0)], PER, E1 // 2)

            @block.gpsimd
            def _(g):
                pipeline(g, [(split_rest, 0)], PER, E1 // 2)


def build(nc, a, out):
    with ExitStack() as top:
        def sb(name, shape, dt=F32):
            return top.enter_context(nc.sbuf_tensor(name, shape, dt))

        x_nat, xT = sb("x_nat", [P, NT, D]), sb("xT", [P, B * T])
        ident, ones = sb("ident", [P, P]), sb("ones", [P, P])
        epsc, mask = sb("epsc", [P, 1]), sb("mask", [P, HG])
        bqkv = sb("bqkv", [P, 3 * H0])
        b1 = sb("b1", [P, 2])
        bgT, buT = sb("bgT", [P, E0 * F0 // P]), sb("buT", [P, E0 * F0 // P])
        combine = sb("combine", [P, NT, E1])

        sems = {n: Counted(top.enter_context(nc.semaphore(n))) for n in (
            "turned", "turn_copied", "stats", "mean_var", "std", "rstd", "off", "normed_v", "normed_a", "gained", "shifted",
            "scaled", "out")}

        wq, wd, wu, bu = sb("wq", [P, D]), sb("wd", [P, LAT]), sb("wu", [LAT, 2 * D]), sb("bu", [P, 2 * D])
        cos, sin = sb("cos", [P, NB, HD1 // 2]), sb("sin", [P, NB, HD1 // 2])
        gw, num = sb("gw", [P, E1]), sb("num", [P, E1])

        s_w, s_wo, s_own, s_1 = (top.enter_context(nc.semaphore(n)) for n in ("w_qkv_in", "w_out_in", "own_in", "small_1"))
        early = top.enter_context(ExitStack())

        def sb1(name, shape):
            return early.enter_context(nc.sbuf_tensor(name, shape, F32))

        rows, sc, se, seT = sb1("rows", [P, 4, D]), sb1("sc", [P, 1]), sb1("se", [P, ST, D]), sb1("seT", [P, ST * P])
        with ExitStack() as first:
            def sb0(name, shape):
                return first.enter_context(nc.sbuf_tensor(name, shape, F32))

            w = sb0("w_qkv", [P, 3, H0 // 2, 2, HD0])
            posT, wo, bo = sb0("posT", [P, T]), sb0("wo0", [P, H0 // 2, D]), sb0("bo0", [P, D])
            posb = sb0("posb", [P, 2, 4, T])
            QKV = [sb0("q_cols", [P, 2, P, H0]), sb0("k_cols", [P, 2, P, H0]), sb0("v_cols", [P, 2, P // 2, H0])]
            b_qkv = a["L0_attn_b_qkv"].rearrange("(h c d) -> c h d", c=3, d=HD0)
            preamble(nc, a, sems, x_nat, xT, ident, mask, ones, epsc, [
                ([(c * H0, half * HD0, b_qkv[c]) for c in range(3) for half in range(2)], 3 * H0, P, bqkv),
                ([(0, 0, a["L0_ffn_bg"].rearrange("e (k p) -> (e k) p", p=P))], E0 * F0 // P, P, bgT),
                ([(0, 0, a["L0_ffn_bu"].rearrange("e (k p) -> (e k) p", p=P))], E0 * F0 // P, P, buT),
                ([(0, 0, a["L1_attn_bq"][None, :])], 1, P, b1[:, 0:1]),
                ([(0, 0, a["L1_attn_bkv_down"][None, :])], 1, LAT, b1[:, 1:2]),
            ], rows, sc, se, seT, w, posT, posb, wo, bo, QKV, (
                (wq[:, :], a["L1_attn_Wq"]), (wd[:, :], a["L1_attn_Wkv_down"]), (wu[:, :], a["L1_attn_Wkv_up"]),
                (bu[:, :], a["L1_attn_bkv_up"][None, :].broadcast_to([P, 2 * D])),
                (cos[:, :, :], a["cos"]), (sin[:, :, :], a["sin"]),
                (gw[:, :], a["L1_ffn_gate_w"]), (num[:, :], a["numbers"])), s_w, s_wo, s_own, s_1)
            attention0(nc, x_nat, xT, ident, w, bqkv, wo, posb, QKV, s_w, s_wo, s_own)
            norm_rows(nc, "n0", sems, x_nat, x_nat, epsc)
        with ExitStack() as mid:
            def sb2(name, shape, dt=F32):
                return mid.enter_context(nc.sbuf_tensor(name, shape, dt))

            xn, xnT = sb2("xn", [P, NT, D]), sb2("xnT", [P, B * T])
            slotsT, eout = sb2("slotsT", [P, B, ST * P]), sb2("eout", [P, ST, B, D])
            norm_rows(nc, "n1", sems, x_nat, xn, epsc, rows[:, 0, :], rows[:, 1, :], xnT, ident)
            bufs0 = sb2("wg0", [P, R0, F0]), sb2("wu0", [P, R0, F0]), sb2("wd0", [P, R0, F0 // P, D])
            bdb = sb2("bd", [P, E0, D])
            LT = sb2("logitsT", [P, B * ST, T])
            s_w0 = [mid.enter_context(nc.semaphore(f"weights0_{q}")) for q in range(R0)]
            s_bd = mid.enter_context(nc.semaphore("bd_in"))
            weights = a["L0_ffn_Wg"], a["L0_ffn_Wu"], a["L0_ffn_Wd"]

            def load_experts(sp):
                for q in range(R0):
                    load_expert0(sp, bufs0, *weights, s_w0, 0, q)
                sp.dma_start(bdb[:, :, :], a["L0_ffn_bd"][None, :, :].broadcast_to([P, E0, D])).then_inc(s_bd, 16)

            dispatch0(nc, xn, xnT, seT, LT, slotsT, ident, load_experts)
            experts0(nc, slotsT, eout, bgT, buT, bufs0, bdb, s_w0, s_bd, *weights)
            combine0(nc, x_nat, LT, eout, ident)
        early.close()
        with ExitStack() as mid:
            def sb3(name, shape, dt=F32):
                return mid.enter_context(nc.sbuf_tensor(name, shape, dt))

            bias = sb3("bias", [P, NB, T])
            s_bias = mid.enter_context(nc.semaphore("att_bias_in"))

            def load_bias(sp):
                sp.dma_start(bias[:, :, :], a["att_bias"]).then_inc(s_bias, 16)

            norm_rows(nc, "n3", sems, x_nat, x_nat, epsc, turned=xT, ident=ident, loads=load_bias)
            qsT, ksT = sb3("qsT", [P, G1, B * T], F32R), sb3("ksT", [P, G1, B * T], F32R)
            vN, inf = sb3("vN", [P, NT, D]), sb3("inf", [P, NT, D])
            prepare1(nc, xT, ident, qsT, ksT, vN, inf, b1, ones, wq, wd, wu, bu, cos, sin, s_1)
            attention1(nc, x_nat, xT, qsT, ksT, vN, inf, mask, ident, bias, a["L1_attn_Wo"], a["L1_attn_bo"], s_bias)
        bufs = sb("wgu", [P, 2, 2, F1]), sb("wd1", [P, 2, FT, D])
        s_w1 = [top.enter_context(nc.semaphore(f"weights1_{q}")) for q in range(2)]
        experts = a["L1_ffn_w_gate"], a["L1_ffn_w_up"], a["L1_ffn_w_down"]

        def load_experts(sp):
            for q in range(2):
                load_expert1(sp, bufs, *experts, s_w1, 0, q)

        norm_rows(nc, "n4", sems, x_nat, x_nat, epsc, turned=xT, ident=ident, loads=load_experts)
        experts1(nc, x_nat, xT, combine, gw, num, s_1, bufs, s_w1, *experts)
        norm_rows(nc, "n5", sems, x_nat, x_nat, epsc, out=out)


_OUTS = [((B, T, D), "float32")]


def _constants():
    f = np.float32
    pos = np.arange(T, dtype=f)[:, None]
    div = np.exp(np.arange(0, HD0, 2, dtype=f) * f(-(np.log(10000.0) / HD0))).astype(f)
    ang = (pos * div).astype(f)
    pe = np.zeros((T, HD0), f)
    pe[:, 0::2], pe[:, 1::2] = np.sin(ang), np.cos(ang)
    own = np.repeat(np.tile(np.eye(GT, dtype=f), (1, GC)), H0, axis=1)
    inv = (f(1.0) / np.power(f(10000.0), np.arange(0, HD1, 2, dtype=f) / f(HD1))).astype(f)
    fr = np.outer(np.arange(T, dtype=f), inv).astype(f)
    by_block = lambda t: np.ascontiguousarray(t.reshape(NB, P, -1).transpose(1, 0, 2))
    idx = np.arange(T, dtype=f)
    dist = idx[:, None] - idx[None, :]
    decay = np.exp(-np.maximum(dist, f(0.0)) * f(0.01)).astype(f)
    bias = (f(-0.1) * np.log(np.abs(dist) + f(1.0)) + np.log(decay + f(1e-9))).astype(f)
    return {
        "ident": np.eye(P, dtype=f),
        "mask": np.kron(np.eye(HG, dtype=f), np.ones((RS, 1), f)),
        "own": np.stack([own, f(NOT_OWN) * (f(1.0) - own)]),
        "posT": np.ascontiguousarray(np.concatenate([pe.T, pe.T])),
        "cos": by_block(np.cos(fr).astype(f)), "sin": by_block(np.sin(fr).astype(f)),
        "att_bias": by_block(-bias),
        "numbers": np.tile(np.arange(E1, dtype=f), (P, 1)),
    }


def kernel(**inputs):
    import concourse.bacc as _bacc
    from concourse.bass_utils import run_bass_kernel_spmd as _run

    nc = _bacc.Bacc("TRN2", target_bir_lowering=False, num_devices=1)
    arrays, args = {}, {}
    for name, value in (*inputs.items(), *_constants().items()):
        value = np.ascontiguousarray(value)
        arrays[f"in_{name}_dram"] = value
        args[name] = nc.dram_tensor(f"in_{name}_dram", value.shape, mybir.dt.from_np(value.dtype), kind="ExternalInput").ap()
    outs = [nc.dram_tensor(f"out_{i}_dram", shape, mybir.dt.from_np(np.dtype(dtype)), kind="ExternalOutput").ap()
            for i, (shape, dtype) in enumerate(_OUTS)]
    build(nc, args, outs[0])
    r = _run(nc, [arrays], core_ids=[0])
    return r.results[0]["out_0_dram"]
```
